# Optimizing a Trainium2 kernel written in Bass

```python
import numpy as np
import jax
import jax.numpy as jnp

def _softmax(x, axis=-1):
    return jax.nn.softmax(x, axis=axis)

def _gelu(x):
    return jax.nn.gelu(x, approximate=True)

def _silu(x):
    return jax.nn.silu(x)

def _sigmoid(x):
    return jax.nn.sigmoid(x)

def _layernorm(x, axis=-1, eps=1e-05):
    m = jnp.mean(x, axis=axis, keepdims=True)
    v = jnp.var(x, axis=axis, keepdims=True)
    return (x - m) / jnp.sqrt(v + eps)

def _scatter_add(tgt, idx, src, axis=0):
    return tgt.at[idx].add(src)

def _segment_sum(src, seg, n):
    return jax.ops.segment_sum(src, seg, n)
kernel_name = 'mk_sandwich_d1_jaxref_r8_993c89'

def setup_inputs(seed: int=0):
    np.random.seed(seed)
    _w = jnp.asarray

    def _L0_attn_setup():
        import jax, jax.numpy as jnp
        import numpy as np
        B, S, SE, H, NH = (1, 256, 256, 128, 16)
        HD = H // NH
        INNER = 4 * H
        EPS = 1e-05

        def layer_norm(x, g, b):
            mu = jnp.mean(x, axis=-1, keepdims=True)
            var = jnp.mean(jnp.square(x - mu), axis=-1, keepdims=True)
            return (x - mu) * jax.lax.rsqrt(var + EPS) * g + b

        def split_heads(x):
            b, t, _ = x.shape
            return x.reshape(b, t, NH, HD).transpose(0, 2, 1, 3)

        def merge_heads(x):
            b, nh, t, hd = x.shape
            return x.transpose(0, 2, 1, 3).reshape(b, t, nh * hd)

        def _attn_core(q, k, v, extra_bias=None, causal_bool=False, tril_diag2_additive=False):
            w = jnp.einsum('bhqd,bhkd->bhqk', q, k) / jnp.sqrt(jnp.asarray(HD, q.dtype))
            ql, kl = (q.shape[-2], k.shape[-2])
            neg = jnp.finfo(w.dtype).min
            if causal_bool:
                mask = jnp.tril(jnp.ones((ql, kl), bool))
                w = jnp.where(mask[None, None], w, neg)
            if tril_diag2_additive:
                cm = jnp.tril(jnp.ones((ql, kl), w.dtype), k=2)
                w = w + jnp.where(cm == 0, neg, jnp.zeros((), w.dtype))[None, None]
            if extra_bias is not None:
                w = w + extra_bias[:, None, None, :]
            w = jax.nn.softmax(w, axis=-1)
            return jnp.einsum('bhqk,bhkd->bhqd', w, v)
        key = jax.random.key(seed)
        ks = jax.random.split(key, 16)
        n = lambda k, shp: jax.random.normal(k, shp, jnp.float32) * 0.02
        return {'hidden_states': jax.random.normal(ks[0], (B, S, H), jnp.float32), 'encoder_hidden_states': jax.random.normal(ks[1], (B, SE, H), jnp.float32), 'scorer_logits': jax.random.normal(ks[2], (B, SE), jnp.float32), 'ln1_g': jnp.ones((H,), jnp.float32), 'ln1_b': jnp.zeros((H,), jnp.float32), 'c_attn_w': n(ks[3], (H, 3 * H)), 'c_attn_b': jnp.zeros((3 * H,), jnp.float32), 'attn_proj_w': n(ks[4], (H, H)), 'attn_proj_b': jnp.zeros((H,), jnp.float32), 'lnx_g': jnp.ones((H,), jnp.float32), 'lnx_b': jnp.zeros((H,), jnp.float32), 'q_attn_w': n(ks[5], (H, H)), 'q_attn_b': jnp.zeros((H,), jnp.float32), 'x_kv_w': n(ks[6], (H, 2 * H)), 'x_kv_b': jnp.zeros((2 * H,), jnp.float32), 'x_proj_w': n(ks[7], (H, H)), 'x_proj_b': jnp.zeros((H,), jnp.float32), 'ln2_g': jnp.ones((H,), jnp.float32), 'ln2_b': jnp.zeros((H,), jnp.float32), 'fc_w': n(ks[8], (H, INNER)), 'fc_b': jnp.zeros((INNER,), jnp.float32), 'mlp_proj_w': n(ks[9], (INNER, H)), 'mlp_proj_b': jnp.zeros((H,), jnp.float32)}
    _L0_attn_in = _L0_attn_setup()

    def _L0_ffn_setup():
        import jax, jax.numpy as jnp
        import numpy as np
        D_MODEL = 128
        FFN = 128
        N_EXPERTS = 8
        N_SHARED = 1
        TOP_K = 2
        B, S = (2, 256)

        def _swiglu(h):
            a, b = jnp.split(h, 2, axis=-1)
            return jax.nn.silu(a) * b
        key = jax.random.key(seed)
        ks = jax.random.split(key, 12)
        sc = 0.02
        return {'x': jax.random.normal(ks[0], (B, S, D_MODEL), dtype=jnp.float32), 'gate_w': jax.random.normal(ks[1], (D_MODEL, N_EXPERTS), dtype=jnp.float32) * sc, 'gate_b': jnp.zeros((N_EXPERTS,), dtype=jnp.float32), 'sw1': jax.random.normal(ks[2], (N_SHARED, D_MODEL, 2 * FFN), dtype=jnp.float32) * sc, 'sb1': jnp.zeros((N_SHARED, 2 * FFN), dtype=jnp.float32), 'sw2': jax.random.normal(ks[3], (N_SHARED, FFN, D_MODEL), dtype=jnp.float32) * sc, 'sb2': jnp.zeros((N_SHARED, D_MODEL), dtype=jnp.float32), 'rw1': jax.random.normal(ks[4], (N_EXPERTS, D_MODEL, 2 * FFN), dtype=jnp.float32) * sc, 'rb1': jnp.zeros((N_EXPERTS, 2 * FFN), dtype=jnp.float32), 'rw2': jax.random.normal(ks[5], (N_EXPERTS, FFN, D_MODEL), dtype=jnp.float32) * sc, 'rb2': jnp.zeros((N_EXPERTS, D_MODEL), dtype=jnp.float32)}
    _L0_ffn_in = _L0_ffn_setup()
    _d = {'L0_attn_hidden_states': _L0_attn_in['hidden_states'], 'L0_attn_encoder_hidden_states': _L0_attn_in['encoder_hidden_states'], 'L0_attn_scorer_logits': _L0_attn_in['scorer_logits'], 'L0_attn_ln1_g': _L0_attn_in['ln1_g'], 'L0_attn_ln1_b': _L0_attn_in['ln1_b'], 'L0_attn_c_attn_w': _L0_attn_in['c_attn_w'], 'L0_attn_c_attn_b': _L0_attn_in['c_attn_b'], 'L0_attn_attn_proj_w': _L0_attn_in['attn_proj_w'], 'L0_attn_attn_proj_b': _L0_attn_in['attn_proj_b'], 'L0_attn_lnx_g': _L0_attn_in['lnx_g'], 'L0_attn_lnx_b': _L0_attn_in['lnx_b'], 'L0_attn_q_attn_w': _L0_attn_in['q_attn_w'], 'L0_attn_q_attn_b': _L0_attn_in['q_attn_b'], 'L0_attn_x_kv_w': _L0_attn_in['x_kv_w'], 'L0_attn_x_kv_b': _L0_attn_in['x_kv_b'], 'L0_attn_x_proj_w': _L0_attn_in['x_proj_w'], 'L0_attn_x_proj_b': _L0_attn_in['x_proj_b'], 'L0_attn_ln2_g': _L0_attn_in['ln2_g'], 'L0_attn_ln2_b': _L0_attn_in['ln2_b'], 'L0_attn_fc_w': _L0_attn_in['fc_w'], 'L0_attn_fc_b': _L0_attn_in['fc_b'], 'L0_attn_mlp_proj_w': _L0_attn_in['mlp_proj_w'], 'L0_attn_mlp_proj_b': _L0_attn_in['mlp_proj_b'], 'L0_ffn_gate_w': _L0_ffn_in['gate_w'], 'L0_ffn_gate_b': _L0_ffn_in['gate_b'], 'L0_ffn_sw1': _L0_ffn_in['sw1'], 'L0_ffn_sb1': _L0_ffn_in['sb1'], 'L0_ffn_sw2': _L0_ffn_in['sw2'], 'L0_ffn_sb2': _L0_ffn_in['sb2'], 'L0_ffn_rw1': _L0_ffn_in['rw1'], 'L0_ffn_rb1': _L0_ffn_in['rb1'], 'L0_ffn_rw2': _L0_ffn_in['rw2'], 'L0_ffn_rb2': _L0_ffn_in['rb2']}
    _x0 = _d['L0_attn_hidden_states']
    _d['L0_attn_hidden_states'] = jax.random.normal(jax.random.fold_in(jax.random.key(seed), 1), (32, 256, 128), dtype=_x0.dtype)
    del _x0
    return _d

def reference(L0_attn_hidden_states, L0_attn_encoder_hidden_states, L0_attn_scorer_logits, L0_attn_ln1_g, L0_attn_ln1_b, L0_attn_c_attn_w, L0_attn_c_attn_b, L0_attn_attn_proj_w, L0_attn_attn_proj_b, L0_attn_lnx_g, L0_attn_lnx_b, L0_attn_q_attn_w, L0_attn_q_attn_b, L0_attn_x_kv_w, L0_attn_x_kv_b, L0_attn_x_proj_w, L0_attn_x_proj_b, L0_attn_ln2_g, L0_attn_ln2_b, L0_attn_fc_w, L0_attn_fc_b, L0_attn_mlp_proj_w, L0_attn_mlp_proj_b, L0_ffn_gate_w, L0_ffn_gate_b, L0_ffn_sw1, L0_ffn_sb1, L0_ffn_sw2, L0_ffn_sb2, L0_ffn_rw1, L0_ffn_rb1, L0_ffn_rw2, L0_ffn_rb2):

    def _L0_attn_ref(hidden_states, encoder_hidden_states, scorer_logits, ln1_g, ln1_b, c_attn_w, c_attn_b, attn_proj_w, attn_proj_b, lnx_g, lnx_b, q_attn_w, q_attn_b, x_kv_w, x_kv_b, x_proj_w, x_proj_b, ln2_g, ln2_b, fc_w, fc_b, mlp_proj_w, mlp_proj_b):
        import jax, jax.numpy as jnp
        import numpy as np
        B, S, SE, H, NH = (1, 256, 256, 128, 16)
        HD = H // NH
        INNER = 4 * H
        EPS = 1e-05

        def layer_norm(x, g, b):
            mu = jnp.mean(x, axis=-1, keepdims=True)
            var = jnp.mean(jnp.square(x - mu), axis=-1, keepdims=True)
            return (x - mu) * jax.lax.rsqrt(var + EPS) * g + b

        def split_heads(x):
            b, t, _ = x.shape
            return x.reshape(b, t, NH, HD).transpose(0, 2, 1, 3)

        def merge_heads(x):
            b, nh, t, hd = x.shape
            return x.transpose(0, 2, 1, 3).reshape(b, t, nh * hd)

        def _attn_core(q, k, v, extra_bias=None, causal_bool=False, tril_diag2_additive=False):
            w = jnp.einsum('bhqd,bhkd->bhqk', q, k) / jnp.sqrt(jnp.asarray(HD, q.dtype))
            ql, kl = (q.shape[-2], k.shape[-2])
            neg = jnp.finfo(w.dtype).min
            if causal_bool:
                mask = jnp.tril(jnp.ones((ql, kl), bool))
                w = jnp.where(mask[None, None], w, neg)
            if tril_diag2_additive:
                cm = jnp.tril(jnp.ones((ql, kl), w.dtype), k=2)
                w = w + jnp.where(cm == 0, neg, jnp.zeros((), w.dtype))[None, None]
            if extra_bias is not None:
                w = w + extra_bias[:, None, None, :]
            w = jax.nn.softmax(w, axis=-1)
            return jnp.einsum('bhqk,bhkd->bhqd', w, v)
        residual = hidden_states
        x = layer_norm(hidden_states, ln1_g, ln1_b)
        qkv = x @ c_attn_w + c_attn_b
        q, k, v = jnp.split(qkv, 3, axis=-1)
        a = _attn_core(split_heads(q), split_heads(k), split_heads(v), causal_bool=True)
        a = merge_heads(a) @ attn_proj_w + attn_proj_b
        hidden_states = a + residual
        residual = hidden_states
        x = layer_norm(hidden_states, lnx_g, lnx_b)
        q = x @ q_attn_w + q_attn_b
        kv = encoder_hidden_states @ x_kv_w + x_kv_b
        k, v = jnp.split(kv, 2, axis=-1)
        a = _attn_core(split_heads(q), split_heads(k), split_heads(v), extra_bias=scorer_logits, tril_diag2_additive=True)
        a = merge_heads(a) @ x_proj_w + x_proj_b
        hidden_states = residual + a
        residual = hidden_states
        x = layer_norm(hidden_states, ln2_g, ln2_b)
        h = jax.nn.gelu(x @ fc_w + fc_b, approximate=True)
        hidden_states = residual + (h @ mlp_proj_w + mlp_proj_b)
        return hidden_states

    def _L0_ffn_ref(x, gate_w, gate_b, sw1, sb1, sw2, sb2, rw1, rb1, rw2, rb2):
        import jax, jax.numpy as jnp
        import numpy as np
        D_MODEL = 128
        FFN = 128
        N_EXPERTS = 8
        N_SHARED = 1
        TOP_K = 2
        B, S = (2, 256)

        def _swiglu(h):
            a, b = jnp.split(h, 2, axis=-1)
            return jax.nn.silu(a) * b
        hs = jnp.einsum('bsd,ndf->nbsf', x, sw1) + sb1[:, None, None, :]
        shared_out = jnp.einsum('nbsf,nfd->bsd', _swiglu(hs), sw2) + sb2.sum(0)
        probs = jax.nn.softmax(x @ gate_w + gate_b, axis=-1)
        topk_probs, topk_idx = jax.lax.top_k(probs, TOP_K)
        cw = jnp.sum(jax.nn.one_hot(topk_idx, N_EXPERTS, dtype=x.dtype) * topk_probs[..., None], axis=2)
        hr = jnp.einsum('bsd,edf->ebsf', x, rw1) + rb1[:, None, None, :]
        out_e = jnp.einsum('ebsf,efd->ebsd', _swiglu(hr), rw2) + rb2[:, None, None, :]
        routed_out = jnp.einsum('ebsd,bse->bsd', out_e, cw)
        return shared_out + routed_out
    x = L0_attn_hidden_states
    x = x + _layernorm(_L0_attn_ref(_layernorm(x, axis=-1), L0_attn_encoder_hidden_states, L0_attn_scorer_logits, L0_attn_ln1_g, L0_attn_ln1_b, L0_attn_c_attn_w, L0_attn_c_attn_b, L0_attn_attn_proj_w, L0_attn_attn_proj_b, L0_attn_lnx_g, L0_attn_lnx_b, L0_attn_q_attn_w, L0_attn_q_attn_b, L0_attn_x_kv_w, L0_attn_x_kv_b, L0_attn_x_proj_w, L0_attn_x_proj_b, L0_attn_ln2_g, L0_attn_ln2_b, L0_attn_fc_w, L0_attn_fc_b, L0_attn_mlp_proj_w, L0_attn_mlp_proj_b), axis=-1)
    x = x + _layernorm(_L0_ffn_ref(_layernorm(x, axis=-1), L0_ffn_gate_w, L0_ffn_gate_b, L0_ffn_sw1, L0_ffn_sb1, L0_ffn_sw2, L0_ffn_sb2, L0_ffn_rw1, L0_ffn_rb1, L0_ffn_rw2, L0_ffn_rb2), axis=-1)
    return x

_drawn_inputs = setup_inputs


def setup_inputs(seed=0):
    import zlib

    import numpy as np

    out = dict(_drawn_inputs(seed))
    spreads = {'L0_attn_ln1_g': (1.0, 0.6),
     'L0_attn_ln1_b': (0.0, 0.8),
     'L0_attn_c_attn_b': (0.0, 0.55),
     'L0_attn_attn_proj_b': (0.0, 0.1),
     'L0_attn_lnx_g': (1.0, 0.6),
     'L0_attn_lnx_b': (0.0, 0.8),
     'L0_attn_q_attn_b': (0.0, 0.8),
     'L0_attn_x_kv_b': (0.0, 0.583),
     'L0_attn_x_proj_b': (0.0, 0.1),
     'L0_attn_ln2_g': (1.0, 0.6),
     'L0_attn_ln2_b': (0.0, 2.0),
     'L0_attn_fc_b': (0.0, 0.569),
     'L0_attn_mlp_proj_b': (0.0, 0.276),
     'L0_ffn_gate_b': (0.0, 0.1),
     'L0_ffn_sb1': (0.0, 1.95),
     'L0_ffn_sb2': (0.0, 0.1),
     'L0_ffn_rb1': (0.0, 0.8),
     'L0_ffn_rb2': (0.0, 0.632)}
    factors = {'L0_attn_encoder_hidden_states': 8.0,
     'L0_attn_scorer_logits': 8.0,
     'L0_attn_c_attn_w': 8.0,
     'L0_attn_attn_proj_w': 3.602,
     'L0_attn_q_attn_w': 8.0,
     'L0_attn_x_kv_w': 8.0,
     'L0_attn_x_proj_w': 4.316,
     'L0_ffn_rw1': 8.0,
     'L0_ffn_rw2': 8.0,
     'L0_ffn_sw1': 4.766}
    for name, (base, spread) in spreads.items():
        noise = np.random.default_rng([zlib.crc32(name.encode()), seed]).standard_normal(out[name].shape)
        drawn = base * np.exp(spread * noise) if base else spread * noise
        out[name] = jnp.asarray(drawn.astype(out[name].dtype))
    for name, factor in factors.items():
        out[name] = (out[name] * factor).astype(out[name].dtype)
    return out
```

```python
import concourse.bass as bass
from concourse import mybir
from contextlib import ExitStack

F32 = mybir.dt.float32
BF16 = mybir.dt.bfloat16
ALU = mybir.AluOpType
ACT = mybir.ActivationFunctionType
AX = mybir.AxisListType


class Names:
    pass


class Signal:

    def __init__(self, sem, per):
        self.sem, self.per = sem, per

    def done(self, j):
        return self.sem, j + 1 if self.per == 1 else j * self.per + self.per

    def part(self, j, k):
        return self.sem, j * self.per + k

    def before(self, j):
        return self.sem, j if self.per == 1 else j * self.per


def sandwich_kernel(nc, out, hs, enc, scorer, ln1_g, ln1_b, c_attn_w, c_attn_b, attn_proj_w, attn_proj_b,
                    lnx_g, lnx_b, q_attn_w, q_attn_b, x_kv_w, x_kv_b, x_proj_w, x_proj_b, ln2_g, ln2_b,
                    fc_w, fc_b, mlp_proj_w, mlp_proj_b, gate_w, gate_b, sw1, sb1, sw2, sb2, rw1, rb1, rw2, rb2):
    B, T, D = hs.shape
    H, HD = 16, 8
    NE = rw1.shape[0]
    NC = fc_w.shape[1] // 128
    PAIRS = B // 2
    NT = 2 * T
    NB = NT // 128
    EPS = 1e-5
    SCALE = float(HD) ** -0.5
    MASKED = -3.0e38
    QPARTS = [0, 1, 2, 0, 1, 0]
    KPARTS = [0, 0, 0, 1, 1, 2]
    ROW_BIAS, ROWS_S, ROW_MAX, ROWS_ST = 64, 96, 96, 99
    XW = 130

    ctx = ExitStack()
    with ctx:
        ctx.enter_context(nc.allow_non_contiguous_dma(reason="small vectors and permuted rows, once"))

        def sb(name, shape, dt=F32):
            return ctx.enter_context(nc.sbuf_tensor(name, shape, dt))

        def signal(name, per):
            return Signal(ctx.enter_context(nc.semaphore(name)), per)

        identf = sb("identf", [128, 128])
        identb = sb("identb", [128, 128], BF16)
        mask_q = sb("mask_q", [128, 2, 128], BF16)
        mask_k = sb("mask_k", [128, 2, 128], BF16)
        xmask_q = sb("xmask_q", [128, 128 + XW], BF16)
        xmask_k = sb("xmask_k", [128, 128 + XW], BF16)
        lower = sb("lower", [128, NE, NE])
        half_neg = sb("half_neg", [128, NB])
        wqkv = sb("wqkv", [128, 3 * D])
        wq = sb("wq", [128, D])
        wk = sb("wk", [128, D])
        wo = sb("wo", [128, D])
        wxq0 = sb("wxq0", [128, D])
        wxq = sb("wxq", [128, D])
        wxkv = sb("wxkv", [128, 2 * D])
        wxk = sb("wxk", [128, D])
        wxo = sb("wxo", [128, D])
        wfc = sb("wfc", [128, NC * 128])
        wmlp = sb("wmlp", [128, NC, D])
        wgate = sb("wgate", [128, NE])
        w1 = sb("w1", [128, NE + 1, 2 * 128])
        w2 = sb("w2", [128, NE + 1, D])
        b1 = sb("b1", [128, NE + 1, 2])
        b2 = sb("b2", [NE + 1, D])
        cols = sb("cols", [128, 16])
        G1, B1, GX, BX, G2, B2, BQ, BK, BV, BXQ, BXK, BXV, BQS, BXQS = range(14)
        bfc = sb("bfc", [128, NC])
        bo = sb("bo", [128, D])
        bxo = sb("bxo", [128, D])
        bmlp = sb("bmlp", [128, D])
        bgate = sb("bgate", [128, NE])
        enc_tm = sb("enc_tm", [128, 2, D])
        encT = sb("encT", [128, T])
        kxf = sb("kxf", [128, T])
        kxr = sb("kxr", [128, T])
        kx_parts = sb("kx_parts", [128, 3, T], BF16)
        key_bias = sb("key_bias", [1, T])
        key_res = sb("key_res", [1, T])
        bias_parts = sb("bias_parts", [1, 3, T], BF16)

        q_op = sb("q_op", [128, H, NT], BF16)
        k_op = sb("k_op", [128, H, NT], BF16)
        xq_op = sb("xq_op", [128, H, NT], BF16)
        xk_op = sb("xk_op", [128, H, T], BF16)
        v_st = sb("v_st", [128, NB, H, 32])
        xv_st = sb("xv_st", [128, 2, H, 32])

        x_tm = sb("x_tm", [128, NB, D])
        x_keep = sb("x_keep", [128, NB, D])
        y_tm = sb("y_tm", [128, NB, D])
        x1_tm = sb("x1_tm", [128, NB, D])
        xT = sb("xT", [128, NT])
        qf = sb("qf", [128, NT])
        kf = sb("kf", [128, NT])
        qr = sb("qr", [128, NT])
        kr = sb("kr", [128, NT])
        q_parts = sb("q_parts", [128, 3, NT], BF16)
        k_parts = sb("k_parts", [128, 3, NT], BF16)
        rowmax = sb("rowmax", [128, 2, 2, H])
        max_res = sb("max_res", [128, NB, H])
        max_parts = sb("max_parts", [128, NB, 8, H], BF16)
        wait_slot = sb("wait_slot", [128, 1])
        maxT = sb("maxT", [3 * H, NT], BF16)
        probs = sb("probs", [128, 2, 4, T + XW])
        ctx_fm = sb("ctx_fm", [128, 2, NT])
        rden = sb("rden", [128, NB, H])
        ctx_tm = sb("ctx_tm", [128, NB, D])
        ctxT = sb("ctxT", [128, NT])
        h1 = sb("h1", [128, NB, D])
        stx = sb("stx", [128, NB, 6])
        mvx = sb("mvx", [128, NB, 2])
        tiny = sb("tiny", [128, 8, NB])

        h2 = sb("h2", [128, NB, D])
        x3_tm = sb("x3_tm", [128, NB, D])
        x3T = sb("x3T", [128, NT])
        geluT = sb("geluT", [128, NC, NT])
        h3 = sb("h3", [128, NB, D])
        xn = sb("xn", [128, NB, D])
        z_tm = sb("z_tm", [128, NB, D])
        zT = sb("zT", [128, NT])
        logit = sb("logit", [128, NB, NE])
        prob = sb("prob", [128, NB, NE])
        rt = sb("rt", [128, 4, NB])
        more = sb("more", [128, NB, NE * NE])
        same = sb("same", [128, NB, NE * NE])
        rank = sb("rank", [128, NB, NE])
        gates = sb("gates", [128, NB, NE + 1])
        gatesT = sb("gatesT", [NE + 1, NT])
        silu_a = sb("silu_a", [128, NT])
        hT = sb("hT", [128, 2, NT])
        acc = sb("acc", [128, NB, D])
        o_tm = sb("o_tm", [128, NB, D])
        sty = sb("sty", [128, NB, 6])
        mvy = sb("mvy", [128, NB, 2])
        tiny_y = sb("tiny_y", [128, 4, NB])

        pa = ctx.enter_context(nc.psum_tensor("pa", [128, 4, 512], F32))
        pw = ctx.enter_context(nc.psum_tensor("pw", [128, 4, 512], F32))

        loaded = signal("loaded", 0)
        filled = signal("filled", 0)
        shaped = signal("shaped", 0)
        padded = signal("padded", 0)
        made = signal("made", 0)
        enc_ps = signal("enc_ps", 0)
        enc_sb = signal("enc_sb", 0)
        xk_dma = signal("xk_dma", 0)
        x_in = signal("x_in", 16)
        x_kept = signal("x_kept", 16)
        y_ready = signal("y_ready", NB)
        yb_ready = signal("yb_ready", 1)
        var_y = signal("var_y", 3)
        rstd_y = signal("rstd_y", 1)
        rstd_01 = signal("rstd_01", 1)

        def attention(n, cross):
            a = Names()
            a.cross = cross
            a.qop, a.kop = (xq_op, xk_op) if cross else (q_op, k_op)
            a.mq, a.mk = (xmask_q, xmask_k) if cross else (mask_q, mask_k)
            a.seen = XW if cross else 128
            a.v = xv_st if cross else v_st
            a.stats, a.aggr = signal(n + "_stats", NB), signal(n + "_aggr", NB)
            a.var_eps, a.rstd = signal(n + "_var_eps", 1), signal(n + "_rstd", 1)
            a.x_ready = signal(n + "_x_ready", NB)
            a.xT_ps, a.xT_sb = signal(n + "_xT_ps", 1), signal(n + "_xT_sb", 1)
            a.q_ps, a.k_ps, a.v_ps = signal(n + "_q_ps", 1), signal(n + "_k_ps", 1), signal(n + "_v_ps", 1)
            a.qf, a.qhi = signal(n + "_qf", 1), signal(n + "_qhi", 1)
            a.qr, a.qmid, a.qlo = signal(n + "_qr", 1), signal(n + "_qmid", 1), signal(n + "_qlo", 1)
            a.kf, a.khi = signal(n + "_kf", 1), signal(n + "_khi", 1)
            a.kr, a.kmid, a.klo = signal(n + "_kr", 1), signal(n + "_kmid", 1), signal(n + "_klo", 1)
            a.v_sb = signal(n + "_v_sb", 2)
            a.q_dma, a.k_dma = signal(n + "_q_dma", 96), signal(n + "_k_dma", 96)
            a.s_ps, a.s_max = signal(n + "_s_ps", H), signal(n + "_s_max", 2 * H)
            a.m1, a.mr, a.m2, a.m3 = (signal(n + x, 1) for x in ("_m1", "_mr", "_m2", "_m3"))
            a.mT_ps, a.mT_sb, a.m_dma = signal(n + "_mT_ps", 1), signal(n + "_mT_sb", 1), signal(n + "_m_dma", 16)
            a.st_ps, a.exp, a.pv = signal(n + "_st_ps", H), signal(n + "_exp", H), signal(n + "_pv", 8)
            a.ctx_sb, a.cT_ps = signal(n + "_ctx_sb", 2), signal(n + "_cT_ps", 2)
            a.rden, a.ctx_n = signal(n + "_rden", 2), signal(n + "_ctx_n", 2)
            a.nT_ps, a.nT_sb = signal(n + "_nT_ps", 1), signal(n + "_nT_sb", 1)
            a.o_ps, a.h = signal(n + "_o_ps", 1), signal(n + "_h", 1)
            return a

        sa = attention("self", False)
        ca = attention("cross", True)
        h1b = signal("h1b", 1)
        h2b = signal("h2b", 1)

        def norm(n):
            a = Names()
            a.stats, a.aggr = signal(n + "_stats", NB), signal(n + "_aggr", NB)
            a.var_eps, a.rstd, a.out = signal(n + "_var_eps", 1), signal(n + "_rstd", 1), signal(n + "_out", NB)
            return a

        n_mlp, n_post, n_z, n_end = norm("n_mlp"), norm("n_post"), norm("n_z"), norm("n_end")
        x3T_ps, x3T_sb = signal("x3T_ps", 1), signal("x3T_sb", 1)
        fc_ps, gelu = signal("fc_ps", NC), signal("gelu", NC)
        mlp_ps, h3_sb = signal("mlp_ps", 1), signal("h3_sb", 1)
        xn_ready = signal("xn_ready", 1)
        zT_ps, zT_sb = signal("zT_ps", 1), signal("zT_sb", 1)
        gate_ps, route, gate_exp = signal("gate_ps", 1), signal("route", 9), signal("gate_exp", 1)
        n_rank = signal("n_rank", 2 * NB + 3)
        gatesT_ps, gatesT_sb = signal("gatesT_ps", 1), signal("gatesT_sb", 1)
        a_ps, b_ps, silu = signal("a_ps", NE + 1), signal("b_ps", NE + 1), signal("silu", NE + 1)
        h_sb, e_ps = signal("h_sb", NE + 1), signal("e_ps", NE + 1)
        acc_sb = signal("acc_sb", 1 + NB * NE)
        o_ready = signal("o_ready", NB)
        o_dma = signal("o_dma", 16)

        block = ctx.enter_context(nc.Block())
        wide = [(w, s) for w, s in ((wqkv, c_attn_w), (wxq0, q_attn_w), (wxkv, x_kv_w), (wfc, fc_w),
                                    (wgate, gate_w))]
        vectors = [(G1, ln1_g), (B1, ln1_b), (GX, lnx_g), (BX, lnx_b), (G2, ln2_g), (B2, ln2_b)]

        def rows_dh(v):
            return v.rearrange("(h d o) -> d h o", d=HD, o=1)

        def load_setup(eng, half):
            jobs = [(w[:], s) for w, s in wide]
            jobs += [(wmlp[:], mlp_proj_w.rearrange("(c p) n -> p c n", p=128))]
            jobs += [(w1[:, 0:NE, :], rw1.rearrange("e p n -> p e n")), (w1[:, NE, :], sw1[0])]
            jobs += [(w2[:, 0:NE, :], rw2.rearrange("e p n -> p e n")), (w2[:, NE, :], sw2[0])]
            jobs += [(b1[:, 0:NE, :], rb1.rearrange("e (a p) -> p e a", p=128)),
                     (b1[:, NE, :], sb1.rearrange("o (a p) -> p (o a)", p=128))]
            jobs += [(b2[0:NE, :], rb2), (b2[NE:NE + 1, :], sb2)]
            jobs += [(cols[:, n:n + 1], v.rearrange("(p o) -> p o", o=1)) for n, v in vectors]
            jobs += [(cols[:, BQ:BQ + 1], rows_dh(c_attn_b[0:D])), (cols[:, BK:BK + 1], rows_dh(c_attn_b[D:2 * D])),
                     (cols[:, BXQ:BXQ + 1], rows_dh(q_attn_b)), (cols[:, BXK:BXK + 1], rows_dh(x_kv_b[0:D]))]
            for s in range(2):
                for j in range(4):
                    p = (4 * s + j) * 16
                    for w, v in ((wo, attn_proj_w), (wxo, x_proj_w)):
                        jobs += [(w[p:p + 16, :], v.rearrange("(s a j d) n -> s j a d n", s=2, a=2, j=4)[s, j])]
                    for n, v in ((BV, c_attn_b[2 * D:3 * D]), (BXV, x_kv_b[D:2 * D])):
                        jobs += [(cols[p:p + 16, n:n + 1],
                                  v.rearrange("(s a j d o) -> s j a d o", s=2, a=2, j=4, o=1)[s, j])]
            jobs += [(bfc[:], fc_b.rearrange("(c p) -> p c", p=128))]
            jobs += [(w[:], v.rearrange("(o n) -> o n", o=1).to_broadcast([128, n]))
                     for w, v, n in ((bo, attn_proj_b, D), (bxo, x_proj_b, D), (bmlp, mlp_proj_b, D), (bgate, gate_b, NE))]
            jobs += [(enc_tm[:], enc[0].rearrange("(k p) f -> p k f", p=128)), (key_bias[:], scorer)]
            for o, i in jobs[half::2]:
                eng.dma_start(o, i).then_inc(loaded.sem, 16)
            return len(jobs)

        LOADS = []
        PADS = 14
        XK_PARTS = 17
        SETUP_MADE = XK_PARTS + 2

        @block.sync
        def _(sp):
            def pair_of(x, j):
                return x[bass.ds(sp.snap(2 * j), 2)].rearrange("b (q p) f -> p (b q) f", p=128)

            def load_x(j):
                src = pair_of(hs, j)
                sp.wait_ge(*y_ready.before(j))
                sp.wait_ge(*sa.x_ready.before(j))
                sp.dma_start(x_tm[:], src).then_inc(x_in.sem, 16)

            def keep_x(j):
                src = pair_of(hs, j)
                sp.wait_ge(*xn_ready.before(j))
                sp.dma_start(x_keep[:], src).then_inc(x_kept.sem, 16)

            def store_out(j):
                dst = pair_of(out, j)
                sp.wait_ge(*o_ready.done(j))
                sp.dma_start(dst, o_tm[:]).then_inc(o_dma.sem, 16)

            def operand(a, parts, op, which, hi, mid, lo, dma, j):
                sp.wait_ge(*hi.done(j))
                sp.wait_ge(*a.nT_ps.before(j))
                for made_part, n in ((hi, 0), (mid, 1), (lo, 2)):
                    if n:
                        sp.wait_ge(*made_part.done(j))
                    for slot in range(6):
                        if which[slot] == n:
                            sp.dma_start(op[slot * HD:(slot + 1) * HD, :, :], parts[:, n, :]).then_inc(dma.sem, 16)

            def max_rows(a, j):
                sp.wait_ge(*a.mT_sb.done(j))
                sp.dma_start(a.qop[ROW_MAX:ROW_MAX + 3, :, :], maxT[:]).then_inc(a.m_dma.sem, 16)

            def body(j, behind):
                operand(sa, q_parts, q_op, QPARTS, sa.qhi, sa.qmid, sa.qlo, sa.q_dma, j)
                operand(sa, k_parts, k_op, KPARTS, sa.khi, sa.kmid, sa.klo, sa.k_dma, j)
                max_rows(sa, j)
                keep_x(j)
                operand(ca, q_parts, xq_op, QPARTS, ca.qhi, ca.qmid, ca.qlo, ca.q_dma, j)
                max_rows(ca, j)
                if behind:
                    store_out(j - 1)

            load_x(0)
            n = load_setup(sp, 0)
            LOADS.append(n)
            sp.wait_ge(padded.sem, PADS)
            sp.wait_ge(made.sem, XK_PARTS)
            for slot in range(6):
                sp.dma_start(xk_op[slot * HD:(slot + 1) * HD, :, :], kx_parts[:, KPARTS[slot], :]).then_inc(xk_dma.sem, 16)
            for n in range(3):
                sp.dma_start(xk_op[ROW_BIAS + n:ROW_BIAS + n + 1, :, :],
                             bias_parts[:, n:n + 1, :].to_broadcast([1, H, T])).then_inc(xk_dma.sem, 16)
            body(0, False)
            load_x(1)
            with sp.Fori(1, PAIRS - 1) as i:
                body(i, True)
                load_x(i + 1)
            body(PAIRS - 1, True)
            store_out(PAIRS - 1)
            sp.wait_ge(*o_dma.done(PAIRS - 1))

        @block.gpsimd
        def _(pool):
            pool.memset(identf[:], 0.0).then_inc(filled.sem, 1)
            pool.memset(identb[:], 0.0).then_inc(filled.sem, 1)
            pool.memset(mask_q[:], 0.0).then_inc(filled.sem, 1)
            pool.memset(mask_k[:], 0.0).then_inc(filled.sem, 1)
            pool.memset(xmask_q[:], 0.0).then_inc(filled.sem, 1)
            pool.memset(xmask_k[:], 0.0).then_inc(filled.sem, 1)
            pool.memset(lower[:], 1.0).then_inc(filled.sem, 1)
            pool.memset(half_neg[:], -0.5).then_inc(filled.sem, 1)
            pool.memset(gates[:], 1.0).then_inc(filled.sem, 1)
            pool.wait_ge(filled.sem, 9)

            def select(m, cmp, fill, base, pattern, channel):
                pool.affine_select(out=m, in_=m, compare_op=cmp, fill=fill, base=base, pattern=pattern,
                                   channel_multiplier=channel).then_inc(shaped.sem, 1)

            select(identf[:], ALU.not_equal, 1.0, 0, [[-1, 128]], 1)
            select(identb[:], ALU.not_equal, 1.0, 0, [[-1, 128]], 1)
            select(mask_q[:], ALU.is_ge, MASKED, 0, [[0, 2], [-1, 128]], 1)
            select(mask_k[:], ALU.is_ge, MASKED, 0, [[0, 2], [1, 128]], -1)
            select(xmask_q[:, 0:128], ALU.is_ge, MASKED, 2, [[-1, 128]], 1)
            select(xmask_q[:, 128:], ALU.is_ge, MASKED, 2, [[-1, XW]], 1)
            select(xmask_k[:, 0:128], ALU.is_ge, MASKED, 2, [[1, 128]], -1)
            select(xmask_k[:, 128:], ALU.is_ge, MASKED, 0, [[1, XW]], -1)
            select(lower[:], ALU.is_gt, 0.0, 0, [[1, NE], [-1, NE]], 0)

            def power(n_var, n_out, var, out_, j):
                pool.wait_ge(*n_var)
                pool.tensor_tensor(out_, var, half_neg[:], ALU.pow).then_inc(n_out.sem, 1)

            def low_part(r, parts, a_r, a_mid, a_lo, a_dma, j):
                pool.wait_ge(*a_r.done(j))
                pool.wait_ge(*a_mid.done(j))
                pool.wait_ge(*a_dma.before(j))
                pool.tensor_tensor(parts[:, 2, :], r[:], parts[:, 1, :], ALU.subtract).then_inc(a_lo.sem, 1)

            def add_bias(dst, base, bias, ready, before, out_sig, j):
                pool.wait_ge(*ready)
                if before is not None:
                    pool.wait_ge(*before)
                pool.tensor_tensor(dst[:], base[:], bias[:].rearrange("p (o f) -> p o f", o=1).to_broadcast([128, NB, D]),
                                   ALU.add).then_inc(out_sig.sem, 1)

            def norm_power(n, tile, row, j):
                power(n.var_eps.done(j), n.rstd, tile[:, row, :], tile[:, row + 1, :], j)

            def front(j):
                power(var_y.part(j, 1), rstd_y, tiny[:, 0, :], tiny[:, 1, :], j)
                power(var_y.done(j), rstd_01, tiny[:, 3, :], tiny[:, 4, :], j)
                add_bias(y_tm, y_tm, bo, y_ready.done(j), None, yb_ready, j)
                low_part(qr, q_parts, sa.qr, sa.qmid, sa.qlo, ca.q_dma, j)
                low_part(kr, k_parts, sa.kr, sa.kmid, sa.klo, sa.k_dma, j)

            def mlp(j):
                norm_power(n_mlp, tiny_y, 0, j)
                norm_power(n_post, tiny_y, 0, j)
                norm_power(n_z, tiny_y, 0, j)

            def middle(j):
                norm_power(ca, tiny, 5, j)
                add_bias(h1, h1, bxo, ca.x_ready.done(j), None, h1b, j)
                low_part(qr, q_parts, ca.qr, ca.qmid, ca.qlo, sa.q_dma, j)

            def body(j, behind):
                front(j)
                if behind:
                    mlp(j - 1)
                middle(j)
                if behind:
                    norm_power(n_end, tiny_y, 0, j - 1)

            body(0, False)
            body(1, True)
            with pool.Fori(2, PAIRS) as i:
                body(i, True)
            mlp(PAIRS - 1)
            norm_power(n_end, tiny_y, 0, PAIRS - 1)

        @block.scalar
        def _(act):
            n = load_setup(act, 1)
            total = 16 * n
            act.wait_ge(loaded.sem, total)
            act.wait_ge(enc_ps.sem, 1)
            act.activation(encT[:], pw[:, 0, 0:T], ACT.Identity).then_inc(enc_sb.sem, 1)
            act.wait_ge(enc_ps.sem, 2)
            act.activation(kxf[:], pw[:, 1, 0:T], ACT.Identity, bias=cols[:, BXK:BXK + 1]).then_inc(enc_sb.sem, 1)
            act.activation(kx_parts[:, 0, :], pw[:, 1, 0:T], ACT.Identity, bias=cols[:, BXK:BXK + 1]).then_inc(enc_sb.sem, 1)

            def features(a, g, b, j, dst, before):
                act.wait_ge(*a.xT_ps.done(j))
                for w in before:
                    act.wait_ge(*w)
                act.activation(dst[:], pw[:, 0, :], ACT.Identity, bias=cols[:, b:b + 1],
                               scale=cols[:, g:g + 1]).then_inc(a.xT_sb.sem, 1)

            def high_part(bank, f, parts, bias, scale, ready, before, f_sig, hi_sig):
                act.wait_ge(*ready)
                for w in before:
                    act.wait_ge(*w)
                act.activation(f[:], pw[:, bank, :], ACT.Identity, bias=bias, scale=scale).then_inc(f_sig.sem, 1)
                act.activation(parts[:, 0, :], pw[:, bank, :], ACT.Identity, bias=bias, scale=scale).then_inc(hi_sig.sem, 1)

            def front(j):
                features(sa, G1, B1, j, xT, [ca.q_ps.before(j)])
                high_part(1, qf, q_parts, cols[:, BQS:BQS + 1], SCALE, sa.q_ps.done(j),
                          [ca.qr.before(j), ca.q_dma.before(j)], sa.qf, sa.qhi)
                high_part(2, kf, k_parts, cols[:, BK:BK + 1], 1.0, sa.k_ps.done(j),
                          [sa.kr.before(j), sa.k_dma.before(j)], sa.kf, sa.khi)

            def values(j):
                act.wait_ge(*sa.v_ps.done(j))
                act.wait_ge(*sa.pv.before(j))
                for half in range(2):
                    src = pw[:, 3, :].rearrange("p (g a j d) -> p g a j d", a=2, j=4, d=HD)[:, :, half]
                    dst = v_st[:].rearrange("p t (s a j) c -> p (t s) a j c", s=2, a=2)[:, :, half, :,
                                                                                       16 * half:16 * half + HD]
                    act.activation(dst, src, ACT.Identity).then_inc(sa.v_sb.sem, 1)

            def max_rows(a, j, other):
                act.wait_ge(*a.mT_ps.done(j))
                act.wait_ge(*other)
                act.activation(maxT[:], pw[0:3 * H, 0, :].bitcast(BF16)[:, 0:NT], ACT.Identity).then_inc(a.mT_sb.sem, 1)

            def exps(a, j):
                for g in range(H):
                    four, pair = divmod(g, 2)
                    act.wait_ge(*a.st_ps.part(j, g + 1))
                    if four >= 2:
                        act.wait_ge(*a.pv.part(j, four - 1))
                    else:
                        act.wait_ge(*(ca.pv.before(j) if a is sa else sa.pv.done(j)))
                    act.activation(probs[:, four % 2, 2 * pair:2 * pair + 2, 0:T + a.seen],
                                   pa[:, 2 * (g % 2):2 * (g % 2) + 2, 0:T + a.seen], ACT.Exp).then_inc(a.exp.sem, 1)

            def context_copy(a, s, j):
                act.wait_ge(*a.pv.part(j, 4 * s + 4))
                act.wait_ge(*(ca.cT_ps.before(j) if a is sa else sa.cT_ps.done(j)))
                act.activation(ctx_fm[:, s, :], pw[:, 2 + s, :], ACT.Identity).then_inc(a.ctx_sb.sem, 1)

            def context_T(a, bv, j):
                act.wait_ge(*a.nT_ps.done(j))
                act.wait_ge(*(ca.o_ps.before(j) if a is sa else sa.o_ps.done(j)))
                act.activation(ctxT[:], pw[:, 2, :], ACT.Identity, bias=cols[:, bv:bv + 1]).then_inc(a.nT_sb.sem, 1)

            def middle(j):
                features(ca, GX, BX, j, xT, [sa.v_ps.done(j)])
                high_part(1, qf, q_parts, cols[:, BXQS:BXQS + 1], SCALE, ca.q_ps.done(j),
                          [sa.qr.done(j), sa.q_dma.done(j)], ca.qf, ca.qhi)

            def mlp(j):
                act.wait_ge(*x3T_ps.done(j))
                act.wait_ge(*fc_ps.before(j))
                act.activation(x3T[:], pa[:, 0, :], ACT.Identity, bias=cols[:, B2:B2 + 1],
                               scale=cols[:, G2:G2 + 1]).then_inc(x3T_sb.sem, 1)
                act.wait_ge(*mlp_ps.before(j))
                for c in range(NC):
                    act.wait_ge(*fc_ps.part(j, c + 1))
                    act.activation(geluT[:, c, :], pa[:, (c + 1) % 4, :], ACT.Gelu_apprx_tanh,
                                   bias=bfc[:, c:c + 1]).then_inc(gelu.sem, 1)

            def router(j):
                act.wait_ge(*zT_ps.done(j))
                act.wait_ge(*b_ps.before(j))
                act.activation(zT[:], pa[:, 2, :], ACT.Identity).then_inc(zT_sb.sem, 1)
                act.wait_ge(*route.part(j, 3))
                act.activation(prob[:], logit[:], ACT.Exp).then_inc(gate_exp.sem, 1)

            def gates_T(j):
                act.wait_ge(*gatesT_ps.done(j))
                act.activation(gatesT[:], pa[0:NE + 1, 3, :], ACT.Identity).then_inc(gatesT_sb.sem, 1)

            def experts(j, first, last):
                for n in range(first, last):
                    e = n - 1 if n else NE
                    act.wait_ge(*a_ps.part(j, n + 1))
                    act.wait_ge(*h_sb.part(j, n))
                    act.activation(silu_a[:], pa[:, 0, :], ACT.Silu, bias=b1[:, e, 0:1]).then_inc(silu.sem, 1)

            def body(j, behind):
                front(j)
                values(j)
                if behind:
                    mlp(j - 1)
                    router(j - 1)
                    gates_T(j - 1)
                    experts(j - 1, 0, 1)
                max_rows(sa, j, ca.m_dma.before(j))
                if behind:
                    experts(j - 1, 1, 3)
                exps(sa, j)
                context_copy(sa, 0, j)
                context_copy(sa, 1, j)
                if behind:
                    experts(j - 1, 3, 4)
                context_T(sa, BV, j)
                if behind:
                    experts(j - 1, 4, 6)
                middle(j)
                if behind:
                    experts(j - 1, 6, 8)
                max_rows(ca, j, sa.m_dma.done(j))
                if behind:
                    experts(j - 1, 8, 9)
                exps(ca, j)
                context_copy(ca, 0, j)
                context_copy(ca, 1, j)
                context_T(ca, BXV, j)

            act.wait_ge(made.sem, SETUP_MADE)
            body(0, False)
            body(1, True)
            with act.Fori(2, PAIRS) as i:
                body(i, True)
            mlp(PAIRS - 1)
            router(PAIRS - 1)
            gates_T(PAIRS - 1)
            experts(PAIRS - 1, 0, 1)
            experts(PAIRS - 1, 1, NE + 1)

        @block.vector
        def _(dve):
            for op in (q_op, xq_op, k_op, xk_op):
                dve.memset(op[32:64].bitcast(mybir.dt.uint32), 0).then_inc(padded.sem, 1)
                dve.memset(op[64:128].bitcast(mybir.dt.uint32), 0).then_inc(padded.sem, 1)
            dve.wait_ge(padded.sem, 8)
            dve.memset(xq_op[ROW_BIAS:ROW_BIAS + 3], 1.0).then_inc(padded.sem, 1)
            dve.memset(k_op[ROW_MAX:ROW_MAX + 3], -1.0).then_inc(padded.sem, 1)
            dve.memset(xk_op[ROW_MAX:ROW_MAX + 3], -1.0).then_inc(padded.sem, 1)
            for tile in (v_st, xv_st, max_parts):
                dve.memset(tile[:], 0.0).then_inc(padded.sem, 1)
            dve.wait_ge(padded.sem, PADS)
            steps = [0]

            def make(ins):
                steps[0] += 1
                ins.then_inc(made.sem, 1)
                dve.wait_ge(made.sem, steps[0])

            for tile in (v_st, xv_st):
                for half in range(2):
                    make(dve.memset(tile[:].rearrange("p t (s a j) c -> p (t s) a j c", s=2, a=2)
                                    [:, :, half, :, 16 * half + HD], 1.0))
            dve.wait_ge(loaded.sem, 16 * LOADS[0])
            for dst, src in ((wq, wqkv[:, 0:D]), (wk, wqkv[:, D:2 * D]), (wxq, wxq0[:]), (wxk, wxkv[:, 0:D])):
                make(dve.tensor_copy(dst[:].rearrange("p (d h) -> p d h", d=HD), src.rearrange("p (h d) -> p d h", d=HD)))
            make(dve.tensor_scalar(cols[:, BQS:BQS + 1], cols[:, BQ:BQ + 1], SCALE, None, ALU.mult))
            make(dve.tensor_scalar(cols[:, BXQS:BXQS + 1], cols[:, BXQ:BXQ + 1], SCALE, None, ALU.mult))
            make(dve.tensor_copy(bias_parts[:, 0, :], key_bias[:]))
            make(dve.tensor_tensor(key_res[:], key_bias[:], bias_parts[:, 0, :], ALU.subtract))
            make(dve.tensor_copy(bias_parts[:, 1, :], key_res[:]))
            make(dve.tensor_tensor(bias_parts[:, 2, :], key_res[:], bias_parts[:, 1, :], ALU.subtract))
            dve.wait_ge(enc_sb.sem, 3)
            make(dve.tensor_tensor(kxr[:], kxf[:], kx_parts[:, 0, :], ALU.subtract))
            make(dve.tensor_copy(kx_parts[:, 1, :], kxr[:]))
            make(dve.tensor_tensor(kx_parts[:, 2, :], kxr[:], kx_parts[:, 1, :], ALU.subtract))
            dve.wait_ge(enc_ps.sem, 3)
            for half in range(2):
                src = pw[:, 2, 0:T].rearrange("p (g a j d) -> p g a j d", a=2, j=4, d=HD)[:, :, half]
                dst = xv_st[:].rearrange("p t (s a j) c -> p (t s) a j c", s=2, a=2)[:, :, half, :,
                                                                                    16 * half:16 * half + HD]
                make(dve.tensor_copy(dst, src))
            assert steps[0] == SETUP_MADE

            def statistics(src, st, mv, s_stats, s_aggr, j):
                for t in range(NB):
                    dve.bn_stats(st[:, t, :], src[:, t, :]).then_inc(s_stats.sem, 1)
                dve.wait_ge(*s_stats.done(j))
                dve.memset(wait_slot[:], 0.0)
                for t in range(NB):
                    dve.bn_aggr(mv[:, t, :], st[:, t, :]).then_inc(s_aggr.sem, 1)
                dve.wait_ge(*s_aggr.done(j))

            def normalised(dst, src, mv, r, sig, j):
                for t in range(NB):
                    dve.tensor_scalar(dst[:, t, :], src[:, t, :], mv[:, t, 0:1], r[:, t:t + 1],
                                      ALU.subtract, ALU.mult).then_inc(sig.sem, 1)

            def residual_parts(f, r, parts, f_sig, hi_sig, r_sig, mid_sig, before, j):
                dve.wait_ge(*f_sig.done(j))
                dve.wait_ge(*hi_sig.done(j))
                dve.wait_ge(*before)
                dve.tensor_tensor(r[:], f[:], parts[:, 0, :], ALU.subtract).then_inc(r_sig.sem, 1)
                dve.wait_ge(*r_sig.done(j))
                dve.tensor_copy(parts[:, 1, :], r[:]).then_inc(mid_sig.sem, 1)

            def front(j):
                dve.wait_ge(*x_in.done(j))
                statistics(x_tm, stx, mvx, sa.stats, sa.aggr, j)
                dve.tensor_scalar(tiny[:, 0, :], mvx[:, :, 1], EPS, None, ALU.add).then_inc(var_y.sem, 1)
                dve.wait_ge(*rstd_y.done(j))
                dve.tensor_tensor(tiny[:, 2, :], tiny[:, 1, :], tiny[:, 1, :], ALU.mult).then_inc(var_y.sem, 1)
                dve.wait_ge(*var_y.part(j, 2))
                dve.tensor_tensor(tiny[:, 7, :], tiny[:, 2, :], mvx[:, :, 1], ALU.mult).then_inc(sa.var_eps.sem, 1)
                dve.wait_ge(*sa.var_eps.done(j))
                dve.tensor_scalar(tiny[:, 3, :], tiny[:, 7, :], EPS, None, ALU.add).then_inc(var_y.sem, 1)
                dve.wait_ge(*ca.h.before(j))
                normalised(y_tm, x_tm, mvx, tiny[:, 1, :], y_ready, j)
                dve.wait_ge(*rstd_01.done(j))
                dve.tensor_tensor(tiny[:, 5, :], tiny[:, 1, :], tiny[:, 4, :], ALU.mult).then_inc(sa.rstd.sem, 1)
                dve.wait_ge(*sa.rstd.done(j))
                dve.wait_ge(*ca.xT_ps.before(j))
                normalised(x1_tm, x_tm, mvx, tiny[:, 5, :], sa.x_ready, j)
                residual_parts(qf, qr, q_parts, sa.qf, sa.qhi, sa.qr, sa.qmid, ca.qlo.before(j), j)
                residual_parts(kf, kr, k_parts, sa.kf, sa.khi, sa.kr, sa.kmid, sa.klo.before(j), j)

            def maxima(a, j):
                for g in range(H):
                    b, hh = divmod(g, H // 2)
                    banks = pa[:, 2 * (g % 2):2 * (g % 2) + 2, :]
                    dve.wait_ge(*a.s_ps.part(j, g + 1))
                    dve.tensor_reduce(rowmax[:, b, 1, 2 * hh:2 * hh + 2], banks[:, :, 0:T], AX.X,
                                      ALU.max).then_inc(a.s_max.sem, 1)
                    dve.tensor_reduce(rowmax[:, b, 0, 2 * hh:2 * hh + 2], banks[:, :, T:T + a.seen], AX.X,
                                      ALU.max).then_inc(a.s_max.sem, 1)
                mx = rowmax[:].rearrange("p b q h -> p (b q) h")
                dve.wait_ge(*a.s_max.done(j))
                dve.tensor_copy(max_parts[:, :, 0, :], mx).then_inc(a.m1.sem, 1)
                dve.wait_ge(*a.m1.done(j))
                dve.tensor_tensor(max_res[:], mx, max_parts[:, :, 0, :], ALU.subtract).then_inc(a.mr.sem, 1)
                dve.wait_ge(*a.mr.done(j))
                dve.tensor_copy(max_parts[:, :, 1, :], max_res[:]).then_inc(a.m2.sem, 1)
                dve.wait_ge(*a.m2.done(j))
                dve.tensor_tensor(max_parts[:, :, 2, :], max_res[:], max_parts[:, :, 1, :],
                                  ALU.subtract).then_inc(a.m3.sem, 1)

            def normalise_context(a, j):
                for n in range(2):
                    blocks = pw[:, n, :].rearrange("p (g c) -> p g c", c=16)
                    dve.wait_ge(*a.cT_ps.part(j, n + 1))
                    r = rden[:, 2 * n:2 * n + 2, :].rearrange("p t h -> p (t h)")
                    dve.reciprocal(r, blocks[:, :, HD]).then_inc(a.rden.sem, 1)
                    dve.wait_ge(*a.rden.part(j, n + 1))
                    dve.tensor_tensor(ctx_tm[:, 2 * n:2 * n + 2, :].rearrange("p t (g d) -> p (t g) d", d=HD),
                                      blocks[:, :, 0:HD],
                                      r.rearrange("p (g o) -> p g o", o=1).to_broadcast([128, 32, HD]),
                                      ALU.mult).then_inc(a.ctx_n.sem, 1)

            def add_residual(a, dst, base, ready, before, j):
                dve.wait_ge(*a.o_ps.done(j))
                dve.wait_ge(*ready)
                for w in before:
                    dve.wait_ge(*w)
                dve.tensor_tensor(dst[:].rearrange("p t f -> p (t f)"), pw[:, 3, :],
                                  base[:].rearrange("p t f -> p (t f)"), ALU.add).then_inc(a.h.sem, 1)

            def after_self(j):
                add_residual(sa, h1, y_tm, yb_ready.done(j), [], j)
                dve.wait_ge(*sa.h.done(j))
                statistics(h1, stx, mvx, ca.stats, ca.aggr, j)
                dve.tensor_scalar(tiny[:, 5, :], mvx[:, :, 1], EPS, None, ALU.add).then_inc(ca.var_eps.sem, 1)
                dve.wait_ge(*ca.rstd.done(j))
                dve.wait_ge(*sa.xT_ps.done(j))
                normalised(x1_tm, h1, mvx, tiny[:, 6, :], ca.x_ready, j)

            def middle(j):
                residual_parts(qf, qr, q_parts, ca.qf, ca.qhi, ca.qr, ca.qmid, sa.qlo.done(j), j)

            def norm_stats(n, src, ready, j):
                dve.wait_ge(*ready)
                statistics(src, sty, mvy, n.stats, n.aggr, j)
                dve.tensor_scalar(tiny_y[:, 0, :], mvy[:, :, 1], EPS, None, ALU.add).then_inc(n.var_eps.sem, 1)
                dve.wait_ge(*n.rstd.done(j))

            def mlp(j):
                norm_stats(n_mlp, h2, ca.h.done(j), j)
                normalised(x3_tm, h2, mvy, tiny_y[:, 1, :], n_mlp.out, j)
                dve.wait_ge(*n_mlp.out.done(j))
                dve.tensor_tensor(h2[:], h2[:], bmlp[:].rearrange("p (o f) -> p o f", o=1).to_broadcast([128, NB, D]),
                                  ALU.add).then_inc(h2b.sem, 1)
                dve.wait_ge(*h2b.done(j))
                dve.wait_ge(*mlp_ps.done(j))
                dve.tensor_tensor(h3[:].rearrange("p t f -> p (t f)"), pa[:, 1, :],
                                  h2[:].rearrange("p t f -> p (t f)"), ALU.add).then_inc(h3_sb.sem, 1)
                norm_stats(n_post, h3, h3_sb.done(j), j)
                normalised(h3, h3, mvy, tiny_y[:, 1, :], n_post.out, j)
                dve.wait_ge(*n_post.out.done(j))
                dve.wait_ge(*x_kept.done(j))
                dve.tensor_tensor(xn[:], h3[:], x_keep[:], ALU.add).then_inc(xn_ready.sem, 1)
                norm_stats(n_z, xn, xn_ready.done(j), j)
                normalised(z_tm, xn, mvy, tiny_y[:, 1, :], n_z.out, j)

            def router(j):
                def over_e(x):
                    return x.rearrange("p (t o) -> p t o", o=1).to_broadcast([128, NB, NE])

                dve.wait_ge(*gate_ps.done(j))
                dve.tensor_tensor(logit[:], pa[:, 3, 0:NB * NE].rearrange("p (t e) -> p t e", e=NE),
                                  bgate[:].rearrange("p (o e) -> p o e", o=1).to_broadcast([128, NB, NE]),
                                  ALU.add).then_inc(route.sem, 1)
                dve.wait_ge(*route.part(j, 1))
                dve.tensor_reduce(rt[:, 0, :], logit[:], AX.X, ALU.max).then_inc(route.sem, 1)
                dve.wait_ge(*route.part(j, 2))
                dve.tensor_tensor(logit[:], logit[:], over_e(rt[:, 0, :]), ALU.subtract).then_inc(route.sem, 1)
                dve.wait_ge(*gate_exp.done(j))
                dve.tensor_reduce(rt[:, 1, :], prob[:], AX.X, ALU.add).then_inc(route.sem, 1)
                dve.wait_ge(*route.part(j, 4))
                dve.reciprocal(rt[:, 2, :], rt[:, 1, :]).then_inc(route.sem, 1)
                dve.wait_ge(*route.part(j, 5))
                dve.tensor_tensor(logit[:], prob[:], over_e(rt[:, 2, :]), ALU.mult).then_inc(route.sem, 1)
                dve.wait_ge(*route.part(j, 6))
                for t in range(NB):
                    other = logit[:, t, :].rearrange("p (o e) -> p o e", o=1).to_broadcast([128, NE, NE])
                    own = logit[:, t, :].rearrange("p (e o) -> p e o", o=1).to_broadcast([128, NE, NE])
                    pairs = more[:, t, :].rearrange("p (e f) -> p e f", f=NE)
                    ties = same[:, t, :].rearrange("p (e f) -> p e f", f=NE)
                    dve.tensor_tensor(pairs, other, own, ALU.is_gt).then_inc(n_rank.sem, 1)
                    dve.tensor_tensor(ties, other, own, ALU.is_equal).then_inc(n_rank.sem, 1)
                dve.wait_ge(*n_rank.part(j, 2 * NB))
                dve.tensor_tensor(same[:], same[:], lower[:].rearrange("p (o e) f -> p o (e f)", o=1)
                                  .to_broadcast([128, NB, NE * NE]), ALU.mult).then_inc(n_rank.sem, 1)
                dve.wait_ge(*n_rank.part(j, 2 * NB + 1))
                dve.tensor_tensor(more[:], more[:], same[:], ALU.add).then_inc(n_rank.sem, 1)
                dve.wait_ge(*n_rank.part(j, 2 * NB + 2))
                dve.tensor_reduce(rank[:], more[:].rearrange("p t (e f) -> p (t e) f", f=NE), AX.X,
                                  ALU.add).then_inc(n_rank.sem, 1)
                dve.wait_ge(*n_rank.done(j))
                dve.scalar_tensor_tensor(out=gates[:, :, 0:NE], in0=rank[:], scalar=1.5, in1=logit[:],
                                         op0=ALU.is_lt, op1=ALU.mult).then_inc(route.sem, 3)

            def experts(j, first, last):
                for n in range(first, last):
                    e = n - 1 if n else NE
                    dve.wait_ge(*silu.part(j, n + 1))
                    dve.wait_ge(*b_ps.part(j, n + 1))
                    if n >= 2:
                        dve.wait_ge(*e_ps.part(j, n - 1))
                    dve.scalar_tensor_tensor(out=hT[:, n % 2, :], in0=pa[:, 1, :], scalar=b1[:, e, 1:2],
                                             in1=silu_a[:], op0=ALU.add, op1=ALU.mult).then_inc(h_sb.sem, 1)
                    if n > first:
                        gather(j, n - 1)
                gather(j, last - 1)

            def gather(j, n):
                dve.wait_ge(*e_ps.part(j, n + 1))
                if n == 0:
                    dve.tensor_copy(acc[:].rearrange("p t f -> p (t f)"), pa[:, 2, :]).then_inc(acc_sb.sem, 1)
                else:
                    for t in range(NB):
                        dve.wait_ge(*acc_sb.part(j, 1 if n == 1 else 1 + NB * (n - 2) + t + 1))
                        dve.scalar_tensor_tensor(out=acc[:, t, :], in0=pa[:, 2 + n % 2, t * D:(t + 1) * D],
                                                 scalar=gates[:, t, n - 1:n], in1=acc[:, t, :],
                                                 op0=ALU.mult, op1=ALU.add).then_inc(acc_sb.sem, 1)

            def finish(j):
                norm_stats(n_end, acc, acc_sb.done(j), j)
                normalised(acc, acc, mvy, tiny_y[:, 1, :], n_end.out, j)
                dve.wait_ge(*n_end.out.done(j))
                dve.wait_ge(*o_dma.before(j))
                for t in range(NB):
                    dve.tensor_tensor(o_tm[:, t, :], acc[:, t, :], xn[:, t, :], ALU.add).then_inc(o_ready.sem, 1)

            def body(j, behind):
                front(j)
                if behind:
                    mlp(j - 1)
                maxima(sa, j)
                if behind:
                    router(j - 1)
                    experts(j - 1, 0, 1)
                    experts(j - 1, 1, 3)
                normalise_context(sa, j)
                if behind:
                    experts(j - 1, 3, 4)
                after_self(j)
                if behind:
                    experts(j - 1, 4, 6)
                middle(j)
                maxima(ca, j)
                if behind:
                    experts(j - 1, 6, 8)
                    experts(j - 1, 8, 9)
                    finish(j - 1)
                normalise_context(ca, j)
                add_residual(ca, h2, h1, h1b.done(j), [], j)

            body(0, False)
            body(1, True)
            with dve.Fori(2, PAIRS) as i:
                body(i, True)
            mlp(PAIRS - 1)
            router(PAIRS - 1)
            experts(PAIRS - 1, 0, 1)
            experts(PAIRS - 1, 1, NE + 1)
            finish(PAIRS - 1)

        @block.tensor
        def _(pe):
            pe.wait_ge(shaped.sem, 9)
            pe.wait_ge(loaded.sem, 16 * LOADS[0])
            for k in range(2):
                last = pe.transpose(pw[:, 0, k * 128:(k + 1) * 128], enc_tm[:, k, :], identf[:])
            last.then_inc(enc_ps.sem, 1)
            pe.wait_ge(made.sem, 8)
            pe.wait_ge(enc_sb.sem, 1)
            pe.matmul(pw[:, 1, 0:T], wxk[:], encT[:], start=True, stop=True).then_inc(enc_ps.sem, 1)
            for k in range(2):
                last = pe.matmul(pw[:, 2, k * D:(k + 1) * D], encT[:, k * 128:(k + 1) * 128], wxkv[:, D:2 * D],
                                 start=True, stop=True)
            last.then_inc(enc_ps.sem, 1)
            pe.wait_ge(made.sem, SETUP_MADE)
            pe.wait_ge(xk_dma.sem, 16 * 9)

            def transposes(bank, src, sig):
                for t in range(NB):
                    last = pe.transpose(bank[:, t * 128:(t + 1) * 128], src[:, t, :], identf[:])
                last.then_inc(sig.sem, 1)

            def front(j):
                pe.wait_ge(*sa.x_ready.done(j))
                pe.wait_ge(*ca.ctx_n.before(j))
                transposes(pw[:, 0, :], x1_tm, sa.xT_ps)
                pe.wait_ge(*sa.xT_sb.done(j))
                pe.matmul(pw[:, 1, :], wq[:], xT[:], start=True, stop=True).then_inc(sa.q_ps.sem, 1)
                pe.wait_ge(*ca.nT_sb.before(j))
                pe.matmul(pw[:, 2, :], wk[:], xT[:], start=True, stop=True).then_inc(sa.k_ps.sem, 1)
                pe.wait_ge(*ca.h.before(j))
                for t in range(NB):
                    last = pe.matmul(pw[:, 3, t * D:(t + 1) * D], xT[:, t * 128:(t + 1) * 128], wqkv[:, 2 * D:3 * D],
                                     start=True, stop=True)
                last.then_inc(sa.v_ps.sem, 1)

            def scores(a, j):
                pe.wait_ge(*a.q_dma.done(j))
                if not a.cross:
                    pe.wait_ge(*a.k_dma.done(j))
                for g in range(H):
                    b, hh = divmod(g, H // 2)
                    if g >= 2:
                        pe.wait_ge(*a.s_max.part(j, 2 * (g - 1)))
                    for h in (2 * hh, 2 * hh + 1):
                        bank = pa[:, 2 * (g % 2) + h % 2, :]
                        q0 = b * T
                        k0 = 0 if a.cross else b * T
                        pe.matmul(bank[:, 0:T], a.qop[0:ROWS_S, h, q0 + 128:q0 + 256], a.kop[0:ROWS_S, h, k0:k0 + T],
                                  start=True, stop=False, skip_group_check=True)
                        pe.matmul(bank[:, T:T + a.seen], a.qop[0:ROWS_S, h, q0:q0 + 128],
                                  a.kop[0:ROWS_S, h, k0:k0 + a.seen], start=False, stop=False, skip_group_check=True)
                        mask = a.mq[:] if a.cross else a.mq[:].rearrange("p a b -> p (a b)")
                        last = pe.matmul(bank[:, 128:T + a.seen], identb[:], mask, start=False, stop=True,
                                         skip_group_check=True)
                    last.then_inc(a.s_ps.sem, 1)

            def max_rows(a, j):
                pe.wait_ge(*a.m3.done(j))
                pe.wait_ge(*(sa.xT_sb.done(j) if a is sa else ca.xT_sb.done(j)))
                for t in range(NB):
                    last = pe.transpose(pw[:, 0, :].bitcast(BF16)[:, t * 128:(t + 1) * 128],
                                        max_parts[:, t].rearrange("p a h -> p (a h)"), identb[:])
                last.then_inc(a.mT_ps.sem, 1)

            def score_group(a, g, j):
                s, b, aa, jj = g // 8, g // 4 % 2, g // 2 % 2, g % 2
                if g >= 2:
                    pe.wait_ge(*a.exp.part(j, g - 1))
                q0 = b * T
                k0 = 0 if a.cross else b * T
                late = T - a.seen
                for n in range(2):
                    h = 8 * s + 4 * aa + 2 * jj + n
                    bank = pa[:, 2 * (g % 2) + n, :]
                    pe.matmul(bank[:, 0:T], a.kop[0:ROWS_ST, h, k0:k0 + 128], a.qop[0:ROWS_ST, h, q0:q0 + T],
                              start=True, stop=False, skip_group_check=True)
                    pe.matmul(bank[:, T:T + a.seen], a.kop[0:ROWS_ST, h, k0 + 128:k0 + T],
                              a.qop[0:ROWS_ST, h, q0 + late:q0 + T], start=False, stop=False, skip_group_check=True)
                    if a.cross:
                        pe.matmul(bank[:, 0:128], identb[:], a.mk[:, 0:128], start=False, stop=False, skip_group_check=True)
                        last = pe.matmul(bank[:, T:T + XW], identb[:], a.mk[:, 128:128 + XW], start=False, stop=True,
                                         skip_group_check=True)
                    else:
                        pe.matmul(bank[:, 0:128], identb[:], a.mk[:, 0, :], start=False, stop=False, skip_group_check=True)
                        last = pe.matmul(bank[:, T:T + 128], identb[:], a.mk[:, 1, :], start=False, stop=True,
                                         skip_group_check=True)
                last.then_inc(a.st_ps.sem, 1)

            def value_group(a, four, j):
                s, b, aa = four // 4, four // 2 % 2, four % 2
                pe.wait_ge(*a.exp.part(j, 2 * four + 2))
                late = T - a.seen
                bank = pw[:, 2 + s, :]
                for half in range(2):
                    for jj in range(4):
                        h = 8 * s + 4 * aa + jj
                        v = a.v[:, half if a.cross else 2 * b + half, h, :]
                        q0 = b * T + (late if half else 0)
                        last = pe.matmul(bank[32 * jj:32 * jj + 32, q0:(b + 1) * T], v,
                                         probs[:, four % 2, jj, (T if half else 0):(T + a.seen if half else T)],
                                         start=(aa == 0 and half == 0), stop=(aa == 1 and half == 1),
                                         skip_group_check=True)
                last.then_inc(a.pv.sem, 1)

            def attend(a, j):
                pe.wait_ge(*a.m_dma.done(j))
                if not a.cross:
                    pe.wait_ge(*a.v_sb.done(j))
                    pe.wait_ge(*a.khi.done(j))
                else:
                    pe.wait_ge(*sa.nT_sb.done(j))
                    pe.wait_ge(*sa.h.done(j))
                pe.wait_ge(*a.s_max.done(j))
                for four in range(8):
                    score_group(a, 2 * four, j)
                    score_group(a, 2 * four + 1, j)
                    if four:
                        value_group(a, four - 1, j)
                value_group(a, 7, j)

            def context_T(a, j):
                pe.wait_ge(*a.mT_sb.done(j))
                pe.wait_ge(*a.qhi.done(j))
                pe.wait_ge(*a.ctx_sb.done(j))
                for n in range(2):
                    for t in (2 * n, 2 * n + 1):
                        for s in range(2):
                            at = (t % 2) * 256 + s * 128
                            last = pe.transpose(pw[:, n, at:at + 128], ctx_fm[:, s, t * 128:(t + 1) * 128], identf[:])
                    last.then_inc(a.cT_ps.sem, 1)

            def context_back(a, j):
                pe.wait_ge(*a.ctx_n.done(j))
                transposes(pw[:, 2, :], ctx_tm, a.nT_ps)

            def project(a, w, j):
                pe.wait_ge(*a.nT_sb.done(j))
                for t in range(NB):
                    last = pe.matmul(pw[:, 3, t * D:(t + 1) * D], ctxT[:, t * 128:(t + 1) * 128], w[:],
                                     start=True, stop=True)
                last.then_inc(a.o_ps.sem, 1)

            def cross_query(j):
                pe.wait_ge(*ca.x_ready.done(j))
                transposes(pw[:, 0, :], x1_tm, ca.xT_ps)
                pe.wait_ge(*ca.xT_sb.done(j))
                pe.matmul(pw[:, 1, :], wxq[:], xT[:], start=True, stop=True).then_inc(ca.q_ps.sem, 1)

            def mlp(j):
                pe.wait_ge(*n_mlp.out.done(j))
                pe.wait_ge(*ca.exp.done(j))
                transposes(pa[:, 0, :], x3_tm, x3T_ps)
                pe.wait_ge(*x3T_sb.done(j))
                for c in range(NC):
                    pe.matmul(pa[:, (c + 1) % 4, :], wfc[:, c * 128:(c + 1) * 128], x3T[:], start=True,
                              stop=True).then_inc(fc_ps.sem, 1)
                pe.wait_ge(*gelu.done(j))
                for t in range(NB):
                    for c in range(NC):
                        last = pe.matmul(pa[:, 1, t * D:(t + 1) * D], geluT[:, c, t * 128:(t + 1) * 128], wmlp[:, c, :],
                                         start=(c == 0), stop=(c == NC - 1))
                last.then_inc(mlp_ps.sem, 1)

            def router(j):
                pe.wait_ge(*n_z.out.done(j))
                transposes(pa[:, 2, :], z_tm, zT_ps)
                pe.wait_ge(*zT_sb.done(j))
                for t in range(NB):
                    last = pe.matmul(pa[:, 3, t * NE:(t + 1) * NE], zT[:, t * 128:(t + 1) * 128], wgate[:],
                                     start=True, stop=True)
                last.then_inc(gate_ps.sem, 1)

            def up(j, n):
                e = n - 1 if n else NE
                if n:
                    pe.wait_ge(*silu.part(j, n))
                pe.matmul(pa[:, 0, :], w1[:, e, 0:128], zT[:], start=True, stop=True).then_inc(a_ps.sem, 1)
                if n:
                    pe.wait_ge(*h_sb.part(j, n))
                pe.matmul(pa[:, 1, :], w1[:, e, 128:256], zT[:], start=True, stop=True).then_inc(b_ps.sem, 1)

            def down(j, n):
                e = n - 1 if n else NE
                if n >= 2:
                    pe.wait_ge(*acc_sb.part(j, 1 + NB * (n - 2)))
                if n == 0:
                    pe.wait_ge(*route.done(j))
                    for t in range(NB):
                        last = pe.transpose(pa[0:NE + 1, 3, t * 128:(t + 1) * 128], gates[:, t, :], identf[:])
                    last.then_inc(gatesT_ps.sem, 1)
                    pe.wait_ge(*gatesT_sb.done(j))
                pe.wait_ge(*h_sb.part(j, n + 1))
                for t in range(NB):
                    to = pa[:, 2 + n % 2, t * D:(t + 1) * D]
                    last = pe.matmul(to, hT[:, n % 2, t * 128:(t + 1) * 128], w2[:, e, :], start=True, stop=(n > 0))
                    if n == 0:
                        last = pe.matmul(to, gatesT[:, t * 128:(t + 1) * 128], b2[:], start=False, stop=True)
                last.then_inc(e_ps.sem, 1)

            def experts(j, first, last):
                up(j, first)
                for n in range(first + 1, last):
                    up(j, n)
                    down(j, n - 1)
                down(j, last - 1)

            def shared_banks_free(j, n):
                pe.wait_ge(*acc_sb.part(j, 1 + NB * (n - 1)))

            def body(j, behind):
                front(j)
                if behind:
                    mlp(j - 1)
                    pe.wait_ge(*h3_sb.done(j - 1))
                else:
                    pass
                scores(sa, j)
                if behind:
                    pe.wait_ge(*sa.s_max.done(j))
                    router(j - 1)
                    experts(j - 1, 0, 1)
                max_rows(sa, j)
                if behind:
                    experts(j - 1, 1, 3)
                    shared_banks_free(j - 1, 3)
                attend(sa, j)
                context_T(sa, j)
                if behind:
                    pe.wait_ge(*sa.exp.done(j))
                    experts(j - 1, 3, 4)
                context_back(sa, j)
                project(sa, wo, j)
                if behind:
                    experts(j - 1, 4, 6)
                cross_query(j)
                if behind:
                    shared_banks_free(j - 1, 6)
                else:
                    pe.wait_ge(*sa.exp.done(j))
                scores(ca, j)
                if behind:
                    pe.wait_ge(*ca.s_max.done(j))
                    experts(j - 1, 6, 8)
                max_rows(ca, j)
                if behind:
                    experts(j - 1, 8, 9)
                    shared_banks_free(j - 1, 9)
                attend(ca, j)
                context_T(ca, j)
                context_back(ca, j)
                project(ca, wxo, j)

            body(0, False)
            body(1, True)
            with pe.Fori(2, PAIRS) as i:
                body(i, True)
            mlp(PAIRS - 1)
            pe.wait_ge(*h3_sb.done(PAIRS - 1))
            router(PAIRS - 1)
            experts(PAIRS - 1, 0, 1)
            experts(PAIRS - 1, 1, NE + 1)


_INS = ['hidden_states', 'encoder_hidden_states', 'scorer_logits', 'ln1_g', 'ln1_b', 'c_attn_w', 'c_attn_b',
        'attn_proj_w', 'attn_proj_b', 'lnx_g', 'lnx_b', 'q_attn_w', 'q_attn_b', 'x_kv_w', 'x_kv_b', 'x_proj_w',
        'x_proj_b', 'ln2_g', 'ln2_b', 'fc_w', 'fc_b', 'mlp_proj_w', 'mlp_proj_b']
_FFN = ['gate_w', 'gate_b', 'sw1', 'sb1', 'sw2', 'sb2', 'rw1', 'rb1', 'rw2', 'rb2']


def kernel(**inputs):
    import numpy as _np
    import concourse.bacc as _bacc
    from concourse import mybir as _mybir
    from concourse.bass_utils import run_bass_kernel_spmd as _run

    nc = _bacc.Bacc("TRN2", target_bir_lowering=False, num_devices=1)
    names = ["L0_attn_" + n for n in _INS] + ["L0_ffn_" + n for n in _FFN]
    arrays, args = {}, []
    for name in names:
        a = _np.ascontiguousarray(inputs[name])
        arrays[f"in_{name}"] = a
        args.append(nc.dram_tensor(f"in_{name}", a.shape, _mybir.dt.from_np(a.dtype), kind="ExternalInput").ap())
    shape = arrays["in_L0_attn_hidden_states"].shape
    out = nc.dram_tensor("out_0", shape, F32, kind="ExternalOutput").ap()
    sandwich_kernel(nc, out, *args)
    r = _run(nc, [arrays], core_ids=[0])
    return r.results[0]["out_0"]
```

```python
import concourse.bass as bass
from concourse import mybir
from contextlib import ExitStack

F32 = mybir.dt.float32
BF16 = mybir.dt.bfloat16
ALU = mybir.AluOpType
ACT = mybir.ActivationFunctionType
AX = mybir.AxisListType


class Names:
    pass


class Signal:

    def __init__(self, sem, per, pairs):
        self.sem, self.per, self.pairs = sem, per, pairs

    def done(self, j):
        return self.sem, j + 1 if self.per == 1 else j * self.per + self.per

    def part(self, j, k):
        return self.sem, j * self.per + k

    def before(self, j):
        if isinstance(j, int):
            j = min(max(j, 0), self.pairs)
        return self.sem, j if self.per == 1 else j * self.per


def sandwich_kernel(nc, out, hs, enc, scorer, ln1_g, ln1_b, c_attn_w, c_attn_b, attn_proj_w, attn_proj_b,
                    lnx_g, lnx_b, q_attn_w, q_attn_b, x_kv_w, x_kv_b, x_proj_w, x_proj_b, ln2_g, ln2_b,
                    fc_w, fc_b, mlp_proj_w, mlp_proj_b, gate_w, gate_b, sw1, sb1, sw2, sb2, rw1, rb1, rw2, rb2):
    B, T, D = hs.shape
    H, HD = 16, 8
    NE = rw1.shape[0]
    NC = fc_w.shape[1] // 128
    PAIRS = B // 2
    NT = 2 * T
    NB = NT // 128
    EPS = 1e-5
    SCALE = float(HD) ** -0.5
    MASKED = -3.0e38
    QPARTS = [0, 1, 2, 0, 1, 0]
    KPARTS = [0, 0, 0, 1, 1, 2]
    ROW_BIAS, ROWS_S, ROW_MAX, ROWS_ST = 64, 96, 96, 99
    XW = 130

    ctx = ExitStack()
    with ctx:
        ctx.enter_context(nc.allow_non_contiguous_dma(reason="small vectors and permuted rows, once"))

        def sb(name, shape, dt=F32):
            return ctx.enter_context(nc.sbuf_tensor(name, shape, dt))

        def signal(name, per):
            return Signal(ctx.enter_context(nc.semaphore(name)), per, PAIRS)

        identf = sb("identf", [128, 128])
        identb = sb("identb", [128, 128], BF16)
        mask_q = sb("mask_q", [128, 2, 128], BF16)
        mask_k = sb("mask_k", [128, 2, 128], BF16)
        xmask_q = sb("xmask_q", [128, 128 + XW], BF16)
        xmask_k = sb("xmask_k", [128, 128 + XW], BF16)
        lower = sb("lower", [128, NE, NE])
        half_neg = sb("half_neg", [128, NB])
        wqkv = sb("wqkv", [128, 3 * D])
        wq = sb("wq", [128, D])
        wk = sb("wk", [128, D])
        wo = sb("wo", [128, D])
        wxq0 = sb("wxq0", [128, D])
        wxq = sb("wxq", [128, D])
        wxkv = sb("wxkv", [128, 2 * D])
        wxk = sb("wxk", [128, D])
        wxo = sb("wxo", [128, D])
        wfc = sb("wfc", [128, NC * 128])
        wmlp = sb("wmlp", [128, NC, D])
        wgate = sb("wgate", [128, NE])
        w1 = sb("w1", [128, NE + 1, 2 * 128])
        w2 = sb("w2", [128, NE + 1, D])
        b1 = sb("b1", [128, NE + 1, 2])
        b2 = sb("b2", [NE + 1, D])
        cols = sb("cols", [128, 16])
        G1, B1, GX, BX, G2, B2, BQ, BK, BV, BXQ, BXK, BXV, BQS, BXQS = range(14)
        bfc = sb("bfc", [128, NC])
        bo = sb("bo", [128, D])
        bxo = sb("bxo", [128, D])
        bmlp = sb("bmlp", [128, D])
        bgate = sb("bgate", [128, NE])
        enc_tm = sb("enc_tm", [128, 2, D])
        encT = sb("encT", [128, T])
        kxf = sb("kxf", [128, T])
        kxr = sb("kxr", [128, T])
        kx_parts = sb("kx_parts", [128, 3, T], BF16)
        key_bias = sb("key_bias", [1, T])
        key_res = sb("key_res", [1, T])
        bias_parts = sb("bias_parts", [1, 3, T], BF16)

        q_op = sb("q_op", [128, H, NT], BF16)
        k_op = sb("k_op", [128, H, NT], BF16)
        xq_op = sb("xq_op", [128, H, NT], BF16)
        xk_op = sb("xk_op", [128, H, T], BF16)
        v_st = sb("v_st", [128, NB, H, 32])
        xv_st = sb("xv_st", [128, 2, H, 32])

        x_tm = sb("x_tm", [128, NB, D])
        x_keep = sb("x_keep", [128, NB, D])
        y_tm = sb("y_tm", [128, NB, D])
        yb_tm = sb("yb_tm", [128, NB, D])
        x1_tm = sb("x1_tm", [128, NB, D])
        x2_tm = sb("x2_tm", [128, NB, D])
        xT = sb("xT", [128, NT])
        qf = sb("qf", [128, NT])
        kf = sb("kf", [128, NT])
        qr = sb("qr", [128, NT])
        kr = sb("kr", [128, NT])
        xqf = sb("xqf", [128, NT])
        xqr = sb("xqr", [128, NT])
        xq_parts = sb("xq_parts", [128, 3, NT], BF16)
        q_parts = sb("q_parts", [128, 3, NT], BF16)
        k_parts = sb("k_parts", [128, 3, NT], BF16)
        rowmax = sb("rowmax", [128, 2, 2, H])
        max_res = sb("max_res", [128, NB, H])
        max_parts = sb("max_parts", [128, NB, 8, H], BF16)
        wait_slot = sb("wait_slot", [128, 1])
        maxT = sb("maxT", [3 * H, NT], BF16)
        probs = sb("probs", [128, 2, 4, T + XW])
        ctx_fm = sb("ctx_fm", [128, 2, NT])
        rden = sb("rden", [128, NB, H])
        ctx_tm = sb("ctx_tm", [128, NB, D])
        ctxT = sb("ctxT", [128, NT])
        h1 = sb("h1", [128, NB, D])
        h1b = sb("h1b", [128, NB, D])
        stx = sb("stx", [128, NB, 6])
        mvx = sb("mvx", [128, NB, 2])
        tiny = sb("tiny", [128, 8, NB])
        st2 = sb("st2", [128, NB, 6])
        mv2 = sb("mv2", [128, NB, 2])
        tiny2 = sb("tiny2", [128, 2, NB])
        st3 = sb("st3", [128, NB, 6])
        mv3 = sb("mv3", [128, NB, 2])
        tiny3 = sb("tiny3", [128, 2, NB])

        h2 = sb("h2", [128, NB, D])
        x3_tm = sb("x3_tm", [128, NB, D])
        x3T = sb("x3T", [128, NT])
        geluT = sb("geluT", [128, NC, NT])
        h3 = sb("h3", [128, NB, D])
        xn = sb("xn", [128, NB, D])
        z_tm = sb("z_tm", [128, NB, D])
        zT = sb("zT", [128, NT])
        logit = sb("logit", [128, NB, NE])
        prob = sb("prob", [128, NB, NE])
        rt = sb("rt", [128, 4, NB])
        more = sb("more", [128, NB, NE * NE])
        same = sb("same", [128, NB, NE * NE])
        rank = sb("rank", [128, NB, NE])
        gates = sb("gates", [128, NB, NE + 1])
        gatesT = sb("gatesT", [NE + 1, NT])
        silu_a = sb("silu_a", [128, NT])
        hT = sb("hT", [128, 2, NT])
        acc = sb("acc", [128, NB, D])
        o_tm = sb("o_tm", [128, NB, D])
        sty = sb("sty", [128, NB, 6])
        mvy = sb("mvy", [128, NB, 2])
        tiny_y = sb("tiny_y", [128, 4, NB])

        ps = ctx.enter_context(nc.psum_tensor("ps", [128, 8, 512], F32))

        loaded = signal("loaded", 0)
        filled = signal("filled", 0)
        shaped = signal("shaped", 0)
        padded = signal("padded", 0)
        made = signal("made", 0)
        enc_ps = signal("enc_ps", 0)
        enc_sb = signal("enc_sb", 0)
        xk_dma = signal("xk_dma", 0)
        x_in = signal("x_in", 16)
        x_kept = signal("x_kept", 16)
        y_ready = signal("y_ready", NB)
        yb_ready = signal("yb_ready", 1)
        var_y = signal("var_y", 3)
        rstd_y = signal("rstd_y", 1)
        rstd_01 = signal("rstd_01", 1)

        def attention(n, cross):
            a = Names()
            a.cross = cross
            a.qop, a.kop = (xq_op, xk_op) if cross else (q_op, k_op)
            a.mq, a.mk = (xmask_q, xmask_k) if cross else (mask_q, mask_k)
            a.seen = XW if cross else 128
            a.v = xv_st if cross else v_st
            a.stats, a.aggr = signal(n + "_stats", NB), signal(n + "_aggr", NB)
            a.var_eps, a.rstd = signal(n + "_var_eps", 1), signal(n + "_rstd", 1)
            a.x_ready = signal(n + "_x_ready", NB)
            a.xT_ps, a.xT_sb = signal(n + "_xT_ps", 1), signal(n + "_xT_sb", 1)
            a.q_ps, a.k_ps, a.v_ps = signal(n + "_q_ps", 1), signal(n + "_k_ps", 1), signal(n + "_v_ps", 1)
            a.qf, a.qhi = signal(n + "_qf", 1), signal(n + "_qhi", 1)
            a.qr, a.qmid, a.qlo = signal(n + "_qr", 1), signal(n + "_qmid", 1), signal(n + "_qlo", 1)
            a.kf, a.khi = signal(n + "_kf", 1), signal(n + "_khi", 1)
            a.kr, a.kmid, a.klo = signal(n + "_kr", 1), signal(n + "_kmid", 1), signal(n + "_klo", 1)
            a.v_sb = signal(n + "_v_sb", 2)
            a.q_dma, a.k_dma = signal(n + "_q_dma", 96), signal(n + "_k_dma", 96)
            a.s_ps, a.s_max = signal(n + "_s_ps", 2 * H), signal(n + "_s_max", 4 * H)
            a.m1, a.mr, a.m2, a.m3 = (signal(n + x, 1) for x in ("_m1", "_mr", "_m2", "_m3"))
            a.mT_ps, a.mT_sb, a.m_dma = signal(n + "_mT_ps", 1), signal(n + "_mT_sb", 1), signal(n + "_m_dma", 16)
            a.st_ps, a.exp, a.pv = signal(n + "_st_ps", H), signal(n + "_exp", H), signal(n + "_pv", 8)
            a.ctx_sb, a.cT_ps = signal(n + "_ctx_sb", 2), signal(n + "_cT_ps", 2)
            a.rden, a.ctx_n = signal(n + "_rden", 2), signal(n + "_ctx_n", 2)
            a.nT_ps, a.nT_sb = signal(n + "_nT_ps", 1), signal(n + "_nT_sb", 1)
            a.o_ps, a.h = signal(n + "_o_ps", 1), signal(n + "_h", 1)
            return a

        sa = attention("self", False)
        ca = attention("cross", True)
        h1b_ready = signal("h1b_ready", 1)
        h2b_ready = signal("h2b_ready", 1)

        def norm(n):
            a = Names()
            a.stats, a.aggr = signal(n + "_stats", NB), signal(n + "_aggr", NB)
            a.var_eps, a.rstd, a.out = signal(n + "_var_eps", 1), signal(n + "_rstd", 1), signal(n + "_out", NB)
            return a

        n_mlp, n_post, n_z, n_end = norm("n_mlp"), norm("n_post"), norm("n_z"), norm("n_end")
        x3T_ps, x3T_sb = signal("x3T_ps", 1), signal("x3T_sb", 1)
        fc_ps, gelu = signal("fc_ps", NC), signal("gelu", NC)
        mlp_ps, h3_sb = signal("mlp_ps", 1), signal("h3_sb", 1)
        xn_ready = signal("xn_ready", 1)
        zT_ps, zT_sb = signal("zT_ps", 1), signal("zT_sb", 1)
        gate_ps, route, gate_exp = signal("gate_ps", 1), signal("route", 9), signal("gate_exp", 1)
        n_rank = signal("n_rank", 2 * NB + 3)
        gatesT_ps, gatesT_sb = signal("gatesT_ps", 1), signal("gatesT_sb", 1)
        a_ps, b_ps, silu = signal("a_ps", NE + 1), signal("b_ps", NE + 1), signal("silu", NE + 1)
        h_sb, e_ps = signal("h_sb", NE + 1), signal("e_ps", NE + 1)
        acc_sb = signal("acc_sb", 1 + NB * NE)
        o_ready = signal("o_ready", NB)
        o_dma = signal("o_dma", 16)

        block = ctx.enter_context(nc.Block())
        wide = [(w, s) for w, s in ((wqkv, c_attn_w), (wxq0, q_attn_w), (wxkv, x_kv_w), (wfc, fc_w),
                                    (wgate, gate_w))]
        vectors = [(G1, ln1_g), (B1, ln1_b), (GX, lnx_g), (BX, lnx_b), (G2, ln2_g), (B2, ln2_b)]

        def rows_dh(v):
            return v.rearrange("(h d o) -> d h o", d=HD, o=1)

        def load_setup(eng, half):
            jobs = [(w[:], s) for w, s in wide]
            jobs += [(wmlp[:], mlp_proj_w.rearrange("(c p) n -> p c n", p=128))]
            jobs += [(w1[:, 0:NE, :], rw1.rearrange("e p n -> p e n")), (w1[:, NE, :], sw1[0])]
            jobs += [(w2[:, 0:NE, :], rw2.rearrange("e p n -> p e n")), (w2[:, NE, :], sw2[0])]
            jobs += [(b1[:, 0:NE, :], rb1.rearrange("e (a p) -> p e a", p=128)),
                     (b1[:, NE, :], sb1.rearrange("o (a p) -> p (o a)", p=128))]
            jobs += [(b2[0:NE, :], rb2), (b2[NE:NE + 1, :], sb2)]
            jobs += [(cols[:, n:n + 1], v.rearrange("(p o) -> p o", o=1)) for n, v in vectors]
            jobs += [(cols[:, BQ:BQ + 1], rows_dh(c_attn_b[0:D])), (cols[:, BK:BK + 1], rows_dh(c_attn_b[D:2 * D])),
                     (cols[:, BXQ:BXQ + 1], rows_dh(q_attn_b)), (cols[:, BXK:BXK + 1], rows_dh(x_kv_b[0:D]))]
            for s in range(2):
                for j in range(4):
                    p = (4 * s + j) * 16
                    for w, v in ((wo, attn_proj_w), (wxo, x_proj_w)):
                        jobs += [(w[p:p + 16, :], v.rearrange("(s a j d) n -> s j a d n", s=2, a=2, j=4)[s, j])]
                    for n, v in ((BV, c_attn_b[2 * D:3 * D]), (BXV, x_kv_b[D:2 * D])):
                        jobs += [(cols[p:p + 16, n:n + 1],
                                  v.rearrange("(s a j d o) -> s j a d o", s=2, a=2, j=4, o=1)[s, j])]
            jobs += [(bfc[:], fc_b.rearrange("(c p) -> p c", p=128))]
            jobs += [(w[:], v.rearrange("(o n) -> o n", o=1).to_broadcast([128, n]))
                     for w, v, n in ((bo, attn_proj_b, D), (bxo, x_proj_b, D), (bmlp, mlp_proj_b, D), (bgate, gate_b, NE))]
            jobs += [(enc_tm[:], enc[0].rearrange("(k p) f -> p k f", p=128)), (key_bias[:], scorer)]
            for o, i in jobs[half::2]:
                eng.dma_start(o, i).then_inc(loaded.sem, 16)
            return len(jobs)

        FC_BANKS = [6, 7, 5, 4]
        LOADS = []
        PADS = 14
        XK_PARTS = 17
        SETUP_MADE = XK_PARTS + 2

        def exists(*pairs):
            return all(not isinstance(j, int) or 0 <= j < PAIRS for j in pairs)

        def program(eng, body):
            for i in range(-1, 3):
                body(i)
            with eng.Fori(3, PAIRS - 2) as i:
                body(i)
            for i in range(PAIRS - 2, PAIRS + 2):
                body(i)

        @block.sync
        def _(sp):
            def pair_of(x, j):
                return x[bass.ds(sp.snap(2 * j), 2)].rearrange("b (q p) f -> p (b q) f", p=128)

            def load_x(j):
                src = pair_of(hs, j)
                sp.wait_ge(*y_ready.before(j))
                sp.wait_ge(*sa.x_ready.before(j))
                sp.dma_start(x_tm[:], src).then_inc(x_in.sem, 16)

            def keep_x(j):
                src = pair_of(hs, j)
                sp.wait_ge(*xn_ready.before(j))
                sp.dma_start(x_keep[:], src).then_inc(x_kept.sem, 16)

            def store_out(j):
                dst = pair_of(out, j)
                sp.wait_ge(*o_ready.done(j))
                sp.dma_start(dst, o_tm[:]).then_inc(o_dma.sem, 16)

            def operand(parts, op, which, hi, mid, lo, dma, j):
                for made_part, n in ((hi, 0), (mid, 1), (lo, 2)):
                    sp.wait_ge(*made_part.done(j))
                    for slot in range(6):
                        if which[slot] == n:
                            sp.dma_start(op[slot * HD:(slot + 1) * HD, :, :], parts[:, n, :]).then_inc(dma.sem, 16)

            def max_rows(a, j):
                sp.wait_ge(*a.mT_sb.done(j))
                sp.dma_start(a.qop[ROW_MAX:ROW_MAX + 3, :, :], maxT[:]).then_inc(a.m_dma.sem, 16)

            def body(i):
                if exists(i - 1):
                    max_rows(ca, i - 1)
                if exists(i + 1):
                    operand(q_parts, q_op, QPARTS, sa.qhi, sa.qmid, sa.qlo, sa.q_dma, i + 1)
                    operand(k_parts, k_op, KPARTS, sa.khi, sa.kmid, sa.klo, sa.k_dma, i + 1)
                if exists(i + 2):
                    load_x(i + 2)
                if exists(i - 2):
                    keep_x(i - 2)
                if exists(i + 1):
                    max_rows(sa, i + 1)
                if exists(i):
                    operand(xq_parts, xq_op, QPARTS, ca.qhi, ca.qmid, ca.qlo, ca.q_dma, i)
                if exists(i - 2):
                    store_out(i - 2)

            load_x(0)
            LOADS.append(load_setup(sp, 0))
            sp.wait_ge(padded.sem, PADS)
            sp.wait_ge(made.sem, XK_PARTS)
            for slot in range(6):
                sp.dma_start(xk_op[slot * HD:(slot + 1) * HD, :, :], kx_parts[:, KPARTS[slot], :]).then_inc(xk_dma.sem, 16)
            for n in range(3):
                sp.dma_start(xk_op[ROW_BIAS + n:ROW_BIAS + n + 1, :, :],
                             bias_parts[:, n:n + 1, :].to_broadcast([1, H, T])).then_inc(xk_dma.sem, 16)
            program(sp, body)
            sp.wait_ge(*o_dma.done(PAIRS - 1))

        @block.gpsimd
        def _(pool):
            pool.memset(identf[:], 0.0).then_inc(filled.sem, 1)
            pool.memset(identb[:], 0.0).then_inc(filled.sem, 1)
            pool.memset(mask_q[:], 0.0).then_inc(filled.sem, 1)
            pool.memset(mask_k[:], 0.0).then_inc(filled.sem, 1)
            pool.memset(xmask_q[:], 0.0).then_inc(filled.sem, 1)
            pool.memset(xmask_k[:], 0.0).then_inc(filled.sem, 1)
            pool.memset(lower[:], 1.0).then_inc(filled.sem, 1)
            pool.memset(half_neg[:], -0.5).then_inc(filled.sem, 1)
            pool.memset(gates[:], 1.0).then_inc(filled.sem, 1)
            pool.wait_ge(filled.sem, 9)

            def select(m, cmp, fill, base, pattern, channel):
                pool.affine_select(out=m, in_=m, compare_op=cmp, fill=fill, base=base, pattern=pattern,
                                   channel_multiplier=channel).then_inc(shaped.sem, 1)

            select(identf[:], ALU.not_equal, 1.0, 0, [[-1, 128]], 1)
            select(identb[:], ALU.not_equal, 1.0, 0, [[-1, 128]], 1)
            select(mask_q[:], ALU.is_ge, MASKED, 0, [[0, 2], [-1, 128]], 1)
            select(mask_k[:], ALU.is_ge, MASKED, 0, [[0, 2], [1, 128]], -1)
            select(xmask_q[:, 0:128], ALU.is_ge, MASKED, 2, [[-1, 128]], 1)
            select(xmask_q[:, 128:], ALU.is_ge, MASKED, 2, [[-1, XW]], 1)
            select(xmask_k[:, 0:128], ALU.is_ge, MASKED, 2, [[1, 128]], -1)
            select(xmask_k[:, 128:], ALU.is_ge, MASKED, 0, [[1, XW]], -1)
            select(lower[:], ALU.is_gt, 0.0, 0, [[1, NE], [-1, NE]], 0)

            def power(n_var, n_out, var, out_):
                pool.wait_ge(*n_var)
                pool.tensor_tensor(out_, var, half_neg[:], ALU.pow).then_inc(n_out.sem, 1)

            def low_part(r, parts, a_r, a_mid, a_lo, a_dma, j):
                pool.wait_ge(*a_r.done(j))
                pool.wait_ge(*a_mid.done(j))
                pool.wait_ge(*a_dma.before(j))
                pool.tensor_tensor(parts[:, 2, :], r[:], parts[:, 1, :], ALU.subtract).then_inc(a_lo.sem, 1)

            def add_bias(dst, base, bias, ready, before, out_sig):
                pool.wait_ge(*ready)
                pool.wait_ge(*before)
                pool.tensor_tensor(dst[:], base[:], bias[:].rearrange("p (o f) -> p o f", o=1).to_broadcast([128, NB, D]),
                                   ALU.add).then_inc(out_sig.sem, 1)

            def norm_y(j):
                power(var_y.part(j, 1), rstd_y, tiny[:, 0, :], tiny[:, 1, :])
                power(var_y.done(j), rstd_01, tiny[:, 3, :], tiny[:, 4, :])

            def body(i):
                if exists(i + 1):
                    low_part(qr, q_parts, sa.qr, sa.qmid, sa.qlo, sa.q_dma, i + 1)
                    low_part(kr, k_parts, sa.kr, sa.kmid, sa.klo, sa.k_dma, i + 1)
                if exists(i - 2):
                    power(n_post.var_eps.done(i - 2), n_post.rstd, tiny_y[:, 0, :], tiny_y[:, 1, :])
                if exists(i):
                    power(ca.var_eps.done(i), ca.rstd, tiny2[:, 0, :], tiny2[:, 1, :])
                if exists(i - 2):
                    power(n_z.var_eps.done(i - 2), n_z.rstd, tiny_y[:, 0, :], tiny_y[:, 1, :])
                if exists(i + 1):
                    add_bias(yb_tm, y_tm, bo, y_ready.done(i + 1), sa.h.before(i + 1), yb_ready)
                if exists(i):
                    low_part(xqr, xq_parts, ca.qr, ca.qmid, ca.qlo, ca.q_dma, i)
                if exists(i - 1):
                    power(n_mlp.var_eps.done(i - 1), n_mlp.rstd, tiny3[:, 0, :], tiny3[:, 1, :])
                if exists(i):
                    add_bias(h1b, h1, bxo, sa.h.done(i), ca.h.before(i), h1b_ready)
                if exists(i + 2):
                    norm_y(i + 2)
                if exists(i - 2):
                    power(n_end.var_eps.done(i - 2), n_end.rstd, tiny_y[:, 0, :], tiny_y[:, 1, :])

            norm_y(0)
            program(pool, body)

        @block.scalar
        def _(act):
            n = load_setup(act, 1)
            act.wait_ge(loaded.sem, 16 * n)
            act.wait_ge(enc_ps.sem, 1)
            act.activation(encT[:], ps[:, 0, 0:T], ACT.Identity).then_inc(enc_sb.sem, 1)
            act.wait_ge(enc_ps.sem, 2)
            act.activation(kxf[:], ps[:, 1, 0:T], ACT.Identity, bias=cols[:, BXK:BXK + 1]).then_inc(enc_sb.sem, 1)
            act.activation(kx_parts[:, 0, :], ps[:, 1, 0:T], ACT.Identity, bias=cols[:, BXK:BXK + 1]).then_inc(enc_sb.sem, 1)

            def copy_out(bank, dst, ready, before, sig, bias=0.0, scale=1.0):
                act.wait_ge(*before)
                act.wait_ge(*ready)
                act.activation(dst, bank, ACT.Identity, bias=bias, scale=scale).then_inc(sig.sem, 1)

            def high_part(bank, f, parts, bias, scale, ready, res, dma, f_sig, hi_sig, j):
                act.wait_ge(*res.before(j))
                act.wait_ge(*dma.before(j))
                act.wait_ge(*ready.done(j))
                act.activation(f[:], ps[:, bank, :], ACT.Identity, bias=bias, scale=scale).then_inc(f_sig.sem, 1)
                act.activation(parts[:, 0, :], ps[:, bank, :], ACT.Identity, bias=bias, scale=scale).then_inc(hi_sig.sem, 1)

            def values(j):
                act.wait_ge(*sa.pv.before(j))
                act.wait_ge(*sa.v_ps.done(j))
                for half in range(2):
                    src = ps[:, 6, :].rearrange("p (g a j d) -> p g a j d", a=2, j=4, d=HD)[:, :, half]
                    dst = v_st[:].rearrange("p t (s a j) c -> p (t s) a j c", s=2, a=2)[:, :, half, :,
                                                                                       16 * half:16 * half + HD]
                    act.activation(dst, src, ACT.Identity).then_inc(sa.v_sb.sem, 1)

            def exps(a, j, used_before):
                for g in range(H):
                    four, pair = divmod(g, 2)
                    act.wait_ge(*(a.pv.part(j, four - 1) if four >= 2 else used_before))
                    act.wait_ge(*a.st_ps.part(j, g + 1))
                    act.activation(probs[:, four % 2, 2 * pair:2 * pair + 2, 0:T + a.seen],
                                   ps[:, 2 * (g % 2):2 * (g % 2) + 2, 0:T + a.seen], ACT.Exp).then_inc(a.exp.sem, 1)
                    if g == 11:
                        context_copy(a, 0, j)

            def context_copy(a, s, j):
                other = sa.cT_ps.done(j) if a is ca else ca.cT_ps.before(j - 1)
                act.wait_ge(*other)
                act.wait_ge(*a.pv.part(j, 4 * s + 4))
                act.activation(ctx_fm[:, s, :], ps[:, 4 + s, :], ACT.Identity).then_inc(a.ctx_sb.sem, 1)

            def experts(j, first, last):
                for n in range(first, last):
                    e = n - 1 if n else NE
                    act.wait_ge(*(h_sb.part(j, n) if n else h_sb.before(j)))
                    act.wait_ge(*a_ps.part(j, n + 1))
                    act.activation(silu_a[:], ps[:, 0, :], ACT.Silu, bias=b1[:, e, 0:1]).then_inc(silu.sem, 1)

            def gelus(j, first, last):
                act.wait_ge(*mlp_ps.before(j))
                for c in range(first, last):
                    act.wait_ge(*fc_ps.part(j, c + 1))
                    act.activation(geluT[:, c, :], ps[:, FC_BANKS[c], :], ACT.Gelu_apprx_tanh,
                                   bias=bfc[:, c:c + 1]).then_inc(gelu.sem, 1)

            def body(i):
                if exists(i):
                    exps(sa, i, ca.pv.before(i - 1) if exists(i - 2) else sa.pv.before(i))
                if exists(i):
                    context_copy(sa, 1, i)
                if exists(i - 2):
                    copy_out(ps[:, 0, :], x3T[:], x3T_ps.done(i - 2), fc_ps.before(i - 2), x3T_sb,
                             cols[:, B2:B2 + 1], cols[:, G2:G2 + 1])
                if exists(i + 1):
                    copy_out(ps[:, 1, :], xT[:], sa.xT_ps.done(i + 1), ca.q_ps.before(i), sa.xT_sb,
                             cols[:, B1:B1 + 1], cols[:, G1:G1 + 1])
                if exists(i - 1):
                    copy_out(ps[0:3 * H, 4, :].bitcast(BF16)[:, 0:NT], maxT[:], ca.mT_ps.done(i - 1),
                             sa.m_dma.before(i + 1), ca.mT_sb)
                if exists(i - 2):
                    gelus(i - 2, 0, 1)
                if exists(i + 1):
                    high_part(0, qf, q_parts, cols[:, BQS:BQS + 1], SCALE, sa.q_ps, sa.qr, sa.q_dma, sa.qf, sa.qhi, i + 1)
                if exists(i - 2):
                    gelus(i - 2, 1, 2)
                if exists(i + 1):
                    high_part(1, kf, k_parts, cols[:, BK:BK + 1], 1.0, sa.k_ps, sa.kr, sa.k_dma, sa.kf, sa.khi, i + 1)
                if exists(i - 2):
                    gelus(i - 2, 2, NC)
                if exists(i):
                    copy_out(ps[:, 2, :], ctxT[:], sa.nT_ps.done(i), ca.o_ps.before(i - 1), sa.nT_sb, cols[:, BV:BV + 1])
                if exists(i + 1):
                    values(i + 1)
                if exists(i - 1):
                    exps(ca, i - 1, sa.pv.before(i + 1) if exists(i) else ca.pv.before(i - 1))
                if exists(i - 1):
                    context_copy(ca, 1, i - 1)
                if exists(i - 2):
                    copy_out(ps[:, 0, :], zT[:], zT_ps.done(i - 2), b_ps.before(i - 2), zT_sb)
                if exists(i):
                    copy_out(ps[:, 2, :], xT[:], ca.xT_ps.done(i), sa.v_ps.before(i + 1), ca.xT_sb,
                             cols[:, BX:BX + 1], cols[:, GX:GX + 1])
                if exists(i + 1):
                    copy_out(ps[0:3 * H, 6, :].bitcast(BF16)[:, 0:NT], maxT[:], sa.mT_ps.done(i + 1),
                             ca.m_dma.before(i), sa.mT_sb)
                if exists(i):
                    high_part(3, xqf, xq_parts, cols[:, BXQS:BXQS + 1], SCALE, ca.q_ps, ca.qr, ca.q_dma, ca.qf, ca.qhi, i)
                if exists(i - 2):
                    act.wait_ge(*route.part(i - 2, 3))
                    act.activation(prob[:], logit[:], ACT.Exp).then_inc(gate_exp.sem, 1)
                    experts(i - 2, 0, 1)
                    copy_out(ps[0:NE + 1, 7, :], gatesT[:], gatesT_ps.done(i - 2), e_ps.before(i - 2), gatesT_sb)
                    experts(i - 2, 1, 3)
                if exists(i - 1):
                    copy_out(ps[:, 6, :], ctxT[:], ca.nT_ps.done(i - 1), sa.o_ps.before(i), ca.nT_sb, cols[:, BXV:BXV + 1])
                if exists(i - 2):
                    experts(i - 2, 3, NE + 1)

            act.wait_ge(made.sem, SETUP_MADE)
            program(act, body)

        @block.vector
        def _(dve):
            for op in (q_op, xq_op, k_op, xk_op):
                dve.memset(op[32:64].bitcast(mybir.dt.uint32), 0).then_inc(padded.sem, 1)
                dve.memset(op[64:128].bitcast(mybir.dt.uint32), 0).then_inc(padded.sem, 1)
            dve.wait_ge(padded.sem, 8)
            dve.memset(xq_op[ROW_BIAS:ROW_BIAS + 3], 1.0).then_inc(padded.sem, 1)
            dve.memset(k_op[ROW_MAX:ROW_MAX + 3], -1.0).then_inc(padded.sem, 1)
            dve.memset(xk_op[ROW_MAX:ROW_MAX + 3], -1.0).then_inc(padded.sem, 1)
            for tile in (v_st, xv_st, max_parts):
                dve.memset(tile[:], 0.0).then_inc(padded.sem, 1)
            dve.wait_ge(padded.sem, PADS)
            steps = [0]

            def make(ins):
                steps[0] += 1
                ins.then_inc(made.sem, 1)
                dve.wait_ge(made.sem, steps[0])

            for tile in (v_st, xv_st):
                for half in range(2):
                    make(dve.memset(tile[:].rearrange("p t (s a j) c -> p (t s) a j c", s=2, a=2)
                                    [:, :, half, :, 16 * half + HD], 1.0))
            dve.wait_ge(loaded.sem, 16 * LOADS[0])
            for dst, src in ((wq, wqkv[:, 0:D]), (wk, wqkv[:, D:2 * D]), (wxq, wxq0[:]), (wxk, wxkv[:, 0:D])):
                make(dve.tensor_copy(dst[:].rearrange("p (d h) -> p d h", d=HD), src.rearrange("p (h d) -> p d h", d=HD)))
            make(dve.tensor_scalar(cols[:, BQS:BQS + 1], cols[:, BQ:BQ + 1], SCALE, None, ALU.mult))
            make(dve.tensor_scalar(cols[:, BXQS:BXQS + 1], cols[:, BXQ:BXQ + 1], SCALE, None, ALU.mult))
            make(dve.tensor_copy(bias_parts[:, 0, :], key_bias[:]))
            make(dve.tensor_tensor(key_res[:], key_bias[:], bias_parts[:, 0, :], ALU.subtract))
            make(dve.tensor_copy(bias_parts[:, 1, :], key_res[:]))
            make(dve.tensor_tensor(bias_parts[:, 2, :], key_res[:], bias_parts[:, 1, :], ALU.subtract))
            dve.wait_ge(enc_sb.sem, 3)
            make(dve.tensor_tensor(kxr[:], kxf[:], kx_parts[:, 0, :], ALU.subtract))
            make(dve.tensor_copy(kx_parts[:, 1, :], kxr[:]))
            make(dve.tensor_tensor(kx_parts[:, 2, :], kxr[:], kx_parts[:, 1, :], ALU.subtract))
            dve.wait_ge(enc_ps.sem, 3)
            for half in range(2):
                src = ps[:, 2, 0:T].rearrange("p (g a j d) -> p g a j d", a=2, j=4, d=HD)[:, :, half]
                dst = xv_st[:].rearrange("p t (s a j) c -> p (t s) a j c", s=2, a=2)[:, :, half, :,
                                                                                    16 * half:16 * half + HD]
                make(dve.tensor_copy(dst, src))
            assert steps[0] == SETUP_MADE

            def statistics(src, st, mv, s_stats, s_aggr, j):
                for t in range(NB):
                    dve.bn_stats(st[:, t, :], src[:, t, :]).then_inc(s_stats.sem, 1)
                dve.wait_ge(*s_stats.done(j))
                dve.memset(wait_slot[:], 0.0)
                for t in range(NB):
                    dve.bn_aggr(mv[:, t, :], st[:, t, :]).then_inc(s_aggr.sem, 1)
                dve.wait_ge(*s_aggr.done(j))

            def normalised(dst, src, mv, r, sig, j):
                for t in range(NB):
                    dve.tensor_scalar(dst[:, t, :], src[:, t, :], mv[:, t, 0:1], r[:, t:t + 1],
                                      ALU.subtract, ALU.mult).then_inc(sig.sem, 1)

            def residual_parts(f, r, parts, f_sig, hi_sig, r_sig, mid_sig, before, j):
                dve.wait_ge(*f_sig.done(j))
                dve.wait_ge(*hi_sig.done(j))
                dve.wait_ge(*before)
                dve.tensor_tensor(r[:], f[:], parts[:, 0, :], ALU.subtract).then_inc(r_sig.sem, 1)
                dve.wait_ge(*r_sig.done(j))
                dve.tensor_copy(parts[:, 1, :], r[:]).then_inc(mid_sig.sem, 1)

            def norm_y(j):
                dve.wait_ge(*x_in.done(j))
                statistics(x_tm, stx, mvx, sa.stats, sa.aggr, j)
                dve.tensor_scalar(tiny[:, 0, :], mvx[:, :, 1], EPS, None, ALU.add).then_inc(var_y.sem, 1)
                dve.wait_ge(*rstd_y.done(j))
                dve.tensor_tensor(tiny[:, 2, :], tiny[:, 1, :], tiny[:, 1, :], ALU.mult).then_inc(var_y.sem, 1)
                dve.wait_ge(*var_y.part(j, 2))
                dve.tensor_tensor(tiny[:, 7, :], tiny[:, 2, :], mvx[:, :, 1], ALU.mult).then_inc(sa.var_eps.sem, 1)
                dve.wait_ge(*sa.var_eps.done(j))
                dve.tensor_scalar(tiny[:, 3, :], tiny[:, 7, :], EPS, None, ALU.add).then_inc(var_y.sem, 1)
                dve.wait_ge(*yb_ready.before(j))
                normalised(y_tm, x_tm, mvx, tiny[:, 1, :], y_ready, j)
                dve.wait_ge(*rstd_01.done(j))
                dve.tensor_tensor(tiny[:, 5, :], tiny[:, 1, :], tiny[:, 4, :], ALU.mult).then_inc(sa.rstd.sem, 1)
                dve.wait_ge(*sa.xT_ps.before(j))
                dve.wait_ge(*sa.rstd.done(j))
                normalised(x1_tm, x_tm, mvx, tiny[:, 5, :], sa.x_ready, j)

            def maxima(a, j):
                for n in range(2 * H):
                    b, h = divmod(n, H)
                    bank = ps[:, 6 + n % 2, :]
                    dve.wait_ge(*a.s_ps.part(j, n + 1))
                    dve.tensor_reduce(rowmax[:, b, 1, h:h + 1], bank[:, 0:T], AX.X, ALU.max).then_inc(a.s_max.sem, 1)
                    dve.tensor_reduce(rowmax[:, b, 0, h:h + 1], bank[:, T:T + a.seen], AX.X,
                                      ALU.max).then_inc(a.s_max.sem, 1)

            def maxima_parts(a, j):
                mx = rowmax[:].rearrange("p b q h -> p (b q) h")
                dve.wait_ge(*a.s_max.done(j))
                dve.tensor_copy(max_parts[:, :, 0, :], mx).then_inc(a.m1.sem, 1)
                dve.wait_ge(*a.m1.done(j))
                dve.tensor_tensor(max_res[:], mx, max_parts[:, :, 0, :], ALU.subtract).then_inc(a.mr.sem, 1)
                dve.wait_ge(*a.mr.done(j))
                dve.tensor_copy(max_parts[:, :, 1, :], max_res[:]).then_inc(a.m2.sem, 1)
                dve.wait_ge(*a.m2.done(j))
                dve.tensor_tensor(max_parts[:, :, 2, :], max_res[:], max_parts[:, :, 1, :],
                                  ALU.subtract).then_inc(a.m3.sem, 1)

            def normalise_context(a, j):
                for n in range(2):
                    blocks = ps[:, 2 + n, :].rearrange("p (g c) -> p g c", c=16)
                    dve.wait_ge(*a.cT_ps.part(j, n + 1))
                    r = rden[:, 2 * n:2 * n + 2, :].rearrange("p t h -> p (t h)")
                    dve.reciprocal(r, blocks[:, :, HD]).then_inc(a.rden.sem, 1)
                    dve.wait_ge(*a.rden.part(j, n + 1))
                    dve.tensor_tensor(ctx_tm[:, 2 * n:2 * n + 2, :].rearrange("p t (g d) -> p (t g) d", d=HD),
                                      blocks[:, :, 0:HD],
                                      r.rearrange("p (g o) -> p g o", o=1).to_broadcast([128, 32, HD]),
                                      ALU.mult).then_inc(a.ctx_n.sem, 1)

            def add_residual(bank, dst, base, ready, base_ready, sig):
                dve.wait_ge(*base_ready)
                dve.wait_ge(*ready)
                dve.tensor_tensor(dst[:].rearrange("p t f -> p (t f)"), ps[:, bank, :],
                                  base[:].rearrange("p t f -> p (t f)"), ALU.add).then_inc(sig.sem, 1)

            def norm_stats(n, src, ready, st, mv, var_eps, j):
                dve.wait_ge(*ready)
                statistics(src, st, mv, n.stats, n.aggr, j)
                dve.tensor_scalar(var_eps, mv[:, :, 1], EPS, None, ALU.add).then_inc(n.var_eps.sem, 1)

            def normalise(n, dst, src, mv, r, sig, j):
                dve.wait_ge(*n.rstd.done(j))
                normalised(dst, src, mv, r, sig, j)

            def over_e(x):
                return x.rearrange("p (t o) -> p t o", o=1).to_broadcast([128, NB, NE])

            def router_logits(j):
                dve.wait_ge(*gate_ps.done(j))
                dve.tensor_tensor(logit[:], ps[:, 1, 0:NB * NE].rearrange("p (t e) -> p t e", e=NE),
                                  bgate[:].rearrange("p (o e) -> p o e", o=1).to_broadcast([128, NB, NE]),
                                  ALU.add).then_inc(route.sem, 1)
                dve.wait_ge(*route.part(j, 1))
                dve.tensor_reduce(rt[:, 0, :], logit[:], AX.X, ALU.max).then_inc(route.sem, 1)
                dve.wait_ge(*route.part(j, 2))
                dve.tensor_tensor(logit[:], logit[:], over_e(rt[:, 0, :]), ALU.subtract).then_inc(route.sem, 1)

            def router_gates(j):
                dve.wait_ge(*gate_exp.done(j))
                dve.tensor_reduce(rt[:, 1, :], prob[:], AX.X, ALU.add).then_inc(route.sem, 1)
                dve.wait_ge(*route.part(j, 4))
                dve.reciprocal(rt[:, 2, :], rt[:, 1, :]).then_inc(route.sem, 1)
                dve.wait_ge(*route.part(j, 5))
                dve.tensor_tensor(logit[:], prob[:], over_e(rt[:, 2, :]), ALU.mult).then_inc(route.sem, 1)
                dve.wait_ge(*route.part(j, 6))
                for t in range(NB):
                    other = logit[:, t, :].rearrange("p (o e) -> p o e", o=1).to_broadcast([128, NE, NE])
                    own = logit[:, t, :].rearrange("p (e o) -> p e o", o=1).to_broadcast([128, NE, NE])
                    pairs = more[:, t, :].rearrange("p (e f) -> p e f", f=NE)
                    ties = same[:, t, :].rearrange("p (e f) -> p e f", f=NE)
                    dve.tensor_tensor(pairs, other, own, ALU.is_gt).then_inc(n_rank.sem, 1)
                    dve.tensor_tensor(ties, other, own, ALU.is_equal).then_inc(n_rank.sem, 1)
                dve.wait_ge(*n_rank.part(j, 2 * NB))
                dve.tensor_tensor(same[:], same[:], lower[:].rearrange("p (o e) f -> p o (e f)", o=1)
                                  .to_broadcast([128, NB, NE * NE]), ALU.mult).then_inc(n_rank.sem, 1)
                dve.wait_ge(*n_rank.part(j, 2 * NB + 1))
                dve.tensor_tensor(more[:], more[:], same[:], ALU.add).then_inc(n_rank.sem, 1)
                dve.wait_ge(*n_rank.part(j, 2 * NB + 2))
                dve.tensor_reduce(rank[:], more[:].rearrange("p t (e f) -> p (t e) f", f=NE), AX.X,
                                  ALU.add).then_inc(n_rank.sem, 1)
                dve.wait_ge(*n_rank.done(j))
                dve.scalar_tensor_tensor(out=gates[:, :, 0:NE], in0=rank[:], scalar=1.5, in1=logit[:],
                                         op0=ALU.is_lt, op1=ALU.mult).then_inc(route.sem, 3)

            def products(j, n):
                e = n - 1 if n else NE
                dve.wait_ge(*(e_ps.part(j, n - 1) if n >= 2 else e_ps.before(j)))
                dve.wait_ge(*silu.part(j, n + 1))
                dve.wait_ge(*b_ps.part(j, n + 1))
                dve.scalar_tensor_tensor(out=hT[:, n % 2, :], in0=ps[:, 1, :], scalar=b1[:, e, 1:2],
                                         in1=silu_a[:], op0=ALU.add, op1=ALU.mult).then_inc(h_sb.sem, 1)

            def gather(j, n):
                dve.wait_ge(*e_ps.part(j, n + 1))
                if n == 0:
                    dve.tensor_copy(acc[:].rearrange("p t f -> p (t f)"), ps[:, 4, :]).then_inc(acc_sb.sem, 1)
                else:
                    for t in range(NB):
                        dve.wait_ge(*acc_sb.part(j, 1 if n == 1 else 1 + NB * (n - 2) + t + 1))
                        dve.scalar_tensor_tensor(out=acc[:, t, :], in0=ps[:, 4 + n % 2, t * D:(t + 1) * D],
                                                 scalar=gates[:, t, n - 1:n], in1=acc[:, t, :],
                                                 op0=ALU.mult, op1=ALU.add).then_inc(acc_sb.sem, 1)

            def finish(j):
                norm_stats(n_end, acc, acc_sb.done(j), sty, mvy, tiny_y[:, 0, :], j)
                normalise(n_end, acc, acc, mvy, tiny_y[:, 1, :], n_end.out, j)
                dve.wait_ge(*o_dma.before(j))
                dve.wait_ge(*n_end.out.done(j))
                for t in range(NB):
                    dve.tensor_tensor(o_tm[:, t, :], acc[:, t, :], xn[:, t, :], ALU.add).then_inc(o_ready.sem, 1)

            def body(i):
                k = i - 2
                if exists(i - 1):
                    maxima(ca, i - 1)
                if exists(i - 1):
                    maxima_parts(ca, i - 1)
                if exists(k):
                    dve.wait_ge(*n_mlp.out.done(k))
                    dve.tensor_tensor(h2[:], h2[:], bmlp[:].rearrange("p (o f) -> p o f", o=1)
                                      .to_broadcast([128, NB, D]), ALU.add).then_inc(h2b_ready.sem, 1)
                if exists(i):
                    normalise_context(sa, i)
                if exists(i + 1):
                    residual_parts(qf, qr, q_parts, sa.qf, sa.qhi, sa.qr, sa.qmid, sa.qlo.before(i + 1), i + 1)
                    residual_parts(kf, kr, k_parts, sa.kf, sa.khi, sa.kr, sa.kmid, sa.klo.before(i + 1), i + 1)
                if exists(k):
                    add_residual(7, h3, h2, mlp_ps.done(k), h2b_ready.done(k), h3_sb)
                    norm_stats(n_post, h3, h3_sb.done(k), sty, mvy, tiny_y[:, 0, :], k)
                if exists(i):
                    add_residual(3, h1, yb_tm, sa.o_ps.done(i), yb_ready.done(i), sa.h)
                    norm_stats(ca, h1, sa.h.done(i), st2, mv2, tiny2[:, 0, :], i)
                if exists(k):
                    normalise(n_post, h3, h3, mvy, tiny_y[:, 1, :], n_post.out, k)
                    dve.wait_ge(*x_kept.done(k))
                    dve.wait_ge(*n_post.out.done(k))
                    dve.tensor_tensor(xn[:], h3[:], x_keep[:], ALU.add).then_inc(xn_ready.sem, 1)
                    norm_stats(n_z, xn, xn_ready.done(k), sty, mvy, tiny_y[:, 0, :], k)
                if exists(i):
                    normalise(ca, x2_tm, h1, mv2, tiny2[:, 1, :], ca.x_ready, i)
                if exists(k):
                    normalise(n_z, z_tm, xn, mvy, tiny_y[:, 1, :], n_z.out, k)
                if exists(i + 1):
                    maxima(sa, i + 1)
                if exists(i + 1):
                    maxima_parts(sa, i + 1)
                if exists(k):
                    router_logits(k)
                if exists(i):
                    residual_parts(xqf, xqr, xq_parts, ca.qf, ca.qhi, ca.qr, ca.qmid, ca.qlo.before(i), i)
                if exists(k):
                    router_gates(k)
                    products(k, 0)
                if exists(i - 1):
                    normalise_context(ca, i - 1)
                if exists(k):
                    for n in range(1, 5):
                        products(k, n)
                        gather(k, n - 1)
                if exists(i - 1):
                    add_residual(7, h2, h1b, ca.o_ps.done(i - 1), h1b_ready.done(i - 1), ca.h)
                    norm_stats(n_mlp, h2, ca.h.done(i - 1), st3, mv3, tiny3[:, 0, :], i - 1)
                if exists(k):
                    for n in range(5, 7):
                        products(k, n)
                        gather(k, n - 1)
                if exists(i - 1):
                    normalise(n_mlp, x3_tm, h2, mv3, tiny3[:, 1, :], n_mlp.out, i - 1)
                if exists(i + 2):
                    norm_y(i + 2)
                if exists(k):
                    for n in range(7, NE + 1):
                        products(k, n)
                        gather(k, n - 1)
                    gather(k, NE)
                    finish(k)

            norm_y(0)
            program(dve, body)

        @block.tensor
        def _(pe):
            pe.wait_ge(shaped.sem, 9)
            pe.wait_ge(loaded.sem, 16 * LOADS[0])
            for k in range(2):
                last = pe.transpose(ps[:, 0, k * 128:(k + 1) * 128], enc_tm[:, k, :], identf[:])
            last.then_inc(enc_ps.sem, 1)
            pe.wait_ge(made.sem, 8)
            pe.wait_ge(enc_sb.sem, 1)
            pe.matmul(ps[:, 1, 0:T], wxk[:], encT[:], start=True, stop=True).then_inc(enc_ps.sem, 1)
            for k in range(2):
                last = pe.matmul(ps[:, 2, k * D:(k + 1) * D], encT[:, k * 128:(k + 1) * 128], wxkv[:, D:2 * D],
                                 start=True, stop=True)
            last.then_inc(enc_ps.sem, 1)
            pe.wait_ge(made.sem, SETUP_MADE)
            pe.wait_ge(xk_dma.sem, 16 * 9)

            def transposes(bank, src, sig):
                for t in range(NB):
                    last = pe.transpose(bank[:, t * 128:(t + 1) * 128], src[:, t, :], identf[:])
                last.then_inc(sig.sem, 1)

            def scores(a, n, j):
                b, h = divmod(n, H)
                if n >= 2:
                    pe.wait_ge(*a.s_max.part(j, 2 * (n - 1)))
                bank = ps[:, 6 + n % 2, :]
                q0 = b * T
                k0 = 0 if a.cross else b * T
                pe.matmul(bank[:, 0:T], a.qop[0:ROWS_S, h, q0 + 128:q0 + 256], a.kop[0:ROWS_S, h, k0:k0 + T],
                          start=True, stop=False, skip_group_check=True)
                pe.matmul(bank[:, T:T + a.seen], a.qop[0:ROWS_S, h, q0:q0 + 128],
                          a.kop[0:ROWS_S, h, k0:k0 + a.seen], start=False, stop=False, skip_group_check=True)
                mask = a.mq[:] if a.cross else a.mq[:].rearrange("p a b -> p (a b)")
                pe.matmul(bank[:, 128:T + a.seen], identb[:], mask, start=False, stop=True,
                          skip_group_check=True).then_inc(a.s_ps.sem, 1)

            def max_rows(a, bank, j):
                pe.wait_ge(*a.m3.done(j))
                for t in range(NB):
                    last = pe.transpose(ps[:, bank, :].bitcast(BF16)[:, t * 128:(t + 1) * 128],
                                        max_parts[:, t].rearrange("p a h -> p (a h)"), identb[:])
                last.then_inc(a.mT_ps.sem, 1)

            def score_group(a, g, j):
                s, b, aa, jj = g // 8, g // 4 % 2, g // 2 % 2, g % 2
                if g >= 2:
                    pe.wait_ge(*a.exp.part(j, g - 1))
                q0 = b * T
                k0 = 0 if a.cross else b * T
                late = T - a.seen
                for n in range(2):
                    h = 8 * s + 4 * aa + 2 * jj + n
                    bank = ps[:, 2 * (g % 2) + n, :]
                    pe.matmul(bank[:, 0:T], a.kop[0:ROWS_ST, h, k0:k0 + 128], a.qop[0:ROWS_ST, h, q0:q0 + T],
                              start=True, stop=False, skip_group_check=True)
                    pe.matmul(bank[:, T:T + a.seen], a.kop[0:ROWS_ST, h, k0 + 128:k0 + T],
                              a.qop[0:ROWS_ST, h, q0 + late:q0 + T], start=False, stop=False, skip_group_check=True)
                    if a.cross:
                        pe.matmul(bank[:, 0:128], identb[:], a.mk[:, 0:128], start=False, stop=False, skip_group_check=True)
                        last = pe.matmul(bank[:, T:T + XW], identb[:], a.mk[:, 128:128 + XW], start=False, stop=True,
                                         skip_group_check=True)
                    else:
                        pe.matmul(bank[:, 0:128], identb[:], a.mk[:, 0, :], start=False, stop=False, skip_group_check=True)
                        last = pe.matmul(bank[:, T:T + 128], identb[:], a.mk[:, 1, :], start=False, stop=True,
                                         skip_group_check=True)
                last.then_inc(a.st_ps.sem, 1)

            def value_group(a, four, j):
                s, b, aa = four // 4, four // 2 % 2, four % 2
                pe.wait_ge(*a.exp.part(j, 2 * four + 2))
                late = T - a.seen
                bank = ps[:, 4 + s, :]
                for half in range(2):
                    for jj in range(4):
                        h = 8 * s + 4 * aa + jj
                        v = a.v[:, half if a.cross else 2 * b + half, h, :]
                        q0 = b * T + (late if half else 0)
                        last = pe.matmul(bank[32 * jj:32 * jj + 32, q0:(b + 1) * T], v,
                                         probs[:, four % 2, jj, (T if half else 0):(T + a.seen if half else T)],
                                         start=(aa == 0 and half == 0), stop=(aa == 1 and half == 1),
                                         skip_group_check=True)
                last.then_inc(a.pv.sem, 1)

            def attention_phase(a, j, other, jo):
                if exists(j):
                    pe.wait_ge(*a.m_dma.done(j))
                    if not a.cross:
                        pe.wait_ge(*a.v_sb.done(j))
                for four in range(8):
                    if exists(j):
                        score_group(a, 2 * four, j)
                        score_group(a, 2 * four + 1, j)
                    if exists(jo):
                        if four == 0:
                            pe.wait_ge(*other.q_dma.done(jo))
                            if not other.cross:
                                pe.wait_ge(*other.k_dma.done(jo))
                        for n in range(4 * four, 4 * four + 4):
                            scores(other, n, jo)
                    if exists(j) and four:
                        value_group(a, four - 1, j)
                if exists(j):
                    value_group(a, 7, j)

            def context_T(a, j):
                pe.wait_ge(*a.ctx_sb.done(j))
                for n in range(2):
                    for t in (2 * n, 2 * n + 1):
                        for s in range(2):
                            at = (t % 2) * 256 + s * 128
                            last = pe.transpose(ps[:, 2 + n, at:at + 128], ctx_fm[:, s, t * 128:(t + 1) * 128], identf[:])
                    last.then_inc(a.cT_ps.sem, 1)

            def by_token(bank, src, w, sig):
                for t in range(NB):
                    last = pe.matmul(ps[:, bank, t * D:(t + 1) * D], src[:, t * 128:(t + 1) * 128], w, start=True, stop=True)
                last.then_inc(sig.sem, 1)

            def by_feature(bank, w, src, sig):
                pe.matmul(ps[:, bank, :], w, src[:], start=True, stop=True).then_inc(sig.sem, 1)

            def fc(j, c):
                by_feature(FC_BANKS[c], wfc[:, c * 128:(c + 1) * 128], x3T, fc_ps)

            def up_a(j, n):
                e = n - 1 if n else NE
                if n:
                    pe.wait_ge(*silu.part(j, n))
                by_feature(0, w1[:, e, 0:128], zT, a_ps)

            def up_b(j, n):
                e = n - 1 if n else NE
                if n:
                    pe.wait_ge(*h_sb.part(j, n))
                by_feature(1, w1[:, e, 128:256], zT, b_ps)

            def down(j, n):
                e = n - 1 if n else NE
                if n >= 2:
                    pe.wait_ge(*acc_sb.part(j, 1 + NB * (n - 2)))
                pe.wait_ge(*h_sb.part(j, n + 1))
                for t in range(NB):
                    to = ps[:, 4 + n % 2, t * D:(t + 1) * D]
                    last = pe.matmul(to, hT[:, n % 2, t * 128:(t + 1) * 128], w2[:, e, :], start=True, stop=(n > 0))
                    if n == 0:
                        last = pe.matmul(to, gatesT[:, t * 128:(t + 1) * 128], b2[:], start=False, stop=True)
                last.then_inc(e_ps.sem, 1)

            def experts(j, first, last):
                for n in range(first, last):
                    up_a(j, n)
                    up_b(j, n)
                    down(j, n - 1)

            def body(i):
                k = i - 2
                if exists(k - 1):
                    pe.wait_ge(*acc_sb.before(k))
                if exists(i - 2):
                    pe.wait_ge(*ca.h.before(i - 1))
                if exists(i - 1):
                    pe.wait_ge(*ca.qhi.done(i - 1))
                attention_phase(sa, i, ca, i - 1)
                if exists(i):
                    pe.wait_ge(*sa.exp.done(i))
                if exists(k):
                    pe.wait_ge(*n_mlp.out.done(k))
                    transposes(ps[:, 0, :], x3_tm, x3T_ps)
                if exists(i + 1):
                    pe.wait_ge(*sa.x_ready.done(i + 1))
                    transposes(ps[:, 1, :], x1_tm, sa.xT_ps)
                if exists(i):
                    context_T(sa, i)
                if exists(i - 1):
                    max_rows(ca, 4, i - 1)
                if exists(k):
                    pe.wait_ge(*ca.s_max.done(i - 1) if exists(i - 1) else x3T_sb.done(k))
                    pe.wait_ge(*x3T_sb.done(k))
                    fc(k, 0)
                    fc(k, 1)
                if exists(i + 1):
                    pe.wait_ge(*sa.xT_sb.done(i + 1))
                    by_feature(0, wq[:], xT, sa.q_ps)
                if exists(k):
                    fc(k, 2)
                if exists(i + 1):
                    by_feature(1, wk[:], xT, sa.k_ps)
                if exists(i - 1):
                    pe.wait_ge(*ca.mT_sb.done(i - 1))
                if exists(k):
                    fc(k, 3)
                if exists(i):
                    pe.wait_ge(*sa.ctx_n.done(i))
                    transposes(ps[:, 2, :], ctx_tm, sa.nT_ps)
                if exists(k):
                    pe.wait_ge(*gelu.done(k))
                if exists(i + 1):
                    if exists(i - 1):
                        pe.wait_ge(*ca.s_max.done(i - 1))
                    by_token(6, xT, wqkv[:, 2 * D:3 * D], sa.v_ps)
                if exists(k):
                    for t in range(NB):
                        for c in range(NC):
                            last = pe.matmul(ps[:, 7, t * D:(t + 1) * D], geluT[:, c, t * 128:(t + 1) * 128], wmlp[:, c, :],
                                             start=(c == 0), stop=(c == NC - 1))
                    last.then_inc(mlp_ps.sem, 1)
                if exists(i):
                    pe.wait_ge(*sa.nT_sb.done(i))
                    by_token(3, ctxT, wo[:], sa.o_ps)
                if exists(i + 1):
                    pe.wait_ge(*sa.qhi.done(i + 1))
                    pe.wait_ge(*sa.khi.done(i + 1))
                    pe.wait_ge(*sa.v_sb.done(i + 1))
                if exists(i):
                    pe.wait_ge(*sa.h.done(i))
                if exists(k):
                    pe.wait_ge(*h3_sb.done(k))
                attention_phase(ca, i - 1, sa, i + 1)
                if exists(i - 1):
                    pe.wait_ge(*ca.exp.done(i - 1))
                if exists(k):
                    pe.wait_ge(*n_z.out.done(k))
                    transposes(ps[:, 0, :], z_tm, zT_ps)
                if exists(i):
                    pe.wait_ge(*ca.x_ready.done(i))
                    transposes(ps[:, 2, :], x2_tm, ca.xT_ps)
                if exists(k):
                    pe.wait_ge(*zT_sb.done(k))
                    for t in range(NB):
                        last = pe.matmul(ps[:, 1, t * NE:(t + 1) * NE], zT[:, t * 128:(t + 1) * 128], wgate[:],
                                         start=True, stop=True)
                    last.then_inc(gate_ps.sem, 1)
                if exists(i + 1):
                    max_rows(sa, 6, i + 1)
                if exists(i):
                    pe.wait_ge(*ca.xT_sb.done(i))
                    by_feature(3, wxq[:], xT, ca.q_ps)
                if exists(k):
                    up_a(k, 0)
                    pe.wait_ge(*route.part(k, 1))
                    up_b(k, 0)
                if exists(i - 1):
                    if exists(i):
                        pe.wait_ge(*ca.qhi.done(i))
                    context_T(ca, i - 1)
                if exists(k):
                    up_a(k, 1)
                    pe.wait_ge(*route.done(k))
                    if exists(i + 1):
                        pe.wait_ge(*sa.s_max.done(i + 1))
                    for t in range(NB):
                        last = pe.transpose(ps[0:NE + 1, 7, t * 128:(t + 1) * 128], gates[:, t, :], identf[:])
                    last.then_inc(gatesT_ps.sem, 1)
                    up_b(k, 1)
                    pe.wait_ge(*gatesT_sb.done(k))
                    down(k, 0)
                    experts(k, 2, 3)
                if exists(i - 1):
                    pe.wait_ge(*ca.ctx_n.done(i - 1))
                    if exists(i + 1):
                        pe.wait_ge(*sa.mT_sb.done(i + 1))
                    transposes(ps[:, 6, :], ctx_tm, ca.nT_ps)
                if exists(k):
                    experts(k, 3, 4)
                if exists(i - 1):
                    pe.wait_ge(*ca.nT_sb.done(i - 1))
                    by_token(7, ctxT, wxo[:], ca.o_ps)
                if exists(k):
                    experts(k, 4, NE + 1)
                    down(k, NE)

            program(pe, body)


_INS = ['hidden_states', 'encoder_hidden_states', 'scorer_logits', 'ln1_g', 'ln1_b', 'c_attn_w', 'c_attn_b',
        'attn_proj_w', 'attn_proj_b', 'lnx_g', 'lnx_b', 'q_attn_w', 'q_attn_b', 'x_kv_w', 'x_kv_b', 'x_proj_w',
        'x_proj_b', 'ln2_g', 'ln2_b', 'fc_w', 'fc_b', 'mlp_proj_w', 'mlp_proj_b']
_FFN = ['gate_w', 'gate_b', 'sw1', 'sb1', 'sw2', 'sb2', 'rw1', 'rb1', 'rw2', 'rb2']


def kernel(**inputs):
    import numpy as _np
    import concourse.bacc as _bacc
    from concourse import mybir as _mybir
    from concourse.bass_utils import run_bass_kernel_spmd as _run

    nc = _bacc.Bacc("TRN2", target_bir_lowering=False, num_devices=1)
    names = ["L0_attn_" + n for n in _INS] + ["L0_ffn_" + n for n in _FFN]
    arrays, args = {}, []
    for name in names:
        a = _np.ascontiguousarray(inputs[name])
        arrays[f"in_{name}"] = a
        args.append(nc.dram_tensor(f"in_{name}", a.shape, _mybir.dt.from_np(a.dtype), kind="ExternalInput").ap())
    shape = arrays["in_L0_attn_hidden_states"].shape
    out = nc.dram_tensor("out_0", shape, F32, kind="ExternalOutput").ap()
    sandwich_kernel(nc, out, *args)
    r = _run(nc, [arrays], core_ids=[0])
    return r.results[0]["out_0"]
```

```python
import concourse.bass as bass
from concourse import mybir
from contextlib import ExitStack

F32 = mybir.dt.float32
BF16 = mybir.dt.bfloat16
ALU = mybir.AluOpType
ACT = mybir.ActivationFunctionType
AX = mybir.AxisListType


class Names:
    pass


class Signal:

    def __init__(self, sem, per, pairs):
        self.sem, self.per, self.pairs = sem, per, pairs

    def done(self, j):
        return self.sem, j + 1 if self.per == 1 else j * self.per + self.per

    def part(self, j, k):
        return self.sem, j * self.per + k

    def before(self, j):
        if isinstance(j, int):
            j = min(max(j, 0), self.pairs)
        return self.sem, j if self.per == 1 else j * self.per


def sandwich_kernel(nc, out, hs, enc, scorer, ln1_g, ln1_b, c_attn_w, c_attn_b, attn_proj_w, attn_proj_b,
                    lnx_g, lnx_b, q_attn_w, q_attn_b, x_kv_w, x_kv_b, x_proj_w, x_proj_b, ln2_g, ln2_b,
                    fc_w, fc_b, mlp_proj_w, mlp_proj_b, gate_w, gate_b, sw1, sb1, sw2, sb2, rw1, rb1, rw2, rb2):
    B, T, D = hs.shape
    H, HD = 16, 8
    NE = rw1.shape[0]
    NC = fc_w.shape[1] // 128
    PAIRS = B // 2
    NT = 2 * T
    NB = NT // 128
    EPS = 1e-5
    SCALE = float(HD) ** -0.5
    MASKED = -3.0e38
    QPARTS = [0, 1, 2, 0, 1, 0]
    KPARTS = [0, 0, 0, 1, 1, 2]
    ROW_BIAS, ROWS_S, ROW_MAX, ROWS_ST = 64, 96, 96, 99
    XW = 130

    ctx = ExitStack()
    with ctx:
        ctx.enter_context(nc.allow_non_contiguous_dma(reason="small vectors and permuted rows, once"))

        def sb(name, shape, dt=F32):
            return ctx.enter_context(nc.sbuf_tensor(name, shape, dt))

        def signal(name, per):
            return Signal(ctx.enter_context(nc.semaphore(name)), per, PAIRS)

        identf = sb("identf", [128, 128])
        identb = sb("identb", [128, 128], BF16)
        mask_q = sb("mask_q", [128, 2, 128], BF16)
        mask_k = sb("mask_k", [128, 2, 128], BF16)
        xmask_q = sb("xmask_q", [128, 128 + XW], BF16)
        xmask_k = sb("xmask_k", [128, 128 + XW], BF16)
        lower = sb("lower", [128, NE, NE])
        half_neg = sb("half_neg", [128, NB])
        wqkv = sb("wqkv", [128, 3 * D])
        wq = sb("wq", [128, D])
        wk = sb("wk", [128, D])
        wo = sb("wo", [128, D])
        wxq0 = sb("wxq0", [128, D])
        wxq = sb("wxq", [128, D])
        wxkv = sb("wxkv", [128, 2 * D])
        wxk = sb("wxk", [128, D])
        wxo = sb("wxo", [128, D])
        wfc = sb("wfc", [128, NC * 128])
        wmlp = sb("wmlp", [128, NC, D])
        wgate = sb("wgate", [128, NE])
        w1 = sb("w1", [128, NE + 1, 2 * 128])
        w2 = sb("w2", [128, NE + 1, D])
        b1 = sb("b1", [128, NE + 1, 2])
        b2 = sb("b2", [NE + 1, D])
        cols = sb("cols", [128, 16])
        G1, B1, GX, BX, G2, B2, BQ, BK, BV, BXQ, BXK, BXV, BQS, BXQS = range(14)
        bfc = sb("bfc", [128, NC])
        bo = sb("bo", [128, D])
        bxo = sb("bxo", [128, D])
        bmlp = sb("bmlp", [128, D])
        bgate = sb("bgate", [128, NE])
        enc_tm = sb("enc_tm", [128, 2, D])
        encT = sb("encT", [128, T])
        kxf = sb("kxf", [128, T])
        kxr = sb("kxr", [128, T])
        kx_parts = sb("kx_parts", [128, 3, T], BF16)
        key_bias = sb("key_bias", [1, T])
        key_res = sb("key_res", [1, T])
        bias_parts = sb("bias_parts", [1, 3, T], BF16)

        q_op = sb("q_op", [128, H, NT], BF16)
        k_op = sb("k_op", [128, H, NT], BF16)
        xq_op = sb("xq_op", [128, H, NT], BF16)
        xk_op = sb("xk_op", [128, H, T], BF16)
        v_st = sb("v_st", [128, NB, H, 32])
        xv_st = sb("xv_st", [128, 2, H, 32])

        x_tm = sb("x_tm", [128, NB, D])
        x_keep = sb("x_keep", [128, NB, D])
        y_tm = sb("y_tm", [128, NB, D])
        yb_tm = sb("yb_tm", [128, NB, D])
        x1_tm = sb("x1_tm", [128, NB, D])
        x2_tm = sb("x2_tm", [128, NB, D])
        xT = sb("xT", [128, NT])
        qf = sb("qf", [128, NT])
        kf = sb("kf", [128, NT])
        qr = sb("qr", [128, NT])
        kr = sb("kr", [128, NT])
        xqf = sb("xqf", [128, NT])
        xqr = sb("xqr", [128, NT])
        xq_parts = sb("xq_parts", [128, 3, NT], BF16)
        q_parts = sb("q_parts", [128, 3, NT], BF16)
        k_parts = sb("k_parts", [128, 3, NT], BF16)
        rowmax = sb("rowmax", [128, 2, 2, H])
        max_res = sb("max_res", [128, NB, H])
        max_parts = sb("max_parts", [128, NB, 8, H], BF16)
        wait_slot = sb("wait_slot", [128, 1])
        maxT = sb("maxT", [3 * H, NT], BF16)
        probs = sb("probs", [128, 2, 4, T + XW])
        ctx_fm = sb("ctx_fm", [128, 2, NT])
        rden = sb("rden", [128, NB, H])
        ctx_tm = sb("ctx_tm", [128, NB, D])
        ctxT = sb("ctxT", [128, NT])
        h1 = sb("h1", [128, NB, D])
        h1b = sb("h1b", [128, NB, D])
        stx = sb("stx", [128, NB, 6])
        mvx = sb("mvx", [128, NB, 2])
        tiny = sb("tiny", [128, 10, NB])
        st2 = sb("st2", [128, NB, 6])
        mv2 = sb("mv2", [128, NB, 2])
        tiny2 = sb("tiny2", [128, 4, NB])
        tiny3 = sb("tiny3", [128, 4, NB])
        tiny_post = sb("tiny_post", [128, 4, NB])
        tiny_z = sb("tiny_z", [128, 4, NB])
        tiny_end = sb("tiny_end", [128, 4, NB])
        st3 = sb("st3", [128, NB, 6])
        mv3 = sb("mv3", [128, NB, 2])

        h2 = sb("h2", [128, NB, D])
        h2b = sb("h2b", [128, NB, D])
        x3_tm = sb("x3_tm", [128, NB, D])
        x3T = sb("x3T", [128, NT])
        geluT = sb("geluT", [128, NC, NT])
        h3 = sb("h3", [128, NB, D])
        xn = sb("xn", [128, NB, D])
        z_tm = sb("z_tm", [128, NB, D])
        zT = sb("zT", [128, NT])
        logit = sb("logit", [128, NB, NE])
        prob = sb("prob", [128, NB, NE])
        rt = sb("rt", [128, 4, NB])
        more = sb("more", [128, NB, NE * NE])
        same = sb("same", [128, NB, NE * NE])
        rank = sb("rank", [128, NB, NE])
        gates = sb("gates", [128, NB, NE + 1])
        gatesT = sb("gatesT", [NE + 1, NT])
        silu_a = sb("silu_a", [128, NT])
        hT = sb("hT", [128, 2, NT])
        acc = sb("acc", [128, NB, D])
        o_tm = sb("o_tm", [128, NB, D])
        sty = sb("sty", [128, NB, 6])
        mvy = sb("mvy", [128, NB, 2])

        ps = ctx.enter_context(nc.psum_tensor("ps", [128, 8, 512], F32))

        loaded = signal("loaded", 0)
        filled = signal("filled", 0)
        shaped = signal("shaped", 0)
        padded = signal("padded", 0)
        made = signal("made", 0)
        enc_ps = signal("enc_ps", 0)
        enc_sb = signal("enc_sb", 0)
        xk_dma = signal("xk_dma", 0)
        x_in = signal("x_in", 16)
        x_kept = signal("x_kept", 16)
        y_ready = signal("y_ready", NB)
        yb_ready = signal("yb_ready", 1)
        var_y, y_nb = signal("var_y", 4), signal("y_nb", 1)
        rstd_y = signal("rstd_y", 1)
        rstd_01 = signal("rstd_01", 1)

        def attention(n, cross):
            a = Names()
            a.cross = cross
            a.qop, a.kop = (xq_op, xk_op) if cross else (q_op, k_op)
            a.mq, a.mk = (xmask_q, xmask_k) if cross else (mask_q, mask_k)
            a.seen = XW if cross else 128
            a.v = xv_st if cross else v_st
            a.stats, a.aggr = signal(n + "_stats", NB), signal(n + "_aggr", NB)
            a.var_eps, a.rstd, a.nb = signal(n + "_var_eps", 2), signal(n + "_rstd", 1), signal(n + "_nb", 1)
            a.x_ready = signal(n + "_x_ready", NB)
            a.xT_ps, a.xT_sb = signal(n + "_xT_ps", 1), signal(n + "_xT_sb", 1)
            a.q_ps, a.k_ps, a.v_ps = signal(n + "_q_ps", 1), signal(n + "_k_ps", 1), signal(n + "_v_ps", 1)
            a.qf, a.qhi = signal(n + "_qf", 1), signal(n + "_qhi", 1)
            a.qr, a.qmid, a.qlo = signal(n + "_qr", 1), signal(n + "_qmid", 1), signal(n + "_qlo", 1)
            a.kf, a.khi = signal(n + "_kf", 1), signal(n + "_khi", 1)
            a.kr, a.kmid, a.klo = signal(n + "_kr", 1), signal(n + "_kmid", 1), signal(n + "_klo", 1)
            a.v_sb = signal(n + "_v_sb", 2)
            a.q_dma, a.k_dma = signal(n + "_q_dma", 96), signal(n + "_k_dma", 96)
            a.s_ps, a.s_max = signal(n + "_s_ps", 2 * H), signal(n + "_s_max", 4 * H)
            a.m1, a.mr, a.m2, a.m3 = (signal(n + x, 1) for x in ("_m1", "_mr", "_m2", "_m3"))
            a.mT_ps, a.mT_sb, a.m_dma = signal(n + "_mT_ps", 1), signal(n + "_mT_sb", 1), signal(n + "_m_dma", 16)
            a.st_ps, a.exp, a.pv = signal(n + "_st_ps", H), signal(n + "_exp", H), signal(n + "_pv", 8)
            a.ctx_sb, a.cT_ps = signal(n + "_ctx_sb", 2), signal(n + "_cT_ps", 2)
            a.rden, a.ctx_n = signal(n + "_rden", 2), signal(n + "_ctx_n", 2)
            a.nT_ps, a.nT_sb = signal(n + "_nT_ps", 1), signal(n + "_nT_sb", 1)
            a.o_ps, a.h = signal(n + "_o_ps", 1), signal(n + "_h", 1)
            return a

        sa = attention("self", False)
        ca = attention("cross", True)
        h1b_ready = signal("h1b_ready", 1)
        h2b_ready = signal("h2b_ready", 1)

        def norm(n):
            a = Names()
            a.stats, a.aggr = signal(n + "_stats", NB), signal(n + "_aggr", NB)
            a.var_eps, a.rstd, a.nb = signal(n + "_var_eps", 2), signal(n + "_rstd", 1), signal(n + "_nb", 1)
            a.out = signal(n + "_out", NB)
            return a

        n_mlp, n_post, n_z, n_end = norm("n_mlp"), norm("n_post"), norm("n_z"), norm("n_end")
        x3T_ps, x3T_sb = signal("x3T_ps", 1), signal("x3T_sb", 1)
        fc_ps, gelu = signal("fc_ps", NC), signal("gelu", NC)
        mlp_ps, h3_sb = signal("mlp_ps", 1), signal("h3_sb", 1)
        xn_ready = signal("xn_ready", 1)
        zT_ps, zT_sb = signal("zT_ps", 1), signal("zT_sb", 1)
        gate_ps, route, gate_exp = signal("gate_ps", 1), signal("route", 9), signal("gate_exp", 1)
        n_rank = signal("n_rank", 2 * NB + 3)
        gatesT_ps, gatesT_sb = signal("gatesT_ps", 1), signal("gatesT_sb", 1)
        a_ps, b_ps, silu = signal("a_ps", NE + 1), signal("b_ps", NE + 1), signal("silu", NE + 1)
        h_sb, e_ps = signal("h_sb", NE + 1), signal("e_ps", NE + 1)
        acc_sb = signal("acc_sb", 1 + NB * NE)
        o_ready = signal("o_ready", 1)
        o_dma = signal("o_dma", 16)

        block = ctx.enter_context(nc.Block())
        wide = [(w, s) for w, s in ((wqkv, c_attn_w), (wxq0, q_attn_w), (wxkv, x_kv_w), (wfc, fc_w),
                                    (wgate, gate_w))]
        vectors = [(G1, ln1_g), (B1, ln1_b), (GX, lnx_g), (BX, lnx_b), (G2, ln2_g), (B2, ln2_b)]

        def rows_dh(v):
            return v.rearrange("(h d o) -> d h o", d=HD, o=1)

        def load_setup(eng, half):
            jobs = [(w[:], s) for w, s in wide]
            jobs += [(wmlp[:], mlp_proj_w.rearrange("(c p) n -> p c n", p=128))]
            jobs += [(w1[:, 0:NE, :], rw1.rearrange("e p n -> p e n")), (w1[:, NE, :], sw1[0])]
            jobs += [(w2[:, 0:NE, :], rw2.rearrange("e p n -> p e n")), (w2[:, NE, :], sw2[0])]
            jobs += [(b1[:, 0:NE, :], rb1.rearrange("e (a p) -> p e a", p=128)),
                     (b1[:, NE, :], sb1.rearrange("o (a p) -> p (o a)", p=128))]
            jobs += [(b2[0:NE, :], rb2), (b2[NE:NE + 1, :], sb2)]
            jobs += [(cols[:, n:n + 1], v.rearrange("(p o) -> p o", o=1)) for n, v in vectors]
            jobs += [(cols[:, BQ:BQ + 1], rows_dh(c_attn_b[0:D])), (cols[:, BK:BK + 1], rows_dh(c_attn_b[D:2 * D])),
                     (cols[:, BXQ:BXQ + 1], rows_dh(q_attn_b)), (cols[:, BXK:BXK + 1], rows_dh(x_kv_b[0:D]))]
            for s in range(2):
                for j in range(4):
                    p = (4 * s + j) * 16
                    for w, v in ((wo, attn_proj_w), (wxo, x_proj_w)):
                        jobs += [(w[p:p + 16, :], v.rearrange("(s a j d) n -> s j a d n", s=2, a=2, j=4)[s, j])]
                    for n, v in ((BV, c_attn_b[2 * D:3 * D]), (BXV, x_kv_b[D:2 * D])):
                        jobs += [(cols[p:p + 16, n:n + 1],
                                  v.rearrange("(s a j d o) -> s j a d o", s=2, a=2, j=4, o=1)[s, j])]
            jobs += [(bfc[:], fc_b.rearrange("(c p) -> p c", p=128))]
            jobs += [(w[:], v.rearrange("(o n) -> o n", o=1).to_broadcast([128, n]))
                     for w, v, n in ((bo, attn_proj_b, D), (bxo, x_proj_b, D), (bmlp, mlp_proj_b, D), (bgate, gate_b, NE))]
            jobs += [(enc_tm[:], enc[0].rearrange("(k p) f -> p k f", p=128)), (key_bias[:], scorer)]
            for o, i in jobs[half::2]:
                eng.dma_start(o, i).then_inc(loaded.sem, 16)
            return len(jobs)

        FC_BANKS = [6, 7, 5, 4]
        LOADS = []
        PADS = 14
        XK_PARTS = 17
        SETUP_MADE = XK_PARTS + 2

        def exists(*pairs):
            return all(not isinstance(j, int) or 0 <= j < PAIRS for j in pairs)

        def program(eng, body):
            for i in range(-1, 4):
                body(i)
            with eng.Fori(4, PAIRS - 2) as i:
                body(i)
            for i in range(PAIRS - 2, PAIRS + 3):
                body(i)

        @block.sync
        def _(sp):
            def pair_of(x, j):
                return x[bass.ds(sp.snap(2 * j), 2)].rearrange("b (q p) f -> p (b q) f", p=128)

            def load_x(j):
                src = pair_of(hs, j)
                sp.wait_ge(*y_ready.before(j))
                sp.wait_ge(*sa.x_ready.before(j))
                sp.dma_start(x_tm[:], src).then_inc(x_in.sem, 16)

            def keep_x(j):
                src = pair_of(hs, j)
                sp.wait_ge(*xn_ready.before(j))
                sp.dma_start(x_keep[:], src).then_inc(x_kept.sem, 16)

            def store_out(j):
                dst = pair_of(out, j)
                sp.wait_ge(*o_ready.done(j))
                sp.dma_start(dst, o_tm[:]).then_inc(o_dma.sem, 16)

            def operand(parts, op, which, hi, mid, lo, dma, j):
                for made_part, n in ((hi, 0), (mid, 1), (lo, 2)):
                    sp.wait_ge(*made_part.done(j))
                    for slot in range(6):
                        if which[slot] == n:
                            sp.dma_start(op[slot * HD:(slot + 1) * HD, :, :], parts[:, n, :]).then_inc(dma.sem, 16)

            def max_rows(a, j):
                sp.wait_ge(*a.mT_sb.done(j))
                sp.dma_start(a.qop[ROW_MAX:ROW_MAX + 3, :, :], maxT[:]).then_inc(a.m_dma.sem, 16)

            def body(i):
                if exists(i - 3):
                    store_out(i - 3)
                if exists(i - 1):
                    max_rows(ca, i - 1)
                if exists(i + 1):
                    operand(q_parts, q_op, QPARTS, sa.qhi, sa.qmid, sa.qlo, sa.q_dma, i + 1)
                    operand(k_parts, k_op, KPARTS, sa.khi, sa.kmid, sa.klo, sa.k_dma, i + 1)
                if exists(i + 2):
                    load_x(i + 2)
                if exists(i - 2):
                    keep_x(i - 2)
                if exists(i + 1):
                    max_rows(sa, i + 1)
                if exists(i):
                    operand(xq_parts, xq_op, QPARTS, ca.qhi, ca.qmid, ca.qlo, ca.q_dma, i)

            load_x(0)
            LOADS.append(load_setup(sp, 0))
            sp.wait_ge(padded.sem, PADS)
            sp.wait_ge(made.sem, XK_PARTS)
            for slot in range(6):
                sp.dma_start(xk_op[slot * HD:(slot + 1) * HD, :, :], kx_parts[:, KPARTS[slot], :]).then_inc(xk_dma.sem, 16)
            for n in range(3):
                sp.dma_start(xk_op[ROW_BIAS + n:ROW_BIAS + n + 1, :, :],
                             bias_parts[:, n:n + 1, :].to_broadcast([1, H, T])).then_inc(xk_dma.sem, 16)
            program(sp, body)
            sp.wait_ge(*o_dma.done(PAIRS - 1))

        @block.gpsimd
        def _(pool):
            pool.memset(identf[:], 0.0).then_inc(filled.sem, 1)
            pool.memset(identb[:], 0.0).then_inc(filled.sem, 1)
            pool.memset(mask_q[:], 0.0).then_inc(filled.sem, 1)
            pool.memset(mask_k[:], 0.0).then_inc(filled.sem, 1)
            pool.memset(xmask_q[:], 0.0).then_inc(filled.sem, 1)
            pool.memset(xmask_k[:], 0.0).then_inc(filled.sem, 1)
            pool.memset(lower[:], 1.0).then_inc(filled.sem, 1)
            pool.memset(half_neg[:], -0.5).then_inc(filled.sem, 1)
            pool.memset(gates[:], 1.0).then_inc(filled.sem, 1)
            pool.wait_ge(filled.sem, 9)

            def select(m, cmp, fill, base, pattern, channel):
                pool.affine_select(out=m, in_=m, compare_op=cmp, fill=fill, base=base, pattern=pattern,
                                   channel_multiplier=channel).then_inc(shaped.sem, 1)

            select(identf[:], ALU.not_equal, 1.0, 0, [[-1, 128]], 1)
            select(identb[:], ALU.not_equal, 1.0, 0, [[-1, 128]], 1)
            select(mask_q[:], ALU.is_ge, MASKED, 0, [[0, 2], [-1, 128]], 1)
            select(mask_k[:], ALU.is_ge, MASKED, 0, [[0, 2], [1, 128]], -1)
            select(xmask_q[:, 0:128], ALU.is_ge, MASKED, 2, [[-1, 128]], 1)
            select(xmask_q[:, 128:], ALU.is_ge, MASKED, 2, [[-1, XW]], 1)
            select(xmask_k[:, 0:128], ALU.is_ge, MASKED, 2, [[1, 128]], -1)
            select(xmask_k[:, 128:], ALU.is_ge, MASKED, 0, [[1, XW]], -1)
            select(lower[:], ALU.is_gt, 0.0, 0, [[1, NE], [-1, NE]], 0)

            def power(n_var, n_out, var, out_):
                pool.wait_ge(*n_var)
                pool.tensor_tensor(out_, var, half_neg[:], ALU.pow).then_inc(n_out.sem, 1)

            def low_part(r, parts, a_r, a_mid, a_lo, a_dma, j):
                pool.wait_ge(*a_r.done(j))
                pool.wait_ge(*a_mid.done(j))
                pool.wait_ge(*a_dma.before(j))
                pool.tensor_tensor(parts[:, 2, :], r[:], parts[:, 1, :], ALU.subtract).then_inc(a_lo.sem, 1)

            def add_bias(dst, base, bias, ready, before, out_sig):
                pool.wait_ge(*ready)
                pool.wait_ge(*before)
                pool.tensor_tensor(dst[:], base[:], bias[:].rearrange("p (o f) -> p o f", o=1).to_broadcast([128, NB, D]),
                                   ALU.add).then_inc(out_sig.sem, 1)

            def minus_mean(n, mean, r, nb, j):
                pool.wait_ge(*n.rstd.done(j))
                pool.tensor_tensor(nb, mean, r, ALU.mult).then_inc(n.nb.sem, 1)

            def rstd(n, t, j):
                power(n.var_eps.done(j), n.rstd, t[:, 0, :], t[:, 1, :])
                minus_mean(n, t[:, 2, :], t[:, 1, :], t[:, 3, :], j)

            def rstd_x(j):
                power(var_y.part(j, 2), rstd_y, tiny[:, 0, :], tiny[:, 1, :])
                pool.wait_ge(*rstd_y.done(j))
                pool.tensor_tensor(tiny[:, 6, :], tiny[:, 8, :], tiny[:, 1, :], ALU.mult).then_inc(y_nb.sem, 1)
                power(var_y.done(j), rstd_01, tiny[:, 3, :], tiny[:, 4, :])
                pool.wait_ge(*rstd_01.done(j))
                pool.tensor_tensor(tiny[:, 5, :], tiny[:, 1, :], tiny[:, 4, :], ALU.mult).then_inc(sa.rstd.sem, 1)
                minus_mean(sa, tiny[:, 8, :], tiny[:, 5, :], tiny[:, 9, :], j)

            def sum_xn(j):
                pool.wait_ge(*n_post.out.done(j))
                pool.wait_ge(*x_kept.done(j))
                pool.wait_ge(*o_ready.before(j))
                pool.tensor_tensor(xn[:], h3[:], x_keep[:], ALU.add).then_inc(xn_ready.sem, 1)

            def finish(j):
                pool.wait_ge(*n_end.out.done(j))
                pool.wait_ge(*o_dma.before(j))
                pool.tensor_tensor(o_tm[:], acc[:], xn[:], ALU.add).then_inc(o_ready.sem, 1)

            def body(i):
                k = i - 2
                if exists(i - 3):
                    rstd(n_end, tiny_end, i - 3)
                if exists(i + 1):
                    rstd_x(i + 1)
                if exists(i - 3):
                    finish(i - 3)
                if exists(k):
                    pool.wait_ge(*n_mlp.out.done(k))
                    add_bias(h2b, h2, bmlp, ca.h.done(k), h3_sb.before(k), h2b_ready)
                if exists(i + 1):
                    low_part(qr, q_parts, sa.qr, sa.qmid, sa.qlo, sa.q_dma, i + 1)
                    low_part(kr, k_parts, sa.kr, sa.kmid, sa.klo, sa.k_dma, i + 1)
                if exists(k):
                    rstd(n_post, tiny_post, k)
                if exists(i):
                    rstd(ca, tiny2, i)
                if exists(k):
                    sum_xn(k)
                if exists(k):
                    rstd(n_z, tiny_z, k)
                if exists(i + 1):
                    add_bias(yb_tm, y_tm, bo, y_ready.done(i + 1), sa.h.before(i + 1), yb_ready)
                if exists(i):
                    low_part(xqr, xq_parts, ca.qr, ca.qmid, ca.qlo, ca.q_dma, i)
                    add_bias(h1b, h1, bxo, sa.h.done(i), ca.h.before(i), h1b_ready)
                if exists(i - 1):
                    rstd(n_mlp, tiny3, i - 1)

            program(pool, body)

        @block.scalar
        def _(act):
            n = load_setup(act, 1)
            act.wait_ge(loaded.sem, 16 * n)
            act.wait_ge(enc_ps.sem, 1)
            act.activation(encT[:], ps[:, 0, 0:T], ACT.Identity).then_inc(enc_sb.sem, 1)
            act.wait_ge(enc_ps.sem, 2)
            act.activation(kxf[:], ps[:, 1, 0:T], ACT.Identity, bias=cols[:, BXK:BXK + 1]).then_inc(enc_sb.sem, 1)
            act.activation(kx_parts[:, 0, :], ps[:, 1, 0:T], ACT.Identity, bias=cols[:, BXK:BXK + 1]).then_inc(enc_sb.sem, 1)

            def copy_out(bank, dst, ready, before, sig, bias=0.0, scale=1.0):
                act.wait_ge(*before)
                act.wait_ge(*ready)
                act.activation(dst, bank, ACT.Identity, bias=bias, scale=scale).then_inc(sig.sem, 1)

            def high_part(bank, f, parts, bias, scale, ready, res, dma, f_sig, hi_sig, j):
                act.wait_ge(*res.before(j))
                act.wait_ge(*dma.before(j))
                act.wait_ge(*ready.done(j))
                act.activation(f[:], ps[:, bank, :], ACT.Identity, bias=bias, scale=scale).then_inc(f_sig.sem, 1)
                act.activation(parts[:, 0, :], ps[:, bank, :], ACT.Identity, bias=bias, scale=scale).then_inc(hi_sig.sem, 1)

            def values(j):
                act.wait_ge(*sa.pv.before(j))
                act.wait_ge(*sa.v_ps.done(j))
                for half in range(2):
                    src = ps[:, 6, :].rearrange("p (g a j d) -> p g a j d", a=2, j=4, d=HD)[:, :, half]
                    dst = v_st[:].rearrange("p t (s a j) c -> p (t s) a j c", s=2, a=2)[:, :, half, :,
                                                                                       16 * half:16 * half + HD]
                    act.activation(dst, src, ACT.Identity).then_inc(sa.v_sb.sem, 1)

            def normalise(n, dst, src, t, sig, j):
                act.wait_ge(*n.nb.done(j))
                for b in range(NB):
                    act.activation(dst[:, b, :], src[:, b, :], ACT.Identity, bias=t[1][:, b:b + 1],
                                   scale=t[0][:, b:b + 1]).then_inc(sig.sem, 1)

            def norm_x(j):
                act.wait_ge(*sa.xT_ps.before(j))
                normalise(sa, x1_tm, x_tm, (tiny[:, 5, :], tiny[:, 9, :]), sa.x_ready, j)
                act.wait_ge(*y_nb.done(j))
                act.wait_ge(*yb_ready.before(j))
                for b in range(NB):
                    act.activation(y_tm[:, b, :], x_tm[:, b, :], ACT.Identity, bias=tiny[:, 6, b:b + 1],
                                   scale=tiny[:, 1, b:b + 1]).then_inc(y_ready.sem, 1)

            def exps(a, j, used_before, first, last):
                for g in range(first, last):
                    four, pair = divmod(g, 2)
                    act.wait_ge(*(a.pv.part(j, four - 1) if four >= 2 else used_before))
                    act.wait_ge(*a.st_ps.part(j, g + 1))
                    act.activation(probs[:, four % 2, 2 * pair:2 * pair + 2, 0:T + a.seen],
                                   ps[:, 2 * (g % 2):2 * (g % 2) + 2, 0:T + a.seen], ACT.Exp).then_inc(a.exp.sem, 1)
                    if g == 11:
                        context_copy(a, 0, j)

            def context_copy(a, s, j):
                other = sa.cT_ps.done(j) if a is ca else ca.cT_ps.before(j - 1)
                act.wait_ge(*other)
                act.wait_ge(*a.pv.part(j, 4 * s + 4))
                act.activation(ctx_fm[:, s, :], ps[:, 4 + s, :], ACT.Identity).then_inc(a.ctx_sb.sem, 1)

            def experts(j, first, last):
                for n in range(first, last):
                    e = n - 1 if n else NE
                    act.wait_ge(*(h_sb.part(j, n) if n else h_sb.before(j)))
                    act.wait_ge(*a_ps.part(j, n + 1))
                    act.activation(silu_a[:], ps[:, 0, :], ACT.Silu, bias=b1[:, e, 0:1]).then_inc(silu.sem, 1)

            def gelus(j, first, last):
                act.wait_ge(*mlp_ps.before(j))
                for c in range(first, last):
                    act.wait_ge(*fc_ps.part(j, c + 1))
                    act.activation(geluT[:, c, :], ps[:, FC_BANKS[c], :], ACT.Gelu_apprx_tanh,
                                   bias=bfc[:, c:c + 1]).then_inc(gelu.sem, 1)

            def body(i):
                k = i - 2
                used = ca.pv.before(i - 1) if exists(i - 2) else sa.pv.before(i)
                if exists(i):
                    exps(sa, i, used, 0, 3)
                if exists(k):
                    act.wait_ge(*x3T_ps.before(k))
                    normalise(n_mlp, x3_tm, h2, (tiny3[:, 1, :], tiny3[:, 3, :]), n_mlp.out, k)
                if exists(i):
                    exps(sa, i, used, 3, 7)
                if exists(i + 1):
                    norm_x(i + 1)
                if exists(i):
                    exps(sa, i, used, 7, 9)
                if exists(i - 3):
                    normalise(n_end, acc, acc, (tiny_end[:, 1, :], tiny_end[:, 3, :]), n_end.out, i - 3)
                if exists(i):
                    exps(sa, i, used, 9, H)
                if exists(i):
                    context_copy(sa, 1, i)
                if exists(i - 2):
                    copy_out(ps[:, 0, :], x3T[:], x3T_ps.done(i - 2), fc_ps.before(i - 2), x3T_sb,
                             cols[:, B2:B2 + 1], cols[:, G2:G2 + 1])
                if exists(i + 1):
                    copy_out(ps[:, 1, :], xT[:], sa.xT_ps.done(i + 1), ca.q_ps.before(i), sa.xT_sb,
                             cols[:, B1:B1 + 1], cols[:, G1:G1 + 1])
                if exists(i - 1):
                    copy_out(ps[0:3 * H, 4, :].bitcast(BF16)[:, 0:NT], maxT[:], ca.mT_ps.done(i - 1),
                             sa.m_dma.before(i + 1), ca.mT_sb)
                if exists(i - 2):
                    gelus(i - 2, 0, 1)
                if exists(i + 1):
                    high_part(0, qf, q_parts, cols[:, BQS:BQS + 1], SCALE, sa.q_ps, sa.qr, sa.q_dma, sa.qf, sa.qhi, i + 1)
                if exists(i - 2):
                    gelus(i - 2, 1, 2)
                if exists(i + 1):
                    high_part(1, kf, k_parts, cols[:, BK:BK + 1], 1.0, sa.k_ps, sa.kr, sa.k_dma, sa.kf, sa.khi, i + 1)
                if exists(i - 2):
                    gelus(i - 2, 2, NC)
                if exists(i):
                    copy_out(ps[:, 2, :], ctxT[:], sa.nT_ps.done(i), ca.o_ps.before(i - 1), sa.nT_sb, cols[:, BV:BV + 1])
                if exists(i + 1):
                    values(i + 1)
                used = sa.pv.before(i + 1) if exists(i) else ca.pv.before(i - 1)
                if exists(i - 1):
                    exps(ca, i - 1, used, 0, 4)
                if exists(k):
                    normalise(n_post, h3, h3, (tiny_post[:, 1, :], tiny_post[:, 3, :]), n_post.out, k)
                if exists(i - 1):
                    exps(ca, i - 1, used, 4, 8)
                if exists(i):
                    act.wait_ge(*ca.xT_ps.before(i))
                    normalise(ca, x2_tm, h1, (tiny2[:, 1, :], tiny2[:, 3, :]), ca.x_ready, i)
                if exists(i - 1):
                    exps(ca, i - 1, used, 8, 13)
                if exists(k):
                    act.wait_ge(*zT_ps.before(k))
                    normalise(n_z, z_tm, xn, (tiny_z[:, 1, :], tiny_z[:, 3, :]), n_z.out, k)
                if exists(i - 1):
                    exps(ca, i - 1, used, 13, H)
                if exists(i - 1):
                    context_copy(ca, 1, i - 1)
                if exists(i - 2):
                    copy_out(ps[:, 0, :], zT[:], zT_ps.done(i - 2), b_ps.before(i - 2), zT_sb)
                if exists(i):
                    copy_out(ps[:, 2, :], xT[:], ca.xT_ps.done(i), sa.v_ps.before(i + 1), ca.xT_sb,
                             cols[:, BX:BX + 1], cols[:, GX:GX + 1])
                if exists(i + 1):
                    copy_out(ps[0:3 * H, 6, :].bitcast(BF16)[:, 0:NT], maxT[:], sa.mT_ps.done(i + 1),
                             ca.m_dma.before(i), sa.mT_sb)
                if exists(i):
                    high_part(3, xqf, xq_parts, cols[:, BXQS:BXQS + 1], SCALE, ca.q_ps, ca.qr, ca.q_dma, ca.qf, ca.qhi, i)
                if exists(i - 2):
                    act.wait_ge(*route.part(i - 2, 3))
                    act.activation(prob[:], logit[:], ACT.Exp).then_inc(gate_exp.sem, 1)
                    experts(i - 2, 0, 1)
                    copy_out(ps[0:NE + 1, 7, :], gatesT[:], gatesT_ps.done(i - 2), e_ps.before(i - 2), gatesT_sb)
                    experts(i - 2, 1, 3)
                if exists(i - 1):
                    copy_out(ps[:, 6, :], ctxT[:], ca.nT_ps.done(i - 1), sa.o_ps.before(i), ca.nT_sb, cols[:, BXV:BXV + 1])
                if exists(i - 2):
                    experts(i - 2, 3, NE + 1)

            act.wait_ge(made.sem, SETUP_MADE)
            program(act, body)

        @block.vector
        def _(dve):
            for op in (q_op, xq_op, k_op, xk_op):
                dve.memset(op[32:64].bitcast(mybir.dt.uint32), 0).then_inc(padded.sem, 1)
                dve.memset(op[64:128].bitcast(mybir.dt.uint32), 0).then_inc(padded.sem, 1)
            dve.wait_ge(padded.sem, 8)
            dve.memset(xq_op[ROW_BIAS:ROW_BIAS + 3], 1.0).then_inc(padded.sem, 1)
            dve.memset(k_op[ROW_MAX:ROW_MAX + 3], -1.0).then_inc(padded.sem, 1)
            dve.memset(xk_op[ROW_MAX:ROW_MAX + 3], -1.0).then_inc(padded.sem, 1)
            for tile in (v_st, xv_st, max_parts):
                dve.memset(tile[:], 0.0).then_inc(padded.sem, 1)
            dve.wait_ge(padded.sem, PADS)
            steps = [0]

            def make(ins):
                steps[0] += 1
                ins.then_inc(made.sem, 1)
                dve.wait_ge(made.sem, steps[0])

            for tile in (v_st, xv_st):
                for half in range(2):
                    make(dve.memset(tile[:].rearrange("p t (s a j) c -> p (t s) a j c", s=2, a=2)
                                    [:, :, half, :, 16 * half + HD], 1.0))
            dve.wait_ge(loaded.sem, 16 * LOADS[0])
            for dst, src in ((wq, wqkv[:, 0:D]), (wk, wqkv[:, D:2 * D]), (wxq, wxq0[:]), (wxk, wxkv[:, 0:D])):
                make(dve.tensor_copy(dst[:].rearrange("p (d h) -> p d h", d=HD), src.rearrange("p (h d) -> p d h", d=HD)))
            make(dve.tensor_scalar(cols[:, BQS:BQS + 1], cols[:, BQ:BQ + 1], SCALE, None, ALU.mult))
            make(dve.tensor_scalar(cols[:, BXQS:BXQS + 1], cols[:, BXQ:BXQ + 1], SCALE, None, ALU.mult))
            make(dve.tensor_copy(bias_parts[:, 0, :], key_bias[:]))
            make(dve.tensor_tensor(key_res[:], key_bias[:], bias_parts[:, 0, :], ALU.subtract))
            make(dve.tensor_copy(bias_parts[:, 1, :], key_res[:]))
            make(dve.tensor_tensor(bias_parts[:, 2, :], key_res[:], bias_parts[:, 1, :], ALU.subtract))
            dve.wait_ge(enc_sb.sem, 3)
            make(dve.tensor_tensor(kxr[:], kxf[:], kx_parts[:, 0, :], ALU.subtract))
            make(dve.tensor_copy(kx_parts[:, 1, :], kxr[:]))
            make(dve.tensor_tensor(kx_parts[:, 2, :], kxr[:], kx_parts[:, 1, :], ALU.subtract))
            dve.wait_ge(enc_ps.sem, 3)
            for half in range(2):
                src = ps[:, 2, 0:T].rearrange("p (g a j d) -> p g a j d", a=2, j=4, d=HD)[:, :, half]
                dst = xv_st[:].rearrange("p t (s a j) c -> p (t s) a j c", s=2, a=2)[:, :, half, :,
                                                                                    16 * half:16 * half + HD]
                make(dve.tensor_copy(dst, src))
            assert steps[0] == SETUP_MADE

            def statistics(src, st, mv, s_stats, s_aggr, j):
                for t in range(NB):
                    dve.bn_stats(st[:, t, :], src[:, t, :]).then_inc(s_stats.sem, 1)
                dve.wait_ge(*s_stats.done(j))
                dve.memset(wait_slot[:], 0.0)
                for t in range(NB):
                    dve.bn_aggr(mv[:, t, :], st[:, t, :]).then_inc(s_aggr.sem, 1)
                dve.wait_ge(*s_aggr.done(j))

            def residual_parts(f, r, parts, f_sig, hi_sig, r_sig, mid_sig, before, j):
                dve.wait_ge(*f_sig.done(j))
                dve.wait_ge(*hi_sig.done(j))
                dve.wait_ge(*before)
                dve.tensor_tensor(r[:], f[:], parts[:, 0, :], ALU.subtract).then_inc(r_sig.sem, 1)
                dve.wait_ge(*r_sig.done(j))
                dve.tensor_copy(parts[:, 1, :], r[:]).then_inc(mid_sig.sem, 1)

            def stats_x(j):
                dve.wait_ge(*x_in.done(j))
                dve.wait_ge(*sa.nb.before(j))
                statistics(x_tm, stx, mvx, sa.stats, sa.aggr, j)
                dve.wait_ge(*y_ready.before(j))
                dve.tensor_scalar(tiny[:, 0, :], mvx[:, :, 1], EPS, None, ALU.add).then_inc(var_y.sem, 1)
                dve.tensor_scalar(tiny[:, 8, :], mvx[:, :, 0], -1.0, None, ALU.mult).then_inc(var_y.sem, 1)

            def stats_y(j):
                dve.wait_ge(*rstd_y.done(j))
                dve.tensor_tensor(tiny[:, 2, :], tiny[:, 1, :], tiny[:, 1, :], ALU.mult).then_inc(var_y.sem, 1)
                dve.wait_ge(*var_y.part(j, 3))
                dve.tensor_tensor(tiny[:, 7, :], tiny[:, 2, :], mvx[:, :, 1], ALU.mult).then_inc(sa.var_eps.sem, 2)
                dve.wait_ge(*sa.var_eps.done(j))
                dve.tensor_scalar(tiny[:, 3, :], tiny[:, 7, :], EPS, None, ALU.add).then_inc(var_y.sem, 1)

            def maxima(a, j, first, last):
                for n in range(first, last):
                    b, h = divmod(n, H)
                    bank = ps[:, 6 + n % 2, :]
                    dve.wait_ge(*a.s_ps.part(j, n + 1))
                    dve.tensor_reduce(rowmax[:, b, 1, h:h + 1], bank[:, 0:T], AX.X, ALU.max).then_inc(a.s_max.sem, 1)
                    dve.tensor_reduce(rowmax[:, b, 0, h:h + 1], bank[:, T:T + a.seen], AX.X,
                                      ALU.max).then_inc(a.s_max.sem, 1)

            def maxima_parts(a, j):
                mx = rowmax[:].rearrange("p b q h -> p (b q) h")
                dve.wait_ge(*a.s_max.done(j))
                dve.tensor_copy(max_parts[:, :, 0, :], mx).then_inc(a.m1.sem, 1)
                dve.wait_ge(*a.m1.done(j))
                dve.tensor_tensor(max_res[:], mx, max_parts[:, :, 0, :], ALU.subtract).then_inc(a.mr.sem, 1)
                dve.wait_ge(*a.mr.done(j))
                dve.tensor_copy(max_parts[:, :, 1, :], max_res[:]).then_inc(a.m2.sem, 1)
                dve.wait_ge(*a.m2.done(j))
                dve.tensor_tensor(max_parts[:, :, 2, :], max_res[:], max_parts[:, :, 1, :],
                                  ALU.subtract).then_inc(a.m3.sem, 1)

            def normalise_context(a, j):
                for n in range(2):
                    blocks = ps[:, 2 + n, :].rearrange("p (g c) -> p g c", c=16)
                    dve.wait_ge(*a.cT_ps.part(j, n + 1))
                    r = rden[:, 2 * n:2 * n + 2, :].rearrange("p t h -> p (t h)")
                    dve.reciprocal(r, blocks[:, :, HD]).then_inc(a.rden.sem, 1)
                    dve.wait_ge(*a.rden.part(j, n + 1))
                    dve.tensor_tensor(ctx_tm[:, 2 * n:2 * n + 2, :].rearrange("p t (g d) -> p (t g) d", d=HD),
                                      blocks[:, :, 0:HD],
                                      r.rearrange("p (g o) -> p g o", o=1).to_broadcast([128, 32, HD]),
                                      ALU.mult).then_inc(a.ctx_n.sem, 1)

            def add_residual(bank, dst, base, ready, base_ready, sig):
                dve.wait_ge(*base_ready)
                dve.wait_ge(*ready)
                dve.tensor_tensor(dst[:].rearrange("p t f -> p (t f)"), ps[:, bank, :],
                                  base[:].rearrange("p t f -> p (t f)"), ALU.add).then_inc(sig.sem, 1)

            def norm_stats(n, src, ready, st, mv, t, j):
                dve.wait_ge(*ready)
                statistics(src, st, mv, n.stats, n.aggr, j)
                dve.wait_ge(*(n.x_ready if n is ca else n.out).before(j))
                dve.tensor_scalar(t[:, 0, :], mv[:, :, 1], EPS, None, ALU.add).then_inc(n.var_eps.sem, 1)
                dve.tensor_scalar(t[:, 2, :], mv[:, :, 0], -1.0, None, ALU.mult).then_inc(n.var_eps.sem, 1)

            def over_e(x):
                return x.rearrange("p (t o) -> p t o", o=1).to_broadcast([128, NB, NE])

            def router_logits(j):
                dve.wait_ge(*gate_ps.done(j))
                dve.tensor_tensor(logit[:], ps[:, 1, 0:NB * NE].rearrange("p (t e) -> p t e", e=NE),
                                  bgate[:].rearrange("p (o e) -> p o e", o=1).to_broadcast([128, NB, NE]),
                                  ALU.add).then_inc(route.sem, 1)
                dve.wait_ge(*route.part(j, 1))
                dve.tensor_reduce(rt[:, 0, :], logit[:], AX.X, ALU.max).then_inc(route.sem, 1)
                dve.wait_ge(*route.part(j, 2))
                dve.tensor_tensor(logit[:], logit[:], over_e(rt[:, 0, :]), ALU.subtract).then_inc(route.sem, 1)

            def router_gates(j):
                dve.wait_ge(*gate_exp.done(j))
                dve.tensor_reduce(rt[:, 1, :], prob[:], AX.X, ALU.add).then_inc(route.sem, 1)
                dve.wait_ge(*route.part(j, 4))
                dve.reciprocal(rt[:, 2, :], rt[:, 1, :]).then_inc(route.sem, 1)
                dve.wait_ge(*route.part(j, 5))
                dve.tensor_tensor(logit[:], prob[:], over_e(rt[:, 2, :]), ALU.mult).then_inc(route.sem, 1)
                dve.wait_ge(*route.part(j, 6))
                for t in range(NB):
                    other = logit[:, t, :].rearrange("p (o e) -> p o e", o=1).to_broadcast([128, NE, NE])
                    own = logit[:, t, :].rearrange("p (e o) -> p e o", o=1).to_broadcast([128, NE, NE])
                    pairs = more[:, t, :].rearrange("p (e f) -> p e f", f=NE)
                    ties = same[:, t, :].rearrange("p (e f) -> p e f", f=NE)
                    dve.tensor_tensor(pairs, other, own, ALU.is_gt).then_inc(n_rank.sem, 1)
                    dve.tensor_tensor(ties, other, own, ALU.is_equal).then_inc(n_rank.sem, 1)
                dve.wait_ge(*n_rank.part(j, 2 * NB))
                dve.tensor_tensor(same[:], same[:], lower[:].rearrange("p (o e) f -> p o (e f)", o=1)
                                  .to_broadcast([128, NB, NE * NE]), ALU.mult).then_inc(n_rank.sem, 1)
                dve.wait_ge(*n_rank.part(j, 2 * NB + 1))
                dve.tensor_tensor(more[:], more[:], same[:], ALU.add).then_inc(n_rank.sem, 1)
                dve.wait_ge(*n_rank.part(j, 2 * NB + 2))
                dve.tensor_reduce(rank[:], more[:].rearrange("p t (e f) -> p (t e) f", f=NE), AX.X,
                                  ALU.add).then_inc(n_rank.sem, 1)
                dve.wait_ge(*n_rank.done(j))
                dve.scalar_tensor_tensor(out=gates[:, :, 0:NE], in0=rank[:], scalar=1.5, in1=logit[:],
                                         op0=ALU.is_lt, op1=ALU.mult).then_inc(route.sem, 3)

            def products(j, n):
                e = n - 1 if n else NE
                dve.wait_ge(*(e_ps.part(j, n - 1) if n >= 2 else e_ps.before(j)))
                dve.wait_ge(*silu.part(j, n + 1))
                dve.wait_ge(*b_ps.part(j, n + 1))
                dve.scalar_tensor_tensor(out=hT[:, n % 2, :], in0=ps[:, 1, :], scalar=b1[:, e, 1:2],
                                         in1=silu_a[:], op0=ALU.add, op1=ALU.mult).then_inc(h_sb.sem, 1)

            def gather(j, n):
                dve.wait_ge(*e_ps.part(j, n + 1))
                if n == 0:
                    dve.tensor_copy(acc[:].rearrange("p t f -> p (t f)"), ps[:, 4, :]).then_inc(acc_sb.sem, 1)
                else:
                    for t in range(NB):
                        dve.wait_ge(*acc_sb.part(j, 1 if n == 1 else 1 + NB * (n - 2) + t + 1))
                        dve.scalar_tensor_tensor(out=acc[:, t, :], in0=ps[:, 4 + n % 2, t * D:(t + 1) * D],
                                                 scalar=gates[:, t, n - 1:n], in1=acc[:, t, :],
                                                 op0=ALU.mult, op1=ALU.add).then_inc(acc_sb.sem, 1)

            def body(i):
                k = i - 2
                if exists(i - 3):
                    norm_stats(n_end, acc, acc_sb.done(i - 3), sty, mvy, tiny_end, i - 3)
                if exists(i - 1):
                    maxima(ca, i - 1, 0, 6)
                if exists(i + 1):
                    stats_x(i + 1)
                if exists(i - 1):
                    maxima(ca, i - 1, 6, 12)
                if exists(i + 1):
                    stats_y(i + 1)
                if exists(i - 1):
                    maxima(ca, i - 1, 12, 2 * H)
                if exists(i - 1):
                    maxima_parts(ca, i - 1)
                if exists(i):
                    normalise_context(sa, i)
                if exists(i + 1):
                    residual_parts(qf, qr, q_parts, sa.qf, sa.qhi, sa.qr, sa.qmid, sa.qlo.before(i + 1), i + 1)
                    residual_parts(kf, kr, k_parts, sa.kf, sa.khi, sa.kr, sa.kmid, sa.klo.before(i + 1), i + 1)
                if exists(k):
                    add_residual(5, h3, h2b, mlp_ps.done(k), h2b_ready.done(k), h3_sb)
                if exists(i):
                    add_residual(4, h1, yb_tm, sa.o_ps.done(i), yb_ready.done(i), sa.h)
                if exists(k):
                    norm_stats(n_post, h3, h3_sb.done(k), sty, mvy, tiny_post, k)
                if exists(i + 1):
                    maxima(sa, i + 1, 0, 6)
                if exists(i):
                    norm_stats(ca, h1, sa.h.done(i), st2, mv2, tiny2, i)
                if exists(i + 1):
                    maxima(sa, i + 1, 6, 16)
                if exists(k):
                    norm_stats(n_z, xn, xn_ready.done(k), sty, mvy, tiny_z, k)
                if exists(i + 1):
                    maxima(sa, i + 1, 16, 2 * H)
                if exists(i + 1):
                    maxima_parts(sa, i + 1)
                if exists(k):
                    router_logits(k)
                if exists(i):
                    residual_parts(xqf, xqr, xq_parts, ca.qf, ca.qhi, ca.qr, ca.qmid, ca.qlo.before(i), i)
                if exists(k):
                    router_gates(k)
                    products(k, 0)
                if exists(i - 1):
                    normalise_context(ca, i - 1)
                if exists(k):
                    for n in range(1, 5):
                        products(k, n)
                        gather(k, n - 1)
                if exists(i - 1):
                    add_residual(7, h2, h1b, ca.o_ps.done(i - 1), h1b_ready.done(i - 1), ca.h)
                if exists(k):
                    for n in range(5, 7):
                        products(k, n)
                        gather(k, n - 1)
                if exists(i - 1):
                    norm_stats(n_mlp, h2, ca.h.done(i - 1), st3, mv3, tiny3, i - 1)
                if exists(k):
                    for n in range(7, NE + 1):
                        products(k, n)
                        gather(k, n - 1)
                    gather(k, NE)

            program(dve, body)

        @block.tensor
        def _(pe):
            pe.wait_ge(shaped.sem, 9)
            pe.wait_ge(loaded.sem, 16 * LOADS[0])
            for k in range(2):
                last = pe.transpose(ps[:, 0, k * 128:(k + 1) * 128], enc_tm[:, k, :], identf[:])
            last.then_inc(enc_ps.sem, 1)
            pe.wait_ge(made.sem, 8)
            pe.wait_ge(enc_sb.sem, 1)
            pe.matmul(ps[:, 1, 0:T], wxk[:], encT[:], start=True, stop=True).then_inc(enc_ps.sem, 1)
            for k in range(2):
                last = pe.matmul(ps[:, 2, k * D:(k + 1) * D], encT[:, k * 128:(k + 1) * 128], wxkv[:, D:2 * D],
                                 start=True, stop=True)
            last.then_inc(enc_ps.sem, 1)
            pe.wait_ge(made.sem, SETUP_MADE)
            pe.wait_ge(xk_dma.sem, 16 * 9)

            def transposes(bank, src, sig):
                for t in range(NB):
                    last = pe.transpose(bank[:, t * 128:(t + 1) * 128], src[:, t, :], identf[:])
                last.then_inc(sig.sem, 1)

            def scores(a, n, j):
                b, h = divmod(n, H)
                if n >= 2:
                    pe.wait_ge(*a.s_max.part(j, 2 * (n - 1)))
                bank = ps[:, 6 + n % 2, :]
                q0 = b * T
                k0 = 0 if a.cross else b * T
                pe.matmul(bank[:, 0:T], a.qop[0:ROWS_S, h, q0 + 128:q0 + 256], a.kop[0:ROWS_S, h, k0:k0 + T],
                          start=True, stop=False, skip_group_check=True)
                pe.matmul(bank[:, T:T + a.seen], a.qop[0:ROWS_S, h, q0:q0 + 128],
                          a.kop[0:ROWS_S, h, k0:k0 + a.seen], start=False, stop=False, skip_group_check=True)
                mask = a.mq[:] if a.cross else a.mq[:].rearrange("p a b -> p (a b)")
                pe.matmul(bank[:, 128:T + a.seen], identb[:], mask, start=False, stop=True,
                          skip_group_check=True).then_inc(a.s_ps.sem, 1)

            def max_rows(a, bank, j):
                pe.wait_ge(*a.m3.done(j))
                for t in range(NB):
                    last = pe.transpose(ps[:, bank, :].bitcast(BF16)[:, t * 128:(t + 1) * 128],
                                        max_parts[:, t].rearrange("p a h -> p (a h)"), identb[:])
                last.then_inc(a.mT_ps.sem, 1)

            def score_group(a, g, j):
                s, b, aa, jj = g // 8, g // 4 % 2, g // 2 % 2, g % 2
                if g >= 2:
                    pe.wait_ge(*a.exp.part(j, g - 1))
                q0 = b * T
                k0 = 0 if a.cross else b * T
                late = T - a.seen
                for n in range(2):
                    h = 8 * s + 4 * aa + 2 * jj + n
                    bank = ps[:, 2 * (g % 2) + n, :]
                    pe.matmul(bank[:, 0:T], a.kop[0:ROWS_ST, h, k0:k0 + 128], a.qop[0:ROWS_ST, h, q0:q0 + T],
                              start=True, stop=False, skip_group_check=True)
                    pe.matmul(bank[:, T:T + a.seen], a.kop[0:ROWS_ST, h, k0 + 128:k0 + T],
                              a.qop[0:ROWS_ST, h, q0 + late:q0 + T], start=False, stop=False, skip_group_check=True)
                    if a.cross:
                        pe.matmul(bank[:, 0:128], identb[:], a.mk[:, 0:128], start=False, stop=False, skip_group_check=True)
                        last = pe.matmul(bank[:, T:T + XW], identb[:], a.mk[:, 128:128 + XW], start=False, stop=True,
                                         skip_group_check=True)
                    else:
                        pe.matmul(bank[:, 0:128], identb[:], a.mk[:, 0, :], start=False, stop=False, skip_group_check=True)
                        last = pe.matmul(bank[:, T:T + 128], identb[:], a.mk[:, 1, :], start=False, stop=True,
                                         skip_group_check=True)
                last.then_inc(a.st_ps.sem, 1)

            def value_group(a, four, j):
                s, b, aa = four // 4, four // 2 % 2, four % 2
                pe.wait_ge(*a.exp.part(j, 2 * four + 2))
                late = T - a.seen
                bank = ps[:, 4 + s, :]
                for half in range(2):
                    for jj in range(4):
                        h = 8 * s + 4 * aa + jj
                        v = a.v[:, half if a.cross else 2 * b + half, h, :]
                        q0 = b * T + (late if half else 0)
                        last = pe.matmul(bank[32 * jj:32 * jj + 32, q0:(b + 1) * T], v,
                                         probs[:, four % 2, jj, (T if half else 0):(T + a.seen if half else T)],
                                         start=(aa == 0 and half == 0), stop=(aa == 1 and half == 1),
                                         skip_group_check=True)
                last.then_inc(a.pv.sem, 1)

            def attention_phase(a, j, other, jo, free_4, free_5):
                if exists(j):
                    pe.wait_ge(*a.m_dma.done(j))
                    if not a.cross:
                        pe.wait_ge(*a.v_sb.done(j))
                if exists(jo):
                    pe.wait_ge(*other.q_dma.done(jo))
                    if not other.cross:
                        pe.wait_ge(*other.k_dma.done(jo))
                for four in range(8):
                    if exists(j):
                        score_group(a, 2 * four, j)
                    if exists(jo):
                        scores(other, 4 * four, jo)
                        scores(other, 4 * four + 1, jo)
                    if exists(j):
                        score_group(a, 2 * four + 1, j)
                    if exists(jo):
                        scores(other, 4 * four + 2, jo)
                    if exists(j) and four:
                        if four == 1:
                            free_4()
                        if four == 5:
                            free_5()
                        value_group(a, four - 1, j)
                    if exists(jo):
                        scores(other, 4 * four + 3, jo)
                if exists(j):
                    value_group(a, 7, j)

            def context_T(a, j):
                pe.wait_ge(*a.ctx_sb.done(j))
                for n in range(2):
                    for t in (2 * n, 2 * n + 1):
                        for s in range(2):
                            at = (t % 2) * 256 + s * 128
                            last = pe.transpose(ps[:, 2 + n, at:at + 128], ctx_fm[:, s, t * 128:(t + 1) * 128], identf[:])
                    last.then_inc(a.cT_ps.sem, 1)

            def by_token(bank, src, w, sig):
                for t in range(NB):
                    last = pe.matmul(ps[:, bank, t * D:(t + 1) * D], src[:, t * 128:(t + 1) * 128], w, start=True, stop=True)
                last.then_inc(sig.sem, 1)

            def by_feature(bank, w, src, sig):
                pe.matmul(ps[:, bank, :], w, src[:], start=True, stop=True).then_inc(sig.sem, 1)

            def fc(j, c):
                by_feature(FC_BANKS[c], wfc[:, c * 128:(c + 1) * 128], x3T, fc_ps)

            def up_a(j, n):
                e = n - 1 if n else NE
                if n:
                    pe.wait_ge(*silu.part(j, n))
                by_feature(0, w1[:, e, 0:128], zT, a_ps)

            def up_b(j, n):
                e = n - 1 if n else NE
                if n:
                    pe.wait_ge(*h_sb.part(j, n))
                by_feature(1, w1[:, e, 128:256], zT, b_ps)

            def down(j, n):
                e = n - 1 if n else NE
                if n >= 2:
                    pe.wait_ge(*acc_sb.part(j, 1 + NB * (n - 2)))
                pe.wait_ge(*h_sb.part(j, n + 1))
                for t in range(NB):
                    to = ps[:, 4 + n % 2, t * D:(t + 1) * D]
                    last = pe.matmul(to, hT[:, n % 2, t * 128:(t + 1) * 128], w2[:, e, :], start=True, stop=(n > 0))
                    if n == 0:
                        last = pe.matmul(to, gatesT[:, t * 128:(t + 1) * 128], b2[:], start=False, stop=True)
                last.then_inc(e_ps.sem, 1)

            def experts(j, first, last):
                for n in range(first, last):
                    up_a(j, n)
                    up_b(j, n)
                    down(j, n - 1)

            def body(i):
                k = i - 2
                def free_experts():
                    if exists(k - 1):
                        pe.wait_ge(*acc_sb.before(k))

                def free_self_output():
                    if exists(i):
                        pe.wait_ge(*sa.h.done(i))

                def free_mlp():
                    if exists(k):
                        pe.wait_ge(*h3_sb.done(k))

                if exists(i - 2):
                    pe.wait_ge(*ca.h.before(i - 1))
                if exists(i - 1):
                    pe.wait_ge(*ca.qhi.done(i - 1))
                if exists(k - 1):
                    pe.wait_ge(*h_sb.before(k))
                attention_phase(sa, i, ca, i - 1, free_experts, free_experts)
                if exists(i):
                    pe.wait_ge(*sa.exp.done(i))
                if exists(k):
                    pe.wait_ge(*n_mlp.out.done(k))
                    transposes(ps[:, 0, :], x3_tm, x3T_ps)
                if exists(i + 1):
                    pe.wait_ge(*sa.x_ready.done(i + 1))
                    transposes(ps[:, 1, :], x1_tm, sa.xT_ps)
                if exists(i):
                    context_T(sa, i)
                if exists(i - 1):
                    max_rows(ca, 4, i - 1)
                if exists(k):
                    pe.wait_ge(*ca.s_max.done(i - 1) if exists(i - 1) else x3T_sb.done(k))
                    pe.wait_ge(*x3T_sb.done(k))
                    fc(k, 0)
                    fc(k, 1)
                if exists(i + 1):
                    pe.wait_ge(*sa.xT_sb.done(i + 1))
                    by_feature(0, wq[:], xT, sa.q_ps)
                if exists(k):
                    fc(k, 2)
                if exists(i + 1):
                    by_feature(1, wk[:], xT, sa.k_ps)
                if exists(i - 1):
                    pe.wait_ge(*ca.mT_sb.done(i - 1))
                if exists(k):
                    fc(k, 3)
                if exists(i):
                    pe.wait_ge(*sa.ctx_n.done(i))
                    transposes(ps[:, 2, :], ctx_tm, sa.nT_ps)
                if exists(k):
                    pe.wait_ge(*gelu.done(k))
                if exists(i + 1):
                    if exists(i - 1):
                        pe.wait_ge(*ca.s_max.done(i - 1))
                    by_token(6, xT, wqkv[:, 2 * D:3 * D], sa.v_ps)
                if exists(k):
                    for t in range(NB):
                        for c in range(NC):
                            last = pe.matmul(ps[:, 5, t * D:(t + 1) * D], geluT[:, c, t * 128:(t + 1) * 128], wmlp[:, c, :],
                                             start=(c == 0), stop=(c == NC - 1))
                    last.then_inc(mlp_ps.sem, 1)
                if exists(i):
                    pe.wait_ge(*sa.nT_sb.done(i))
                    by_token(4, ctxT, wo[:], sa.o_ps)
                if exists(i + 1):
                    pe.wait_ge(*sa.qhi.done(i + 1))
                    pe.wait_ge(*sa.khi.done(i + 1))
                    pe.wait_ge(*sa.v_sb.done(i + 1))
                attention_phase(ca, i - 1, sa, i + 1, free_self_output, free_mlp)
                if exists(i - 1):
                    pe.wait_ge(*ca.exp.done(i - 1))
                if exists(k):
                    pe.wait_ge(*n_z.out.done(k))
                    transposes(ps[:, 0, :], z_tm, zT_ps)
                if exists(i):
                    pe.wait_ge(*ca.x_ready.done(i))
                    transposes(ps[:, 2, :], x2_tm, ca.xT_ps)
                if exists(k):
                    pe.wait_ge(*zT_sb.done(k))
                    for t in range(NB):
                        last = pe.matmul(ps[:, 1, t * NE:(t + 1) * NE], zT[:, t * 128:(t + 1) * 128], wgate[:],
                                         start=True, stop=True)
                    last.then_inc(gate_ps.sem, 1)
                if exists(i + 1):
                    max_rows(sa, 6, i + 1)
                if exists(i):
                    pe.wait_ge(*ca.xT_sb.done(i))
                    by_feature(3, wxq[:], xT, ca.q_ps)
                if exists(k):
                    up_a(k, 0)
                    pe.wait_ge(*route.part(k, 1))
                    up_b(k, 0)
                if exists(i - 1):
                    if exists(i):
                        pe.wait_ge(*ca.qhi.done(i))
                    context_T(ca, i - 1)
                if exists(k):
                    up_a(k, 1)
                    pe.wait_ge(*route.done(k))
                    if exists(i + 1):
                        pe.wait_ge(*sa.s_max.done(i + 1))
                    for t in range(NB):
                        last = pe.transpose(ps[0:NE + 1, 7, t * 128:(t + 1) * 128], gates[:, t, :], identf[:])
                    last.then_inc(gatesT_ps.sem, 1)
                    up_b(k, 1)
                    pe.wait_ge(*gatesT_sb.done(k))
                    down(k, 0)
                    experts(k, 2, 3)
                if exists(i - 1):
                    pe.wait_ge(*ca.ctx_n.done(i - 1))
                    if exists(i + 1):
                        pe.wait_ge(*sa.mT_sb.done(i + 1))
                    transposes(ps[:, 6, :], ctx_tm, ca.nT_ps)
                if exists(k):
                    experts(k, 3, 4)
                if exists(i - 1):
                    pe.wait_ge(*ca.nT_sb.done(i - 1))
                    by_token(7, ctxT, wxo[:], ca.o_ps)
                if exists(k):
                    experts(k, 4, NE + 1)
                    down(k, NE)

            program(pe, body)


_INS = ['hidden_states', 'encoder_hidden_states', 'scorer_logits', 'ln1_g', 'ln1_b', 'c_attn_w', 'c_attn_b',
        'attn_proj_w', 'attn_proj_b', 'lnx_g', 'lnx_b', 'q_attn_w', 'q_attn_b', 'x_kv_w', 'x_kv_b', 'x_proj_w',
        'x_proj_b', 'ln2_g', 'ln2_b', 'fc_w', 'fc_b', 'mlp_proj_w', 'mlp_proj_b']
_FFN = ['gate_w', 'gate_b', 'sw1', 'sb1', 'sw2', 'sb2', 'rw1', 'rb1', 'rw2', 'rb2']


def kernel(**inputs):
    import numpy as _np
    import concourse.bacc as _bacc
    from concourse import mybir as _mybir
    from concourse.bass_utils import run_bass_kernel_spmd as _run

    nc = _bacc.Bacc("TRN2", target_bir_lowering=False, num_devices=1)
    names = ["L0_attn_" + n for n in _INS] + ["L0_ffn_" + n for n in _FFN]
    arrays, args = {}, []
    for name in names:
        a = _np.ascontiguousarray(inputs[name])
        arrays[f"in_{name}"] = a
        args.append(nc.dram_tensor(f"in_{name}", a.shape, _mybir.dt.from_np(a.dtype), kind="ExternalInput").ap())
    shape = arrays["in_L0_attn_hidden_states"].shape
    out = nc.dram_tensor("out_0", shape, F32, kind="ExternalOutput").ap()
    sandwich_kernel(nc, out, *args)
    r = _run(nc, [arrays], core_ids=[0])
    return r.results[0]["out_0"]
```
